# Optimizing a Trainium2 kernel written in Bass

```python
import numpy as np
import jax
import jax.numpy as jnp

def _softmax(x, axis=-1):
    return jax.nn.softmax(x, axis=axis)

def _gelu(x):
    return jax.nn.gelu(x, approximate=True)

def _silu(x):
    return jax.nn.silu(x)

def _sigmoid(x):
    return jax.nn.sigmoid(x)

def _layernorm(x, axis=-1, eps=1e-05):
    m = jnp.mean(x, axis=axis, keepdims=True)
    v = jnp.var(x, axis=axis, keepdims=True)
    return (x - m) / jnp.sqrt(v + eps)

def _scatter_add(tgt, idx, src, axis=0):
    return tgt.at[idx].add(src)

def _segment_sum(src, seg, n):
    return jax.ops.segment_sum(src, seg, n)
kernel_name = 'mk_flamingo_gated_d2_seqx_r4_414dc5'

def setup_inputs(seed: int=0):
    np.random.seed(seed)
    _w = jnp.asarray

    def _rec_inputs():
        import jax
        import jax.numpy as jnp
        _rk = jax.random.key(seed)
        x = 7.22e-05 + 1 * jax.random.normal(jax.random.fold_in(_rk, 1), (8, 112, 256), jnp.float32)
        _lenS = 112 - jax.random.randint(jax.random.fold_in(_rk, 7), (8,), 0, max(1, 112 // 4) + 1, jnp.int32)
        _lenS2 = 375 - jax.random.randint(jax.random.fold_in(_rk, 8), (8,), 0, max(1, 375 // 4) + 1, jnp.int32)
        _ctx_768P = jax.random.normal(jax.random.fold_in(_rk, 11), (8, 16, 192), jnp.float32)
        _ctx_768c = jax.random.dirichlet(jax.random.fold_in(_rk, 511), 0.3 * jnp.ones((16,), jnp.float32), (8, 375))
        _ctx_768t = jnp.einsum('bsk,bkd->bsd', _ctx_768c, _ctx_768P)
        _ctx_768t = _ctx_768t * jax.lax.rsqrt(jnp.mean(jnp.square(_ctx_768t)) + 1e-12) * 0.953939
        ctx_768 = -0.000191848 + 0.999787 * (_ctx_768t + 0.3 * jax.random.normal(jax.random.fold_in(_rk, 611), (8, 375, 192), jnp.float32))
        _g = jax.random.normal(jax.random.fold_in(_rk, 9001), (2, 2), jnp.float32)
        _g = jnp.sign(_g) * jnp.maximum(jnp.abs(_g), 1.0) + (_g == 0) * 1.0
        g_xattn = _g[0]
        g_ffn = _g[1]
        return (x, ctx_768, g_xattn, g_ffn)
    x, ctx_768, g_xattn, g_ffn = _rec_inputs()

    def _L0_xattn_setup():
        import jax, jax.numpy as jnp
        import numpy as np
        NUM_HEADS = 16
        CLAMP = 10000.0
        key = jax.random.key(seed)
        ks = jax.random.split(key, 8)
        B, Nq, Nkv, Cq, Ckv = (4, 512, 512, 256, 192)
        s_q = 1.0 / np.sqrt(Cq)
        s_kv = 1.0 / np.sqrt(Ckv)
        return {'query': jax.random.normal(ks[0], (B, Nq, Cq), jnp.float32), 'key_value': jax.random.normal(ks[1], (B, Nkv, Ckv), jnp.float32), 'Wq': jax.random.normal(ks[2], (Cq, Cq), jnp.float32) * s_q, 'bq': jnp.zeros((Cq,), jnp.float32), 'Wk': jax.random.normal(ks[3], (Ckv, Cq), jnp.float32) * s_kv, 'bk': jnp.zeros((Cq,), jnp.float32), 'Wv': jax.random.normal(ks[4], (Ckv, Cq), jnp.float32) * s_kv, 'bv': jnp.zeros((Cq,), jnp.float32), 'Wo': jax.random.normal(ks[5], (Cq, Cq), jnp.float32) * s_q, 'bo': jnp.zeros((Cq,), jnp.float32)}
    _L0_xattn_all = _L0_xattn_setup()
    _L0_xattn_in = {k: v for k, v in _L0_xattn_all.items() if k in ('Wq', 'bq', 'Wk', 'bk', 'Wv', 'bv', 'Wo', 'bo')}
    del _L0_xattn_all

    def _L0_ffn_setup():
        import jax, jax.numpy as jnp
        import numpy as np
        from jax.scipy.linalg import expm
        B, S, D, E, K, NROT = (2, 512, 256, 8, 2, 3)
        EPS = 1e-05

        def _gelu(x):
            return jax.nn.gelu(x, approximate=False)

        def _forward(x, ln_gamma, ln_beta, abel_w, abel_b, moe_gate_w, moe_gate_b, ew1, eb1, ew2, eb2, gens, gc_w, gc_b):
            residual = x
            mu = jnp.mean(x, axis=-1, keepdims=True)
            var = jnp.mean((x - mu) ** 2, axis=-1, keepdims=True)
            xn = (x - mu) * jax.lax.rsqrt(var + EPS) * ln_gamma + ln_beta
            abel_out = _gelu(xn @ abel_w + abel_b)
            logits = xn @ moe_gate_w + moe_gate_b
            topw, topi = jax.lax.top_k(logits, K)
            topw = jax.nn.softmax(topw, axis=-1)
            w_dense = jnp.sum(jax.nn.one_hot(topi, E, dtype=xn.dtype) * topw[..., None], axis=-2)
            h = _gelu(jnp.einsum('bsd,edh->ebsh', xn, ew1) + eb1[:, None, None, :])
            eo = jnp.einsum('ebsh,ehd->ebsd', h, ew2) + eb2[:, None, None, :]
            moe_out = jnp.einsum('ebsd,bse->bsd', eo, w_dense)
            for i in range(NROT):
                moe_out = moe_out @ expm(gens[i])
            combined = jnp.concatenate([abel_out, moe_out], axis=-1)
            gate = jax.nn.sigmoid(combined @ gc_w + gc_b)
            mixed = abel_out * (1.0 - gate) + moe_out * gate
            return residual + mixed
        key = jax.random.key(seed)
        ks = jax.random.split(key, 16)
        sc = 0.02
        x = jax.random.normal(ks[0], (B, S, D), jnp.float32)
        ln_gamma = 1.0 + sc * jax.random.normal(ks[1], (D,), jnp.float32)
        ln_beta = sc * jax.random.normal(ks[2], (D,), jnp.float32)
        abel_w = sc * jax.random.normal(ks[3], (D, D), jnp.float32)
        abel_b = sc * jax.random.normal(ks[4], (D,), jnp.float32)
        moe_gate_w = sc * jax.random.normal(ks[5], (D, E), jnp.float32)
        moe_gate_b = sc * jax.random.normal(ks[6], (E,), jnp.float32)
        ew1 = sc * jax.random.normal(ks[7], (E, D, 2 * D), jnp.float32)
        eb1 = sc * jax.random.normal(ks[8], (E, 2 * D), jnp.float32)
        ew2 = sc * jax.random.normal(ks[9], (E, 2 * D, D), jnp.float32)
        eb2 = sc * jax.random.normal(ks[10], (E, D), jnp.float32)
        g = sc * jax.random.normal(ks[11], (NROT, D, D), jnp.float32)
        gens = 0.5 * (g - jnp.swapaxes(g, -1, -2))
        gc_w = sc * jax.random.normal(ks[12], (2 * D, 1), jnp.float32)
        gc_b = sc * jax.random.normal(ks[13], (1,), jnp.float32)
        return dict(x=x, ln_gamma=ln_gamma, ln_beta=ln_beta, abel_w=abel_w, abel_b=abel_b, moe_gate_w=moe_gate_w, moe_gate_b=moe_gate_b, ew1=ew1, eb1=eb1, ew2=ew2, eb2=eb2, gens=gens, gc_w=gc_w, gc_b=gc_b)
    _L0_ffn_all = _L0_ffn_setup()
    _L0_ffn_in = {k: v for k, v in _L0_ffn_all.items() if k in ('ln_gamma', 'ln_beta', 'abel_w', 'abel_b', 'moe_gate_w', 'moe_gate_b', 'ew1', 'eb1', 'ew2', 'eb2', 'gens', 'gc_w', 'gc_b')}
    del _L0_ffn_all

    def _L1_xattn_setup():
        import jax, jax.numpy as jnp
        import numpy as np
        HEADS = 16
        DIM_HEAD = 64
        RANK = 32
        LORA_W = 1.0
        IPA_SCALE = 1.0
        IPA_TOKENS = 4
        SCALE = DIM_HEAD ** (-0.5)

        def _split_heads(t):
            b, n, _ = t.shape
            return t.reshape(b, n, HEADS, DIM_HEAD).transpose(0, 2, 1, 3)

        def _merge_heads(t):
            b, h, n, d = t.shape
            return t.transpose(0, 2, 1, 3).reshape(b, n, h * d)

        def _attention(q_in, k_in, v_in):
            q = _split_heads(q_in)
            k = _split_heads(k_in)
            v = _split_heads(v_in)
            s = jnp.einsum('bhid,bhjd->bhij', q, k) * SCALE
            p = jax.nn.softmax(s, axis=-1)
            o = jnp.einsum('bhij,bhjd->bhid', p, v)
            return _merge_heads(o)

        def _lora(t, down, up, alpha):
            return t @ down @ up * (LORA_W * alpha[0] / RANK)
        key = jax.random.key(seed)
        ks = jax.random.split(key, 20)
        B, N, QD, CD, ID = (8, 1024, 256, 192, HEADS * DIM_HEAD)
        CTX = 77 + IPA_TOKENS
        s = 0.02
        return {'x': jax.random.normal(ks[0], (B, N, QD), jnp.float32), 'context': jax.random.normal(ks[1], (B, CTX, CD), jnp.float32), 'Wq': jax.random.normal(ks[2], (QD, ID), jnp.float32) * s, 'Wk': jax.random.normal(ks[3], (CD, ID), jnp.float32) * s, 'Wv': jax.random.normal(ks[4], (CD, ID), jnp.float32) * s, 'Wo': jax.random.normal(ks[5], (ID, QD), jnp.float32) * s, 'bo': jnp.zeros((QD,), jnp.float32), 'q_down': jax.random.normal(ks[6], (QD, RANK), jnp.float32) * s, 'q_up': jax.random.normal(ks[7], (RANK, ID), jnp.float32) * s, 'q_alpha': jnp.ones((1,), jnp.float32) * RANK, 'k_down': jax.random.normal(ks[8], (CD, RANK), jnp.float32) * s, 'k_up': jax.random.normal(ks[9], (RANK, ID), jnp.float32) * s, 'k_alpha': jnp.ones((1,), jnp.float32) * RANK, 'v_down': jax.random.normal(ks[10], (CD, RANK), jnp.float32) * s, 'v_up': jax.random.normal(ks[11], (RANK, ID), jnp.float32) * s, 'v_alpha': jnp.ones((1,), jnp.float32) * RANK, 'o_down': jax.random.normal(ks[12], (ID, RANK), jnp.float32) * s, 'o_up': jax.random.normal(ks[13], (RANK, QD), jnp.float32) * s, 'o_alpha': jnp.ones((1,), jnp.float32) * RANK, 'Wk_ipa': jax.random.normal(ks[14], (CD, ID), jnp.float32) * s, 'Wv_ipa': jax.random.normal(ks[15], (CD, ID), jnp.float32) * s}
    _L1_xattn_all = _L1_xattn_setup()
    _L1_xattn_in = {k: v for k, v in _L1_xattn_all.items() if k in ('Wq', 'Wk', 'Wv', 'Wo', 'bo', 'q_down', 'q_up', 'q_alpha', 'k_down', 'k_up', 'k_alpha', 'v_down', 'v_up', 'v_alpha', 'o_down', 'o_up', 'o_alpha', 'Wk_ipa', 'Wv_ipa')}
    del _L1_xattn_all

    def _L1_ffn_setup():
        import jax, jax.numpy as jnp
        import numpy as np
        B, S, H, I, E_ROUTED, TOP_K = (8, 512, 256, 512, 8, 2)

        def _expert(x, Wg, Wu, Wd):
            return jax.nn.silu(x @ Wg.T) * (x @ Wu.T) @ Wd.T
        key = jax.random.key(seed)
        ks = jax.random.split(key, 9)
        s = 0.02
        return {'x': jax.random.normal(ks[0], (B, S, H), dtype=jnp.float32), 'Wg_s': jax.random.normal(ks[1], (I, H), dtype=jnp.float32) * s, 'Wu_s': jax.random.normal(ks[2], (I, H), dtype=jnp.float32) * s, 'Wd_s': jax.random.normal(ks[3], (H, I), dtype=jnp.float32) * s, 'Wg': jax.random.normal(ks[4], (E_ROUTED, I, H), dtype=jnp.float32) * s, 'Wu': jax.random.normal(ks[5], (E_ROUTED, I, H), dtype=jnp.float32) * s, 'Wd': jax.random.normal(ks[6], (E_ROUTED, H, I), dtype=jnp.float32) * s, 'Wr': jax.random.normal(ks[7], (E_ROUTED, H), dtype=jnp.float32) * s, 'rb': jnp.zeros((E_ROUTED,), dtype=jnp.float32)}
    _L1_ffn_all = _L1_ffn_setup()
    _L1_ffn_in = {k: v for k, v in _L1_ffn_all.items() if k in ('Wg_s', 'Wu_s', 'Wd_s', 'Wg', 'Wu', 'Wd', 'Wr', 'rb')}
    del _L1_ffn_all
    return {'x': x, 'ctx_768': ctx_768, 'g_xattn': g_xattn, 'g_ffn': g_ffn, 'L0_xattn_Wq': _L0_xattn_in['Wq'], 'L0_xattn_bq': _L0_xattn_in['bq'], 'L0_xattn_Wk': _L0_xattn_in['Wk'], 'L0_xattn_bk': _L0_xattn_in['bk'], 'L0_xattn_Wv': _L0_xattn_in['Wv'], 'L0_xattn_bv': _L0_xattn_in['bv'], 'L0_xattn_Wo': _L0_xattn_in['Wo'], 'L0_xattn_bo': _L0_xattn_in['bo'], 'L0_ffn_ln_gamma': _L0_ffn_in['ln_gamma'], 'L0_ffn_ln_beta': _L0_ffn_in['ln_beta'], 'L0_ffn_abel_w': _L0_ffn_in['abel_w'], 'L0_ffn_abel_b': _L0_ffn_in['abel_b'], 'L0_ffn_moe_gate_w': _L0_ffn_in['moe_gate_w'], 'L0_ffn_moe_gate_b': _L0_ffn_in['moe_gate_b'], 'L0_ffn_ew1': _L0_ffn_in['ew1'], 'L0_ffn_eb1': _L0_ffn_in['eb1'], 'L0_ffn_ew2': _L0_ffn_in['ew2'], 'L0_ffn_eb2': _L0_ffn_in['eb2'], 'L0_ffn_gens': _L0_ffn_in['gens'], 'L0_ffn_gc_w': _L0_ffn_in['gc_w'], 'L0_ffn_gc_b': _L0_ffn_in['gc_b'], 'L1_xattn_Wq': _L1_xattn_in['Wq'], 'L1_xattn_Wk': _L1_xattn_in['Wk'], 'L1_xattn_Wv': _L1_xattn_in['Wv'], 'L1_xattn_Wo': _L1_xattn_in['Wo'], 'L1_xattn_bo': _L1_xattn_in['bo'], 'L1_xattn_q_down': _L1_xattn_in['q_down'], 'L1_xattn_q_up': _L1_xattn_in['q_up'], 'L1_xattn_q_alpha': _L1_xattn_in['q_alpha'], 'L1_xattn_k_down': _L1_xattn_in['k_down'], 'L1_xattn_k_up': _L1_xattn_in['k_up'], 'L1_xattn_k_alpha': _L1_xattn_in['k_alpha'], 'L1_xattn_v_down': _L1_xattn_in['v_down'], 'L1_xattn_v_up': _L1_xattn_in['v_up'], 'L1_xattn_v_alpha': _L1_xattn_in['v_alpha'], 'L1_xattn_o_down': _L1_xattn_in['o_down'], 'L1_xattn_o_up': _L1_xattn_in['o_up'], 'L1_xattn_o_alpha': _L1_xattn_in['o_alpha'], 'L1_xattn_Wk_ipa': _L1_xattn_in['Wk_ipa'], 'L1_xattn_Wv_ipa': _L1_xattn_in['Wv_ipa'], 'L1_ffn_Wg_s': _L1_ffn_in['Wg_s'], 'L1_ffn_Wu_s': _L1_ffn_in['Wu_s'], 'L1_ffn_Wd_s': _L1_ffn_in['Wd_s'], 'L1_ffn_Wg': _L1_ffn_in['Wg'], 'L1_ffn_Wu': _L1_ffn_in['Wu'], 'L1_ffn_Wd': _L1_ffn_in['Wd'], 'L1_ffn_Wr': _L1_ffn_in['Wr'], 'L1_ffn_rb': _L1_ffn_in['rb']}

def reference(x, ctx_768, g_xattn, g_ffn, L0_xattn_Wq, L0_xattn_bq, L0_xattn_Wk, L0_xattn_bk, L0_xattn_Wv, L0_xattn_bv, L0_xattn_Wo, L0_xattn_bo, L0_ffn_ln_gamma, L0_ffn_ln_beta, L0_ffn_abel_w, L0_ffn_abel_b, L0_ffn_moe_gate_w, L0_ffn_moe_gate_b, L0_ffn_ew1, L0_ffn_eb1, L0_ffn_ew2, L0_ffn_eb2, L0_ffn_gens, L0_ffn_gc_w, L0_ffn_gc_b, L1_xattn_Wq, L1_xattn_Wk, L1_xattn_Wv, L1_xattn_Wo, L1_xattn_bo, L1_xattn_q_down, L1_xattn_q_up, L1_xattn_q_alpha, L1_xattn_k_down, L1_xattn_k_up, L1_xattn_k_alpha, L1_xattn_v_down, L1_xattn_v_up, L1_xattn_v_alpha, L1_xattn_o_down, L1_xattn_o_up, L1_xattn_o_alpha, L1_xattn_Wk_ipa, L1_xattn_Wv_ipa, L1_ffn_Wg_s, L1_ffn_Wu_s, L1_ffn_Wd_s, L1_ffn_Wg, L1_ffn_Wu, L1_ffn_Wd, L1_ffn_Wr, L1_ffn_rb):
    import jax
    import jax.numpy as jnp

    def _L0_xattn_ref(query, key_value, Wq, bq, Wk, bk, Wv, bv, Wo, bo):
        import jax, jax.numpy as jnp
        import numpy as np
        NUM_HEADS = 16
        CLAMP = 10000.0
        B, Nq, Cq = query.shape
        Nkv = key_value.shape[1]
        H = NUM_HEADS
        D = Cq // H
        scale = D ** (-0.5)
        q = (query @ Wq + bq).reshape(B, Nq, H, D).transpose(0, 2, 1, 3)
        k = (key_value @ Wk + bk).reshape(B, Nkv, H, D).transpose(0, 2, 1, 3)
        v = (key_value @ Wv + bv).reshape(B, Nkv, H, D).transpose(0, 2, 1, 3)
        attn = jnp.einsum('bhqd,bhkd->bhqk', q, k) * scale
        attn = jnp.clip(attn, -CLAMP, CLAMP)
        attn = jax.nn.softmax(attn, axis=-1)
        attn = jnp.where(jnp.any(jnp.isnan(attn)), jnp.asarray(1.0 / Nkv, attn.dtype), attn)
        x = jnp.einsum('bhqk,bhkd->bqhd', attn, v).reshape(B, Nq, Cq)
        return x @ Wo + bo

    def _L0_ffn_ref(x, ln_gamma, ln_beta, abel_w, abel_b, moe_gate_w, moe_gate_b, ew1, eb1, ew2, eb2, gens, gc_w, gc_b):
        import jax, jax.numpy as jnp
        import numpy as np
        from jax.scipy.linalg import expm
        B, S, D, E, K, NROT = (2, 512, 256, 8, 2, 3)
        EPS = 1e-05

        def _gelu(x):
            return jax.nn.gelu(x, approximate=False)

        def _forward(x, ln_gamma, ln_beta, abel_w, abel_b, moe_gate_w, moe_gate_b, ew1, eb1, ew2, eb2, gens, gc_w, gc_b):
            residual = x
            mu = jnp.mean(x, axis=-1, keepdims=True)
            var = jnp.mean((x - mu) ** 2, axis=-1, keepdims=True)
            xn = (x - mu) * jax.lax.rsqrt(var + EPS) * ln_gamma + ln_beta
            abel_out = _gelu(xn @ abel_w + abel_b)
            logits = xn @ moe_gate_w + moe_gate_b
            topw, topi = jax.lax.top_k(logits, K)
            topw = jax.nn.softmax(topw, axis=-1)
            w_dense = jnp.sum(jax.nn.one_hot(topi, E, dtype=xn.dtype) * topw[..., None], axis=-2)
            h = _gelu(jnp.einsum('bsd,edh->ebsh', xn, ew1) + eb1[:, None, None, :])
            eo = jnp.einsum('ebsh,ehd->ebsd', h, ew2) + eb2[:, None, None, :]
            moe_out = jnp.einsum('ebsd,bse->bsd', eo, w_dense)
            for i in range(NROT):
                moe_out = moe_out @ expm(gens[i])
            combined = jnp.concatenate([abel_out, moe_out], axis=-1)
            gate = jax.nn.sigmoid(combined @ gc_w + gc_b)
            mixed = abel_out * (1.0 - gate) + moe_out * gate
            return residual + mixed
        return _forward(x, ln_gamma, ln_beta, abel_w, abel_b, moe_gate_w, moe_gate_b, ew1, eb1, ew2, eb2, gens, gc_w, gc_b)

    def _L1_xattn_ref(x, context, Wq, Wk, Wv, Wo, bo, q_down, q_up, q_alpha, k_down, k_up, k_alpha, v_down, v_up, v_alpha, o_down, o_up, o_alpha, Wk_ipa, Wv_ipa):
        import jax, jax.numpy as jnp
        import numpy as np
        HEADS = 16
        DIM_HEAD = 64
        RANK = 32
        LORA_W = 1.0
        IPA_SCALE = 1.0
        IPA_TOKENS = 4
        SCALE = DIM_HEAD ** (-0.5)

        def _split_heads(t):
            b, n, _ = t.shape
            return t.reshape(b, n, HEADS, DIM_HEAD).transpose(0, 2, 1, 3)

        def _merge_heads(t):
            b, h, n, d = t.shape
            return t.transpose(0, 2, 1, 3).reshape(b, n, h * d)

        def _attention(q_in, k_in, v_in):
            q = _split_heads(q_in)
            k = _split_heads(k_in)
            v = _split_heads(v_in)
            s = jnp.einsum('bhid,bhjd->bhij', q, k) * SCALE
            p = jax.nn.softmax(s, axis=-1)
            o = jnp.einsum('bhij,bhjd->bhid', p, v)
            return _merge_heads(o)

        def _lora(t, down, up, alpha):
            return t @ down @ up * (LORA_W * alpha[0] / RANK)
        q_in = x @ Wq + _lora(x, q_down, q_up, q_alpha)
        end = context.shape[1] - IPA_TOKENS
        org_ctx = context[:, :end, :]
        ipa_ctx = context[:, end:, :]
        k_in = org_ctx @ Wk + _lora(org_ctx, k_down, k_up, k_alpha)
        v_in = org_ctx @ Wv + _lora(org_ctx, v_down, v_up, v_alpha)
        out = _attention(q_in, k_in, v_in)
        ipa_k = ipa_ctx @ Wk_ipa
        ipa_v = ipa_ctx @ Wv_ipa
        out_ipa = _attention(q_in, ipa_k, ipa_v)
        out = out + IPA_SCALE * out_ipa
        return out @ Wo + bo + _lora(out, o_down, o_up, o_alpha)

    def _L1_ffn_ref(x, Wg_s, Wu_s, Wd_s, Wg, Wu, Wd, Wr, rb):
        import jax, jax.numpy as jnp
        import numpy as np
        B, S, H, I, E_ROUTED, TOP_K = (8, 512, 256, 512, 8, 2)

        def _expert(x, Wg, Wu, Wd):
            return jax.nn.silu(x @ Wg.T) * (x @ Wu.T) @ Wd.T
        shared = _expert(x, Wg_s, Wu_s, Wd_s)
        logits = jnp.einsum('bsh,eh->bse', x, Wr) + rb
        probs = jax.nn.sigmoid(logits)
        scores, idx = jax.lax.top_k(probs, TOP_K)
        cw = (jax.nn.one_hot(idx, E_ROUTED, dtype=x.dtype) * scores[..., None]).sum(-2)
        out = shared
        for e in range(E_ROUTED):
            out = out + cw[..., e:e + 1] * _expert(x, Wg[e], Wu[e], Wd[e])
        return out
    x = x + jnp.tanh(g_xattn[0]) * _L0_xattn_ref(_layernorm(x, axis=-1), ctx_768, L0_xattn_Wq, L0_xattn_bq, L0_xattn_Wk, L0_xattn_bk, L0_xattn_Wv, L0_xattn_bv, L0_xattn_Wo, L0_xattn_bo)
    x = x + jnp.tanh(g_ffn[0]) * _L0_ffn_ref(_layernorm(x, axis=-1), L0_ffn_ln_gamma, L0_ffn_ln_beta, L0_ffn_abel_w, L0_ffn_abel_b, L0_ffn_moe_gate_w, L0_ffn_moe_gate_b, L0_ffn_ew1, L0_ffn_eb1, L0_ffn_ew2, L0_ffn_eb2, L0_ffn_gens, L0_ffn_gc_w, L0_ffn_gc_b)
    x = x + jnp.tanh(g_xattn[1]) * _L1_xattn_ref(_layernorm(x, axis=-1), ctx_768, L1_xattn_Wq, L1_xattn_Wk, L1_xattn_Wv, L1_xattn_Wo, L1_xattn_bo, L1_xattn_q_down, L1_xattn_q_up, L1_xattn_q_alpha, L1_xattn_k_down, L1_xattn_k_up, L1_xattn_k_alpha, L1_xattn_v_down, L1_xattn_v_up, L1_xattn_v_alpha, L1_xattn_o_down, L1_xattn_o_up, L1_xattn_o_alpha, L1_xattn_Wk_ipa, L1_xattn_Wv_ipa)
    x = x + jnp.tanh(g_ffn[1]) * _L1_ffn_ref(_layernorm(x, axis=-1), L1_ffn_Wg_s, L1_ffn_Wu_s, L1_ffn_Wd_s, L1_ffn_Wg, L1_ffn_Wu, L1_ffn_Wd, L1_ffn_Wr, L1_ffn_rb)
    return x

_drawn_inputs = setup_inputs


def setup_inputs(seed=0):
    import zlib

    import numpy as np

    out = dict(_drawn_inputs(seed))
    spreads = {'g_ffn': (-1.0, 0.6),
     'L0_xattn_bq': (0.0, 0.482),
     'L0_xattn_bk': (0.0, 2.0),
     'L0_xattn_bv': (0.0, 0.1),
     'L0_xattn_bo': (0.0, 0.1),
     'L1_xattn_bo': (0.0, 0.1),
     'L1_ffn_rb': (0.0, 0.883)}
    factors = {'L0_ffn_ln_gamma': 6.859,
     'L0_ffn_ln_beta': 5.552,
     'L0_ffn_abel_b': 5.017,
     'L0_ffn_moe_gate_b': 4.202,
     'L0_ffn_eb1': 8.0,
     'L0_ffn_eb2': 3.678,
     'L0_ffn_gc_w': 8.0,
     'L1_xattn_Wq': 3.057,
     'L1_xattn_Wk': 6.98,
     'L1_xattn_q_down': 8.0,
     'L1_xattn_q_up': 8.0,
     'L1_xattn_k_down': 8.0,
     'L1_xattn_k_up': 8.0,
     'L1_xattn_Wk_ipa': 3.339,
     'L1_ffn_Wr': 2.669}
    for name, (base, spread) in spreads.items():
        noise = np.random.default_rng([zlib.crc32(name.encode()), seed]).standard_normal(out[name].shape)
        drawn = base * np.exp(spread * noise) if base else spread * noise
        out[name] = jnp.asarray(drawn.astype(out[name].dtype))
    for name, factor in factors.items():
        out[name] = (out[name] * factor).astype(out[name].dtype)
    return out
```

```python
from contextlib import ExitStack

import concourse.bass as bass
from concourse import mybir

F32 = mybir.dt.float32
F16 = mybir.dt.float16
U32 = mybir.dt.uint32
ALU = mybir.AluOpType
ACT = mybir.ActivationFunctionType
AX = mybir.AxisListType

B, S, C = 8, 112, 256
KV, CKV = 375, 192
H = 16
KC = CKV // 2
CHUNK = 125
NCH = KV // CHUNK
T = B * S
HT = T // 2
E = 8
FF = 512
NM = FF // 128
WS = 64.0
CLAMP = 10000.0
EPS = 1e-5
IPA = 4
ORG = KV - IPA
RANK = 32
HS = 16.0
OS = 16.0
SQ, DEG = 2, 8
PARTS = ((0, 0), (0, 1), (1, 0))

ROW = {}
_at = 0
for _n, _l in (("bq", C), ("bo0", C), ("abel_b", C), ("gate_b", E), ("bo1", C), ("rb", E)):
    ROW[_n] = (_at, _l)
    _at += _l
ROWS = _at

PA0 = {"Wq": (0, C), "Wo": (2 * C, C), "abel": (4 * C, C), "gate": (6 * C, E), "router1": (6 * C + 2 * E, E)}
PA0_N = 6 * C + 4 * E
STAGE_N = 3072

LN_SMALL = 7


class Layer:

    def __init__(self, index, dim):
        self.index, self.dim = index, dim
        self.width = H * dim
        self.tiles = self.width // 128
        self.qt = min(4, self.tiles)
        self.per_tile = 128 // dim
        self.vw = min(512, self.width)
        self.keys = KV if index == 0 else ORG
        nq = self.tiles // self.qt
        self.q_units = [("q", g) for g in range(nq)]
        self.k_units = [("k", t) for t in range(self.tiles)]
        self.v_units = [("v", c, w) for c in range(NCH) for w in range(self.width // self.vw)]
        self.i_units = [("i",)] if index else []
        self.front = self.q_units + self.k_units + self.i_units + self.v_units
        self.out = [("t", g) for g in range(nq)] + [("o",)]
        if index == 0:
            at = {0: 0, 1: 1, 2: 2, 3: 6, 4: 8, 5: 10}
            out_at = {0: 4, 1: 7}
        else:
            at = {n: n for n in range(len(self.front))}
            at = {n: min(15, n) for n in range(len(self.front))}
            out_at = {0: 4, 1: 5, 2: 8}
        self.steps = [[] for _ in range(H)]
        for n, u in enumerate(self.front):
            self.steps[at[n]].append(("front", u))
        for n, u in enumerate(self.out):
            self.steps[out_at[n]].append(("out", u))

    def units(self, kinds):
        n, found = 0, []
        for h in range(H):
            for kind, u in self.steps[h]:
                if kind in kinds:
                    found.append((h, kind, u, n))
                    n += 1
        return found


def acts(u):
    return u[0] not in ("i", "o")


def build(nc, a, out):
    ctx = ExitStack()
    with ctx:
        def sb(name, shape, dt=F32):
            return ctx.enter_context(nc.sbuf_tensor(name, shape, dt))

        def sem(name):
            return ctx.enter_context(nc.semaphore(name))

        X = sb("X", [S, B, C])
        Y = sb("Y", [S, B, C])
        Z = sb("Z", [S, B, C])
        xT = sb("xT", [128, 2, 2, T], F16)
        cT = sb("cT", [KC + 1, 2, 2, B * KV], F16)
        ST = sb("ST", [128, 2, STAGE_N])
        W0 = sb("W0", [128, 2, PA0_N], F16)
        WKV0 = sb("WKV0", [KC + 1, 2, 4 * C], F16)
        RW = sb("RW", [1, 2, ROWS], F16)
        W1 = sb("W1", [128, 2, 8 * 1024], F16)
        qz = sb("qz", [128, 2, 2, H, S], F16)
        KT = sb("KT", [128, 12288], F16)
        V = sb("V", [128, 2, 2, NCH, 1024], F16)
        WI1 = KT[0:KC, 0:8192].rearrange("p (q n) -> p q n", q=2)
        flat = ST[:, :, :].rearrange("p a n -> p (a n)")
        P_ = flat[0:S, 0:2 * KV].rearrange("p (a n) -> p a n", a=2)
        SC = flat[0:S, 768:768 + 2 * KV].rearrange("p (a n) -> p a n", a=2)
        OB = flat[0:S, 1536:1536 + 1024]
        PT = flat[0:CHUNK, 2560:2560 + 2 * NCH * S].bitcast(F16)\
            .rearrange("p (a q c n) -> p a q c n", a=2, q=2, c=NCH)
        OT = flat[:, 3328:3328 + 8 * S].bitcast(F16).rearrange("p (q t n) -> p q t n", q=2, t=8)
        qu = flat[:, 4352:4352 + 4 * S].bitcast(F16).rearrange("p (a q t n) -> p a q t n", a=2, q=2, t=2)
        mask = sb("mask", [128, 8], F16)
        qflat = qz[:, :, :, :, :].rearrange("p a q h n -> p (a q h n)")
        hf = qflat[:, 0:4 * HT].bitcast(F32).rearrange("p (a n) -> p a n", a=2)
        sg = qflat[:, 4 * HT:8 * HT].bitcast(F32).rearrange("p (a n) -> p a n", a=2)
        identf = sb("identf", [128, 128])
        ones16 = sb("ones16", [1, 512], F16)
        os16 = sb("os16", [1, S], F16)
        iota8 = sb("iota8", [S, E])
        nm = sb("nm", [S, 4])
        sums = sb("sums", [S, 2, H])
        rinv = sb("rinv", [S, H])
        tg = sb("tg", [S, 4])
        tgs = sb("tgs", [S, 4])
        lora_s = sb("lora_s", [128, 4])
        gc_b = sb("gc_b", [S, 1])
        stats = sb("stats", [S, B, 6])
        mv = sb("mv", [S, B, 2])
        lnc = sb("lnc", [S, LN_SMALL, B])
        lg = sb("lg", [S, B, E])
        m8 = sb("m8", [S, B, 8])
        i8 = sb("i8", [S, B, 8], U32)
        i8f = sb("i8f", [S, B, 8])
        oh = sb("oh", [S, 2, B, E])
        w12 = sb("w12", [S, 4, B])
        wd = sb("wd", [S, B, E + 1])
        wdT = sb("wdT", [E, 2, T], F16)
        gam = sb("gam", [S, 4, C])
        b1 = sb("b1", [128, E, NM])
        bcur = sb("bcur", [128, 2, NM])
        KI = sb("KI", [128, 2, 8, B * IPA], F16)
        zi = sb("zi", [S, 3, H, IPA])
        pn = sb("pn", [S, 2, H, IPA])
        si = sb("si", [S, 3, H])
        eb2 = sb("eb2", [E, 2, C], F16)
        zz = sb("zz", [S, 3, B])

        pb = [ctx.enter_context(nc.psum_tensor(f"pb{i}", [128, 512], F32)) for i in range(8)]
        SB_, TB_, OBK, GB = pb[0:2], pb[2:4], pb[4:6], pb[6:8]

        vi_dram = nc.dram_tensor("vi_scratch", [B * IPA, 2, 1024], F16).ap()

        kT = [[KT[:, (2 * p + q) * 3000:(2 * p + q + 1) * 3000].rearrange("p (t k) -> p t k", t=8)
               for q in range(2)] for p in range(2)]
        MW = KT[:, :].rearrange("p (u q n) -> p u q n", u=2, q=2)
        VF = V[:, :, :, :, :].rearrange("p a b c d -> p (a b c d)")
        HTt = VF[:, 0:2 * 2 * NM * HT].rearrange("p (u q m n) -> p u q m n", u=2, q=2, m=NM)

        AB = VF[0:S, 7168:7168 + 2 * B * C].bitcast(F32).rearrange("p (b c) -> p b c", b=B)
        junk = flat[0:S, 0:2 * B * C].rearrange("p (a b c) -> p a b c", a=2, b=B)
        KF = KT[:, :].rearrange("p (u n) -> p u n", u=4)
        BT = KF[:, 0, :].rearrange("p (q g k n) -> p q g k n", q=2, g=3, k=2)
        R16 = KF[:, 1, :].rearrange("p (q g k n) -> p q g k n", q=2, g=3, k=2)
        RT = KF[:, 2, :].rearrange("p (q g k n) -> p q g k n", q=2, g=3, k=2)
        RF = KF[:, 3, :].bitcast(F32).rearrange("p (g k n) -> p g k n", g=3, k=2)
        eye = sg[:, :, :].rearrange("p a b -> p (a b)")[:, 0:512]

        def w0(name, q, k):
            o, n = PA0[name]
            return W0[:, q, o + k * n:o + (k + 1) * n]

        def row(name, q):
            o, n = ROW[name]
            return RW[0:1, q, o:o + n]

        def bc(ap, shape):
            return ap.broadcast_to(shape)

        names = """x_in small_in ident_set const_set ones_set
            tanh_done lora_scale
            chunk_lora_mm chunk_added chunk_hi chunk_lo
            ln_stats ln_aggr ln_small ln_sqrt ln_norm ln_tmm ln_thi ln_tlo
            ipa_mm ipa_hi ipa_lo ipa_stored ipa_ctx ffn""".split()
        s = {n: sem(n) for n in names}
        s["chunk_in"] = [sem("chunk_in0"), sem("chunk_in1")]
        for L in range(2):
            for n in """s_mm clip_done mx_done exp_done t_mm hi_done lo_done pv_mm g_mm g_hi g_free
                    qz_done o_rd r_done x_up ipa_patch ipa_z ipa_m ipa_e ipa_s ipa_r ipa_pn vi_in""".split():
                s[f"{n}{L}"] = sem(f"{n}{L}")
            for n in """m_in0 m_in1 m_hi m_lo u_mm u_act u_hf u_hi u_lo d_mm acc_done
                    up_sg rt_mm rt_lg rt_m8 rt_i8 rt_sm rt_wd rt_act f_mm f_act f_dve""".split():
                s[f"{n}_{L}"] = sem(f"{n}_{L}")
        for n in "e_mm e_hi e_lo e_f e_in".split():
            s[n] = sem(n)

        layers = [Layer(0, 16), Layer(1, 64)]

        LD = VF[0:RANK, 0:2 * 4992].rearrange("p (q n) -> p q n", q=2)
        LO = {}
        o = 0
        for n_, l_ in (("qd", C), ("qu", 1024), ("kd", CKV), ("ku", 1024),
                       ("vd", CKV), ("vu", 1024), ("od", 1024), ("ou", C)):
            LO[n_] = (o, l_)
            o += l_
        LORA_N = o

        def lo_(name, q, a0, n):
            return LD[:, q, LO[name][0] + a0:LO[name][0] + a0 + n]

        chunks0 = [
            (128, PA0_N, a["pa0"], W0[:, 0, :], W0[:, 1, :], []),
            (KC + 1, 4 * C, a["kv0"], WKV0[:, 0, :], WKV0[:, 1, :], []),
            (1, ROWS, a["rows"], RW[:, 0, :], RW[:, 1, :], []),
            (E, C, a["eb2"], eb2[:, 0, :], eb2[:, 1, :], []),
        ]
        for k in range(2):
            for g in range(2):
                c0, c1 = g * 4 * KV, (g + 1) * 4 * KV
                chunks0.append((KC, 4 * KV, a["ctxT"][k * KC:(k + 1) * KC, c0:c1],
                                cT[0:KC, 0, k, c0:c1], cT[0:KC, 1, k, c0:c1], []))
        half = LORA_N // 2
        chunks1 = [
            (RANK, half, a["lora"][:, 0:half], LD[:, 0, 0:half], LD[:, 1, 0:half], []),
            (RANK, half, a["lora"][:, half:LORA_N], LD[:, 0, half:LORA_N], LD[:, 1, half:LORA_N], []),
        ]
        specs = [("q", 0, 128, C, 1024, "qd", "qu"), ("k", 1, KC, CKV, 1024, "kd", "ku"),
                 ("v", 2, KC, CKV, 1024, "vd", "vu"), ("o", 3, 128, 1024, C, "od", "ou")]
        for name, j, rows, kk, cols, dn, up in specs:
            lora = []
            for kt in range(kk // rows):
                for c0 in range(0, cols, 512):
                    w = min(512, cols)
                    lora.append((kt * cols + c0, w, rows,
                                 [lo_(dn, q, kt * rows, rows) for q in range(2)],
                                 [lo_(up, q, c0, w) for q in range(2)], j))
            chunks1.append((rows, 2048, a["w1" + name], W1[0:rows, 0, j * 2048:(j + 1) * 2048],
                            W1[0:rows, 1, j * 2048:(j + 1) * 2048], lora))
        for j, name in enumerate(("ki", "vi")):
            chunks1.append((KC, 2048, a["w1" + name], WI1[:, 0, j * 2048:(j + 1) * 2048],
                            WI1[:, 1, j * 2048:(j + 1) * 2048], []))
        chunks = chunks0 + chunks1
        lora_before = [sum(len(c[5]) for c in chunks[:n]) for n in range(len(chunks) + 1)]

        def chunks_sync(sp, first, last):
            for n in range(first, last):
                rows, cols, src, hi, lo, lora = chunks[n]
                if n >= 2:
                    sp.wait_ge(s["chunk_lo"], n - 1)
                sp.dma_start(ST[0:rows, n % 2, 0:cols], src).then_inc(s["chunk_in"][n % 2], 16)

        def chunk_arrived(eng, n):
            eng.wait_ge(s["chunk_in"][n % 2], 16 * (n // 2 + 1))

        def chunks_tensor(pe, first, last):
            for n in range(first, last):
                for j, (c0, w, rows, dn, up, _) in enumerate(chunks[n][5]):
                    k = lora_before[n] + j
                    if j == 0 and k == 0:
                        pe.wait_ge(s["chunk_lo"], len(chunks0) + 2)
                    if k >= 2:
                        pe.wait_ge(s["chunk_added"], k - 1)
                    for i, (qa, qb) in enumerate(PARTS):
                        mm = pe.matmul(GB[k % 2][0:rows, 0:w], dn[qa], up[qb], start=(i == 0), stop=(i == 2))
                    mm.then_inc(s["chunk_lora_mm"], 1)

        def chunks_vector(dve, first, last):
            for n in range(first, last):
                rows, cols, src, hi, lo, lora = chunks[n]
                for j, (c0, w, r, dn, up, which) in enumerate(lora):
                    k = lora_before[n] + j
                    if j == 0:
                        chunk_arrived(dve, n)
                    if k == 0:
                        dve.wait_ge(s["lora_scale"], 1)
                    dve.wait_ge(s["chunk_lora_mm"], k + 1)
                    part = ST[0:rows, n % 2, c0:c0 + w]
                    dve.scalar_tensor_tensor(part, GB[k % 2][0:rows, 0:w], lora_s[0:rows, which:which + 1],
                                             part, ALU.mult, ALU.add).then_inc(s["chunk_added"], 1)
                dve.wait_ge(s["chunk_hi"], n + 1)
                dve.scalar_tensor_tensor(lo, ST[0:rows, n % 2, 0:cols], WS if n not in plain else 1.0, hi,
                                         ALU.mult, ALU.subtract).then_inc(s["chunk_lo"], 1)

        def chunks_scalar(act, first, last):
            for n in range(first, last):
                rows, cols, src, hi, lo, lora = chunks[n]
                chunk_arrived(act, n)
                if lora:
                    act.wait_ge(s["chunk_added"], lora_before[n + 1])
                act.activation(hi, ST[0:rows, n % 2, 0:cols], ACT.Copy,
                               scale=WS if n not in plain else 1.0).then_inc(s["chunk_hi"], 1)

        plain = set(range(4, 8))
        NC0, NC1 = len(chunks0), len(chunks)

        def norm_vector(dve, r, src, dst):
            st_, ag_, sm_, nn_ = s["ln_stats"], s["ln_aggr"], s["ln_small"], s["ln_norm"]
            if r:
                dve.wait_ge(nn_, B * r)
            for b in range(B):
                dve.bn_stats(stats[:, b, :], src[:, b, :]).then_inc(st_, 1)
            dve.wait_ge(st_, B * (r + 1))
            for b in range(B):
                dve.bn_aggr(mv[:, b, :], stats[:, b, :]).then_inc(ag_, 1)
            dve.wait_ge(ag_, B * (r + 1))
            k = 6 * r
            dve.tensor_scalar(lnc[:, 0, :], mv[:, :, 1], EPS, None, ALU.add).then_inc(sm_, 1)
            dve.wait_ge(s["ln_sqrt"], r + 1)
            dve.reciprocal(lnc[:, 2, :], lnc[:, 1, :]).then_inc(sm_, 1)
            dve.wait_ge(sm_, k + 2)
            dve.tensor_tensor(lnc[:, 3, :], lnc[:, 2, :], lnc[:, 2, :], ALU.mult).then_inc(sm_, 1)
            dve.wait_ge(sm_, k + 3)
            dve.tensor_tensor(lnc[:, 4, :], lnc[:, 3, :], lnc[:, 0, :], ALU.mult).then_inc(sm_, 1)
            dve.wait_ge(sm_, k + 4)
            dve.tensor_scalar(lnc[:, 5, :], lnc[:, 4, :], -0.5, 1.5, ALU.mult, ALU.add).then_inc(sm_, 1)
            dve.wait_ge(sm_, k + 5)
            dve.tensor_tensor(lnc[:, 6, :], lnc[:, 5, :], lnc[:, 2, :], ALU.mult).then_inc(sm_, 1)
            dve.wait_ge(sm_, k + 6)
            for b in range(B):
                dve.tensor_scalar(dst[:, b, :], src[:, b, :], mv[:, b, 0:1], lnc[:, 6, b:b + 1],
                                  ALU.subtract, ALU.mult).then_inc(nn_, 1)

        def norm_scalar(act, r):
            act.wait_ge(s["ln_small"], 6 * r + 1)
            act.activation(lnc[:, 1, :], lnc[:, 0, :], ACT.Sqrt).then_inc(s["ln_sqrt"], 1)

        GROUPS = [(k, g) for g in range(2) for k in range(2)]

        def turn_tensor(pe, r, src):
            for n, (k, g) in enumerate(GROUPS):
                i = 4 * r + n
                if i >= 2:
                    pe.wait_ge(s["ln_tlo"], i - 1)
                for j in range(4):
                    mm = pe.transpose(GB[i % 2][:, j * S:(j + 1) * S], src[:, 4 * g + j, k * 128:(k + 1) * 128],
                                      identf[0:S, 0:S])
                mm.then_inc(s["ln_tmm"], 1)

        def turn_scalar(act, r):
            for n, (k, g) in enumerate(GROUPS):
                i = 4 * r + n
                act.wait_ge(s["ln_tmm"], i + 1)
                act.activation(xT[:, 0, k, g * HT:(g + 1) * HT], GB[i % 2][:, 0:HT], ACT.Copy)\
                   .then_inc(s["ln_thi"], 1)

        def turn_vector(dve, r):
            for n, (k, g) in enumerate(GROUPS):
                i = 4 * r + n
                dve.wait_ge(s["ln_thi"], i + 1)
                dve.scalar_tensor_tensor(xT[:, 1, k, g * HT:(g + 1) * HT], GB[i % 2][:, 0:HT], 1.0,
                                         xT[:, 0, k, g * HT:(g + 1) * HT], ALU.mult, ALU.subtract)\
                   .then_inc(s["ln_tlo"], 1)

        def psum_out(L, h):
            per = 512 // L.dim
            return OBK[h // per][0:S, (h % per) * L.dim:(h % per + 1) * L.dim]

        def counts(L):
            F, U = len(L.front), len(L.front) + len(L.out)
            hiF = sum(acts(u) for u in L.front)
            hiU = hiF + sum(acts(u) for u in L.out)
            return F, U, hiF, hiU

        def unit_numbers(L, where, bv, bs):
            F, U, hiF, hiU = counts(L)
            if where == "first":
                kinds, n0, s0, h0 = ("front",), F, F, hiF
            elif where == "last":
                kinds, n0, h0 = ("out",), 2 * F + (bv - 1) * U, 2 * hiF + (bv - 1) * hiU
                s0 = 2 * F + (bs - 1) * U
            else:
                kinds, n0, h0 = ("front", "out"), 2 * F + (bv - 1) * U, 2 * hiF + (bv - 1) * hiU
                s0 = 2 * F + (bs - 1) * U
            found, done = [], 0
            for h, kind, u, n in L.units(kinds):
                found.append((h, kind, u, n0 + n, s0 + n, h0 + done))
                done += acts(u)
            return found

        def prologue_units(L):
            found, done = [], 0
            for n, u in enumerate(L.front):
                found.append((0, "front", u, n, n, done))
                done += acts(u)
            return found

        def tail_units(L):
            F, U, hiF, hiU = counts(L)
            n0, h0 = 2 * F + (B - 2) * U + len(L.out), 2 * hiF + (B - 2) * hiU + (hiU - hiF)
            found, done = [], 0
            for n, u in enumerate(L.out):
                found.append((0, "out", u, n0 + n, n0 + n, h0 + done))
                done += acts(u)
            return found

        def front_done(L, bv, bs, which):
            F, U, _, _ = counts(L)
            last = {"q": len(L.q_units), "k": len(L.q_units) + len(L.k_units),
                    "i": len(L.q_units) + len(L.k_units) + len(L.i_units), "v": len(L.front)}[which]
            if isinstance(bs, int) and bs == 0:
                return last
            if bs == 1 and isinstance(bv, int):
                return F + last
            order = [u for _, kind, u, n in L.units(("front", "out")) if True]
            number = {("front", u) if kind == "front" else ("out", u): n
                      for _, kind, u, n in L.units(("front", "out"))}
            u = L.front[last - 1]
            inner = number[("front", u)] + 1
            return 2 * F + (bv - 2) * U + inner

        def attention_tensor(pe, L):
            l = L.index
            g_mm, g_free = s[f"g_mm{l}"], s[f"g_free{l}"]
            dq = C if l == 0 else 1024

            def wq(q, k, t):
                return w0("Wq", q, k)[:, t * 128:(t + 1) * 128] if l == 0 else \
                    W1[:, q, k * 1024 + t * 128:k * 1024 + (t + 1) * 128]

            def wk(q, k, t):
                if l == 0:
                    return WKV0[0:KC + k, q, k * C + t * 128:k * C + (t + 1) * 128]
                return W1[0:KC, q, 2048 + k * 1024 + t * 128:2048 + k * 1024 + (t + 1) * 128]

            def wv(q, k, w):
                if l == 0:
                    return WKV0[0:KC + k, q, 2 * C + k * C:2 * C + (k + 1) * C]
                return W1[0:KC, q, 4096 + k * 1024 + w * 512:4096 + k * 1024 + (w + 1) * 512]

            def wo(q, t):
                return w0("Wo", q, t) if l == 0 else W1[:, q, 6144 + t * C:6144 + (t + 1) * C]

            def unit(kind, u, n, ns, bv, bs, behind=1):
                bank = GB[ns % 2]
                if ns >= 2:
                    pe.wait_ge(g_free, n - 1)
                rows = KC + 1 if l == 0 else KC
                if u[0] == "q":
                    for t in range(L.qt):
                        i = 0
                        for k in range(2):
                            for qa, qb in PARTS:
                                mm = pe.matmul(bank[:, t * S:(t + 1) * S], wq(qa, k, u[1] * 4 + t),
                                               xT[:, qb, k, bass.ds(bv * S, S)], start=(i == 0),
                                               stop=(i == 5 and l == 1))
                                i += 1
                        if l == 0:
                            for q in range(2):
                                mm = pe.matmul(bank[:, t * S:(t + 1) * S], row("bq", q)[:, t * 128:(t + 1) * 128],
                                               ones16[:, 0:S], start=False, stop=(q == 1))
                elif u[0] == "k":
                    i = 0
                    for k in range(2):
                        for qa, qb in PARTS:
                            kr = KC + (k if l == 0 else 0)
                            mm = pe.matmul(bank[:, 0:L.keys], wk(qa, k, u[1]),
                                           cT[0:kr, qb, k, bass.ds(bv * KV, L.keys)], start=(i == 0), stop=(i == 5))
                            i += 1
                elif u[0] == "v":
                    m = min(CHUNK, L.keys - u[1] * CHUNK)
                    i = 0
                    for k in range(2):
                        for qa, qb in PARTS:
                            kr = KC + (k if l == 0 else 0)
                            mm = pe.matmul(bank[0:m, 0:L.vw], cT[0:kr, qa, k, bass.ds(bv * KV + u[1] * CHUNK, m)],
                                           wv(qb, k, u[2]), start=(i == 0), stop=(i == 5))
                            i += 1
                elif u[0] == "i":
                    pe.wait_ge(g_free, front_done(L, bv, bs, "q"))
                    for h in range(H):
                        for i, (qa, qb) in enumerate(PARTS):
                            mm = pe.matmul(bank[0:S, h * IPA:(h + 1) * IPA], qz[:, bs % 2, qa, h, :],
                                           KI[:, qb, h // 2, bass.ds(bv * IPA, IPA)], start=(i == 0), stop=(i == 2))
                elif u[0] == "t":
                    if u[1] == 0:
                        pe.wait_ge(s[f"o_rd{l}"], bv + 1)
                    for j in range(L.qt):
                        c0 = (u[1] * 4 + j) * 128
                        mm = pe.transpose(bank[:, j * S:(j + 1) * S], OB[:, c0:c0 + 128], identf[0:S, 0:S])
                else:
                    pe.wait_ge(g_free, n - behind + 1)
                    i, last = 0, 3 * L.tiles - 1
                    for t in range(L.tiles):
                        for qa, qb in PARTS:
                            pe.matmul(bank[0:S, 0:C], OT[:, qa, t, :], wo(qb, t), start=(i == 0), stop=False)
                            i += 1
                    for q in range(2):
                        mm = pe.matmul(bank[0:S, 0:C], (os16 if l else ones16)[:, 0:S], row(f"bo{l}", q), start=False, stop=(q == 1))
                mm.then_inc(g_mm, 1)

            def scores(bv, bs, h):
                i, st = bv * H + h, bs * H + h
                if h == 0:
                    pe.wait_ge(g_free, front_done(L, bv, bs, "k"))
                    if l == 0:
                        pe.wait_ge(s["qz_done0"], 4 * bv + 4)
                if st >= 2:
                    pe.wait_ge(s["clip_done0"] if l == 0 else s["exp_done1"], i - 1)
                for n, (qa, qb) in enumerate(PARTS):
                    mm = pe.matmul(SB_[st % 2][0:S, 0:L.keys], qz[:, bs % 2, qa, h, :],
                                   kT[bs % 2][qb][:, h // L.per_tile, 0:L.keys], start=(n == 0), stop=(n == 2))
                mm.then_inc(s[f"s_mm{l}"], 1)

            def turn(i, st):
                pe.wait_ge(s["exp_done0"] if l == 0 else s["ipa_patch1"], i + 1)
                if st >= 2:
                    pe.wait_ge(s[f"lo_done{l}"], i - 1)
                for c in range(NCH):
                    mm = pe.transpose(TB_[st % 2][0:CHUNK, c * S:(c + 1) * S],
                                      P_[:, st % 2, c * CHUNK:(c + 1) * CHUNK], identf[0:S, 0:S])
                mm.then_inc(s[f"t_mm{l}"], 1)

            def weigh(bv, bs, h):
                i, st = bv * H + h, bs * H + h
                if h == 0:
                    pe.wait_ge(g_free, front_done(L, bv, bs, "v"))
                    if l == 1:
                        pe.wait_ge(s[f"vi_in{bs % 2}"], (bv - bs % 2) * 16 + 32)
                    if bs >= 1:
                        pe.wait_ge(s[f"o_rd{l}"], bv)
                pe.wait_ge(s[f"lo_done{l}"], i + 1)
                n = 0
                for c in range(NCH):
                    for qa, qb in PARTS:
                        mm = pe.matmul(psum_out(L, h), PT[:, st % 2, qa, c, :],
                                       V[0:CHUNK, bs % 2, qb, c, h * L.dim:(h + 1) * L.dim],
                                       start=(n == 0), stop=(n == 8))
                        n += 1
                mm.then_inc(s[f"pv_mm{l}"], 1)

            def batch(where, bv, bs):
                todo = unit_numbers(L, where, bv, bs)
                at = {u: ns for _, kind, u, n, ns, _ in todo if kind == "out"}
                behind = at[L.out[-1]] - at[L.out[-2]] if at else 1
                for h in range(H):
                    scores(bv, bs, h)
                    for hh, kind, u, n, ns, _ in todo:
                        if hh == h:
                            d = 1 if kind == "front" else -1
                            unit(kind, u, n, ns, bv + d, bs + d, behind)
                    if bs or h >= 2:
                        turn(bv * H + h - 2, bs * H + h - 2)
                    if bs or h >= 3:
                        if h >= 3:
                            weigh(bv, bs, h - 3)
                        else:
                            weigh(bv - 1, bs - 1, H + h - 3)

            for _, kind, u, n, ns, _ in prologue_units(L):
                unit(kind, u, n, ns, 0, 0)
            batch("first", 0, 0)
            with pe.Fori(0, (B - 2) // 2) as r:
                b = r * 2 + 1
                batch("middle", b, 1)
                batch("middle", b + 1, 2)
            batch("last", B - 1, B - 1)
            for i in range(B * H - 2, B * H):
                turn(i, i)
                weigh(B - 1, B - 1, i - 1 - (B - 1) * H)
            weigh(B - 1, B - 1, H - 1)
            for _, kind, u, n, ns, _ in tail_units(L):
                unit(kind, u, n, ns, B - 1, B - 1)

        QSCALE = {0: 0.25 / WS, 1: 0.125 / WS}

        def q_cuts(L, u, bs):
            for side in range(2):
                r = slice(64 * side, 64 * side + 64)
                h0 = 8 * u[1] + side
                yield (r, lambda q, r=r, h0=h0: qz[r, bs % 2, q, h0:h0 + 7:2, :])

        def attention_scalar(act, L):
            l = L.index
            g_mm, g_hi = s[f"g_mm{l}"], s[f"g_hi{l}"]

            def unit(kind, u, n, ns, bv, bs):
                if not acts(u):
                    return
                bank = GB[ns % 2]
                act.wait_ge(g_mm, n + 1)
                if u[0] == "q" and l == 0:
                    act.activation(qu[:, bs % 2, 0, :, :], bank[:, 0:2 * S].rearrange("p (t n) -> p t n", t=2),
                                   ACT.Copy, scale=QSCALE[0]).then_inc(g_hi, 1)
                elif u[0] == "q":
                    for side, (r, dst) in enumerate(q_cuts(L, u, bs)):
                        x = act.activation(dst(0), bank[r, 0:4 * S].rearrange("p (t n) -> p t n", t=4),
                                           ACT.Copy, scale=QSCALE[1])
                        if side:
                            x.then_inc(g_hi, 1)
                elif u[0] == "k":
                    act.activation(kT[bs % 2][0][:, u[1], 0:L.keys], bank[:, 0:L.keys], ACT.Copy,
                                   scale=1.0 / WS).then_inc(g_hi, 1)
                elif u[0] == "v":
                    m = min(CHUNK, L.keys - u[1] * CHUNK)
                    act.activation(V[0:m, bs % 2, 0, u[1], u[2] * 512:u[2] * 512 + L.vw], bank[0:m, 0:L.vw],
                                   ACT.Copy, scale=1.0 / WS).then_inc(g_hi, 1)
                else:
                    g = u[1]
                    act.activation(OT[:, 0, g * L.qt:(g + 1) * L.qt, :],
                                   bank[:, 0:L.qt * S].rearrange("p (t n) -> p t n", t=L.qt), ACT.Copy)\
                       .then_inc(g_hi, 1)

            def exps(bv, bs, h):
                i, st = bv * H + h, bs * H + h
                act.wait_ge(s[f"mx_done{l}"], i + 1)
                if st >= 2:
                    act.wait_ge(s[f"t_mm{l}"], i - 1)
                if h == 0 and bs >= 2:
                    act.wait_ge(s[f"o_rd{l}"], bv - 1)
                src = SC[:, st % 2, :] if l == 0 else SB_[st % 2][0:S, 0:L.keys]
                act.activation(P_[:, st % 2, 0:L.keys], src, ACT.Exp, bias=nm[:, st % 4:st % 4 + 1], scale=1.0,
                               accum_out=sums[:, bs % 2, h:h + 1]).then_inc(s[f"exp_done{l}"], 1)

            def hi(i, st):
                act.wait_ge(s[f"t_mm{l}"], i + 1)
                if st >= 2:
                    act.wait_ge(s[f"pv_mm{l}"], i - 1)
                act.activation(PT[:, st % 2, 0, :, :], TB_[st % 2][0:CHUNK, 0:NCH * S]
                               .rearrange("p (c n) -> p c n", c=NCH), ACT.Copy).then_inc(s[f"hi_done{l}"], 1)

            def ipa_exp(bv, bs):
                act.wait_ge(s["ipa_z1"], bv + 1)
                act.activation(zi[:, 1, :, :], zi[:, 0, :, :], ACT.Exp).then_inc(s["ipa_e1"], 1)

            def batch(where, bv, bs):
                todo = unit_numbers(L, where, bv, bs)
                for h in range(H):
                    exps(bv, bs, h)
                    if bs or h >= 2:
                        hi(bv * H + h - 2, bs * H + h - 2)
                    for hh, kind, u, n, ns, nh in todo:
                        if hh == h:
                            d = 1 if kind == "front" else -1
                            unit(kind, u, n, ns, bv + d, bs + d)
                            if u[0] == "i":
                                ipa_exp(bv + d, bs + d)

            for _, kind, u, n, ns, nh in prologue_units(L):
                unit(kind, u, n, ns, 0, 0)
                if u[0] == "i":
                    ipa_exp(0, 0)
            batch("first", 0, 0)
            with act.Fori(0, (B - 2) // 2) as r:
                b = r * 2 + 1
                batch("middle", b, 1)
                batch("middle", b + 1, 2)
            batch("last", B - 1, B - 1)
            for i in range(B * H - 2, B * H):
                hi(i, i)
            for _, kind, u, n, ns, nh in tail_units(L):
                unit(kind, u, n, ns, B - 1, B - 1)

        def attention_vector(dve, L):
            l = L.index
            g_mm, g_hi, g_free = s[f"g_mm{l}"], s[f"g_hi{l}"], s[f"g_free{l}"]
            step = ALU.mult, ALU.subtract

            def unit(kind, u, n, ns, nh, bv, bs):
                bank = GB[ns % 2]
                if acts(u):
                    dve.wait_ge(g_hi, nh + 1)
                else:
                    dve.wait_ge(g_mm, n + 1)
                if u[0] == "q" and l == 0:
                    x = dve.scalar_tensor_tensor(qu[:, bs % 2, 1, :, :],
                                                 bank[:, 0:2 * S].rearrange("p (t n) -> p t n", t=2), QSCALE[0],
                                                 qu[:, bs % 2, 0, :, :], *step)
                elif u[0] == "q":
                    for r, dst in q_cuts(L, u, bs):
                        x = dve.scalar_tensor_tensor(dst(1), bank[r, 0:4 * S].rearrange("p (t n) -> p t n", t=4),
                                                     QSCALE[1], dst(0), *step)
                elif u[0] == "k":
                    x = dve.scalar_tensor_tensor(kT[bs % 2][1][:, u[1], 0:L.keys], bank[:, 0:L.keys], 1.0 / WS,
                                                 kT[bs % 2][0][:, u[1], 0:L.keys], *step)
                elif u[0] == "v":
                    m = min(CHUNK, L.keys - u[1] * CHUNK)
                    c = slice(u[2] * 512, u[2] * 512 + L.vw)
                    x = dve.scalar_tensor_tensor(V[0:m, bs % 2, 1, u[1], c], bank[0:m, 0:L.vw], 1.0 / WS,
                                                 V[0:m, bs % 2, 0, u[1], c], *step)
                elif u[0] == "t":
                    t = slice(u[1] * L.qt, (u[1] + 1) * L.qt)
                    x = dve.scalar_tensor_tensor(OT[:, 1, t, :],
                                                 bank[:, 0:L.qt * S].rearrange("p (t n) -> p t n", t=L.qt), 1.0,
                                                 OT[:, 0, t, :], *step)
                elif u[0] == "o":
                    xb = X[:, bass.ds(bv, 1), :]
                    x = dve.scalar_tensor_tensor(xb, bank[0:S, 0:C].rearrange("p (a n) -> p a n", a=1),
                                                 tgs[:, l:l + 1], xb, ALU.mult, ALU.add)
                else:
                    sc = bank[0:S, 0:H * IPA].rearrange("p (h j) -> p h j", h=H)
                    if bs >= 1:
                        dve.wait_ge(s["ipa_pn1"], bv)
                    dve.tensor_reduce(si[:, 0, :], sc, AX.X, ALU.max).then_inc(s["ipa_m1"], 1)
                    dve.wait_ge(s["ipa_m1"], bv + 1)
                    dve.tensor_tensor(zi[:, 0, :, :], sc, bc(si[:, 0, :].unsqueeze(2), [S, H, IPA]),
                                      ALU.subtract).then_inc(s["ipa_z1"], 1)
                    dve.wait_ge(s["ipa_z1"], bv + 1)
                    x = dve.tensor_copy(si[:, 0, 0:1], si[:, 0, 1:2])
                x.then_inc(g_free, 1)

            def ipa_rest(bv, bs):
                dve.wait_ge(s["ipa_e1"], bv + 1)
                dve.tensor_reduce(si[:, 1, :], zi[:, 1, :, :], AX.X, ALU.add).then_inc(s["ipa_s1"], 1)
                dve.wait_ge(s["ipa_s1"], bv + 1)
                dve.reciprocal(si[:, 2, :], si[:, 1, :]).then_inc(s["ipa_r1"], 1)
                dve.wait_ge(s["ipa_r1"], bv + 1)
                if bs >= 2:
                    dve.wait_ge(s["ipa_patch1"], (bv - 1) * H)
                dve.tensor_tensor(pn[:, bs % 2, :, :], zi[:, 1, :, :], bc(si[:, 2, :].unsqueeze(2), [S, H, IPA]),
                                  ALU.mult).then_inc(s["ipa_pn1"], 1)

            def maxima(bv, bs, h):
                i, st = bv * H + h, bs * H + h
                dve.wait_ge(s[f"s_mm{l}"], i + 1)
                src = SB_[st % 2][0:S, 0:L.keys]
                if l == 0:
                    if st >= 2:
                        dve.wait_ge(s["exp_done0"], i - 1)
                    dve.tensor_scalar(SC[:, st % 2, :], src, CLAMP, -CLAMP, ALU.min, ALU.max)\
                       .then_inc(s["clip_done0"], 1)
                    dve.wait_ge(s["clip_done0"], i + 1)
                    src = SC[:, st % 2, :]
                dve.tensor_reduce(nm[:, st % 4:st % 4 + 1], src, AX.X, ALU.max, negate=True)\
                   .then_inc(s[f"mx_done{l}"], 1)

            def lo(i, st):
                dve.wait_ge(s[f"hi_done{l}"], i + 1)
                dve.scalar_tensor_tensor(PT[:, st % 2, 1, :, :], TB_[st % 2][0:CHUNK, 0:NCH * S]
                                         .rearrange("p (c n) -> p c n", c=NCH), 1.0, PT[:, st % 2, 0, :, :],
                                         *step).then_inc(s[f"lo_done{l}"], 1)

            def normalise(bv, bs):
                dve.wait_ge(s[f"pv_mm{l}"], bv * H + H)
                if bs >= 1:
                    dve.wait_ge(s[f"o_rd{l}"], bv)
                dve.reciprocal(rinv[:, :], sums[:, bs % 2, :]).then_inc(s[f"r_done{l}"], 1)
                dve.wait_ge(s[f"r_done{l}"], bv + 1)
                per = min(H, 512 // L.dim)
                for n in range(H // per):
                    w = per * L.dim
                    x = dve.scalar_tensor_tensor(
                        OB[:, n * w:(n + 1) * w].rearrange("p (h d) -> p h d", h=per),
                        OBK[n][0:S, 0:w].rearrange("p (h d) -> p h d", h=per), OS if l else 1.0,
                        bc(rinv[:, n * per:(n + 1) * per].unsqueeze(2), [S, per, L.dim]), ALU.mult, ALU.mult)
                x.then_inc(s[f"o_rd{l}"], 1)

            def batch(where, bv, bs):
                todo = unit_numbers(L, where, bv, bs)
                for h in range(H):
                    maxima(bv, bs, h)
                    if bs or h >= 2:
                        lo(bv * H + h - 2, bs * H + h - 2)
                    if bs and h == 3:
                        normalise(bv - 1, bs - 1)
                    for hh, kind, u, n, ns, nh in todo:
                        if hh == h:
                            d = 1 if kind == "front" else -1
                            unit(kind, u, n, ns, nh, bv + d, bs + d)
                            if u[0] == "i":
                                ipa_rest(bv + d, bs + d)

            for _, kind, u, n, ns, nh in prologue_units(L):
                unit(kind, u, n, ns, nh, 0, 0)
                if u[0] == "i":
                    ipa_rest(0, 0)
            batch("first", 0, 0)
            with dve.Fori(0, (B - 2) // 2) as r:
                b = r * 2 + 1
                batch("middle", b, 1)
                batch("middle", b + 1, 2)
            batch("last", B - 1, B - 1)
            for i in range(B * H - 2, B * H):
                lo(i, i)
            normalise(B - 1, B - 1)
            for _, kind, u, n, ns, nh in tail_units(L):
                unit(kind, u, n, ns, nh, B - 1, B - 1)

        def attention_gpsimd(pool, L):
            l = L.index
            if l == 0:
                def masks(bv, bs):
                    pool.wait_ge(s["g_free0"], front_done(L, bv, bs, "q"))
                    for q in range(2):
                        for t in range(2):
                            pool.tensor_tensor(qz[:, bs % 2, q, 8 * t:8 * t + 8, :],
                                               bc(qu[:, bs % 2, q, t, :].unsqueeze(1), [128, 8, S]),
                                               bc(mask[:, :].unsqueeze(2), [128, 8, S]), ALU.mult)\
                                .then_inc(s["qz_done0"], 1)
                masks(0, 0)
                masks(1, 1)
                with pool.Fori(1, B // 2) as r:
                    b = r * 2
                    masks(b, 2)
                    masks(b + 1, 3)
                return

            def patches(bv, bs):
                pool.wait_ge(s["ipa_pn1"], bv + 1)
                for h in range(H):
                    i, st = bv * H + h, bs * H + h
                    pool.wait_ge(s["exp_done1"], i + 1)
                    pool.tensor_tensor(P_[:, st % 2, ORG:KV], pn[:, bs % 2, h, :],
                                       bc(sums[:, bs % 2, h:h + 1], [S, IPA]), ALU.mult)\
                        .then_inc(s["ipa_patch1"], 1)
            patches(0, 0)
            with pool.Fori(0, (B - 2) // 2) as r:
                b = r * 2 + 1
                patches(b, 1)
                patches(b + 1, 2)
            patches(B - 1, B - 1)

        def attention_sync(sp, L):
            for b in range(B):
                if b >= 2:
                    sp.wait_ge(s["pv_mm1"], (b - 1) * H)
                for q in range(2):
                    sp.dma_start(V[CHUNK - IPA:CHUNK, b % 2, q, NCH - 1, :],
                                 vi_dram[b * IPA:(b + 1) * IPA, q, :]).then_inc(s[f"vi_in{b % 2}"], 16)

        cI = [[cT[0:KC, q, k, :].rearrange("p (b n) -> p b n", b=B)[:, :, ORG:KV] for k in range(2)] for q in range(2)]
        vi_sb = hf[0:B * IPA, :, :].rearrange("p a b -> p (a b)").bitcast(F16)[:, 0:1024]
        vi_sb2 = sg[0:B * IPA, :, :].rearrange("p a b -> p (a b)").bitcast(F16)[:, 0:1024]
        ci_sb = hf[0:KC, 1, 0:2 * 2 * B * IPA // 2].bitcast(F16).rearrange("p (q k n) -> p q k n", q=2, k=2)

        def ipa_tensor(pe):
            for t in range(8):
                if t >= 2:
                    pe.wait_ge(s["ipa_lo"], t - 1)
                i = 0
                for k in range(2):
                    for qa, qb in PARTS:
                        mm = pe.matmul(GB[t % 2][:, 0:B * IPA], WI1[:, qa, k * 1024 + t * 128:k * 1024 + (t + 1) * 128],
                                       ci_sb[:, qb, k, :], start=(i == 0), stop=(i == 5))
                        i += 1
                mm.then_inc(s["ipa_mm"], 1)
            for w in range(2):
                pe.wait_ge(s["ipa_lo"], 7 + w)
                i = 0
                for k in range(2):
                    for qa, qb in PARTS:
                        mm = pe.matmul(GB[w % 2][0:B * IPA, :], ci_sb[:, qa, k, :],
                                       WI1[:, qb, 2048 + k * 1024 + w * 512:2048 + k * 1024 + (w + 1) * 512],
                                       start=(i == 0), stop=(i == 5))
                        i += 1
                mm.then_inc(s["ipa_mm"], 1)

        def ipa_scalar(act):
            for t in range(8):
                act.wait_ge(s["ipa_mm"], t + 1)
                act.activation(KI[:, 0, t, :], GB[t % 2][:, 0:B * IPA], ACT.Copy, scale=1.0 / WS)\
                   .then_inc(s["ipa_hi"], 1)
            for w in range(2):
                act.wait_ge(s["ipa_mm"], 9 + w)
                act.activation(vi_sb[:, w * 512:(w + 1) * 512], GB[w % 2][0:B * IPA, :], ACT.Copy, scale=1.0 / WS)\
                   .then_inc(s["ipa_hi"], 1)

        def ipa_vector(dve):
            for t in range(8):
                dve.wait_ge(s["ipa_hi"], t + 1)
                dve.scalar_tensor_tensor(KI[:, 1, t, :], GB[t % 2][:, 0:B * IPA], 1.0 / WS, KI[:, 0, t, :],
                                         ALU.mult, ALU.subtract).then_inc(s["ipa_lo"], 1)
            for w in range(2):
                dve.wait_ge(s["ipa_hi"], 9 + w)
                dve.scalar_tensor_tensor(vi_sb2[:, w * 512:(w + 1) * 512], GB[w % 2][0:B * IPA, :], 1.0 / WS,
                                         vi_sb[:, w * 512:(w + 1) * 512], ALU.mult, ALU.subtract)\
                   .then_inc(s["ipa_lo"], 1)

        def router_tensor(pe, l, turned):
            name, bias = ("gate", "gate_b") if l == 0 else ("router1", "rb")
            pe.wait_ge(s["ln_tlo"], turned)
            for b in range(B):
                dst = pb[4][0:S, b * E:(b + 1) * E]
                i = 0
                for k in range(2):
                    for qa, qb in PARTS:
                        pe.matmul(dst, xT[:, qa, k, b * S:(b + 1) * S], w0(name, qb, k), start=(i == 0), stop=False)
                        i += 1
                for q in range(2):
                    mm = pe.matmul(dst, ones16[:, 0:S], row(bias, q), start=False, stop=(q == 1))
            mm.then_inc(s[f"rt_mm_{l}"], 1)

        def router_scalar(act, l):
            if l == 0:
                act.wait_ge(s["rt_sm_0"], 1)
                act.activation(w12[:, 0, :], w12[:, 2, :], ACT.Sigmoid).then_inc(s["rt_act_0"], 1)
            else:
                act.wait_ge(s["rt_mm_1"], 1)
                act.activation(lg[:, :, :], pb[4][0:S, 0:B * E].rearrange("p (b e) -> p b e", b=B), ACT.Sigmoid,
                               scale=1.0 / WS).then_inc(s["rt_lg_1"], 1)

        def router_vector(dve, l):
            sm, n = s[f"rt_sm_{l}"], 0
            if l == 0:
                dve.wait_ge(s["rt_mm_0"], 1)
                dve.tensor_scalar(lg[:, :, :], pb[4][0:S, 0:B * E].rearrange("p (b e) -> p b e", b=B), 1.0 / WS,
                                  None, ALU.mult).then_inc(s["rt_lg_0"], 1)
            dve.wait_ge(s[f"rt_lg_{l}"], 1)
            for b in range(B):
                dve.max(m8[:, b, :], lg[:, b, :]).then_inc(s[f"rt_m8_{l}"], 1)
            for b in range(B):
                dve.wait_ge(s[f"rt_m8_{l}"], b + 1)
                dve.max_index(i8[:, b, :], m8[:, b, :], lg[:, b, :]).then_inc(s[f"rt_i8_{l}"], 1)
            dve.wait_ge(s[f"rt_i8_{l}"], B)
            if l == 0:
                dve.tensor_tensor(w12[:, 2, :], m8[:, :, 0], m8[:, :, 1], ALU.subtract).then_inc(sm, 1)
            else:
                dve.tensor_copy(w12[:, 0, :], m8[:, :, 0]).then_inc(sm, 1)
            dve.tensor_copy(i8f[:, :, :], i8[:, :, :]).then_inc(sm, 1)
            dve.wait_ge(sm, 2)
            for j in range(2):
                dve.tensor_tensor(oh[:, j, :, :], bc(iota8[:, :].unsqueeze(1), [S, B, E]),
                                  bc(i8f[:, :, j:j + 1], [S, B, E]), ALU.is_equal).then_inc(sm, 1)
            if l == 0:
                dve.wait_ge(s["rt_act_0"], 1)
                dve.tensor_scalar(w12[:, 1, :], w12[:, 0, :], -1.0, 1.0, ALU.mult, ALU.add).then_inc(sm, 1)
            else:
                dve.tensor_copy(w12[:, 1, :], m8[:, :, 1]).then_inc(sm, 1)
            dve.wait_ge(sm, 5)
            for j in range(2):
                dve.tensor_tensor(oh[:, j, :, :], oh[:, j, :, :], bc(w12[:, j, :].unsqueeze(2), [S, B, E]),
                                  ALU.mult).then_inc(sm, 1)
            dve.wait_ge(sm, 7)
            o = l
            dve.tensor_tensor(lg[:, :, :], oh[:, 0, :, :], oh[:, 1, :, :], ALU.add).then_inc(sm, 1)
            dve.wait_ge(sm, 8)
            dve.tensor_scalar(wd[:, :, o:o + E], lg[:, :, :], 1.0 / (WS * HS) if l else 1.0 / WS, None, ALU.mult)\
               .then_inc(s[f"rt_wd_{l}"], 1)
            if l == 1:
                dve.memset(wd[:, :, 0:1], 1.0 / (WS * HS)).then_inc(s["rt_wd_1"], 1)

        def expert_order(e, first, last_split):
            todo = [("up", 0, 0)]
            if not first:
                todo.append(("down", -1, 1))
            if not last_split:
                todo.append(("cut", 1, 0))
            return todo + [("up", 0, 1), ("down", 0, 0)]

        def experts(eng, n, work):
            work("cut", 0, 0, 0)
            def turn(ev, es, first, last):
                for kind, d, half in expert_order(es, first, last):
                    work(kind, ev + d, es + d, half)
            turn(0, 0, True, False)
            pairs = (n - 2) // 2
            with eng.Fori(0, pairs) as r:
                turn(r * 2 + 1, 1, False, False)
                turn(r * 2 + 2, 2, False, False)
            for e in range(1 + 2 * pairs, n):
                turn(e, e, False, e == n - 1)
            work("down", n - 1, n - 1, 1)

        def up_col(l, part, k, m):
            if part == 2:
                return (2 if l else 1) * 1024 + k * C
            return part * 1024 + k * FF + m * 128

        def experts_tensor(pe, l, n):
            def work(kind, ev, es, half):
                if kind == "up":
                    u0, us = (ev * 2 + half) * NM, (es * 2 + half) * NM
                    if half == 0:
                        pe.wait_ge(s[f"m_lo_{l}"], ev + 1)
                    for m in range(NM):
                        if us + m >= 2:
                            pe.wait_ge(s[f"u_hf_{l}"] if l else s[f"u_act_{l}"], u0 + m - 1)
                        for part in range(1 + l):
                            i = 0
                            for k in range(2):
                                for qa, qb in PARTS:
                                    c = up_col(l, part, k, m)
                                    mm = pe.matmul(pb[2 * part + m % 2][:, 0:HT], MW[:, es % 2, qa, c:c + 128],
                                                   xT[:, qb, k, half * HT:(half + 1) * HT],
                                                   start=(i == 0), stop=(i == 5))
                                    i += 1
                        mm.then_inc(s[f"u_mm_{l}"], 1)
                elif kind == "down":
                    d0, dst = (ev * 2 + half) * 4, (es * 2 + half) * 4
                    pe.wait_ge(s[f"u_lo_{l}"], d0 + 4)
                    for j in range(4):
                        if dst + j >= 2:
                            pe.wait_ge(s[f"acc_done_{l}"], d0 + j - 1)
                        i = 0
                        for k in range(NM):
                            for qa, qb in PARTS:
                                c = up_col(l, 2, k, 0)
                                mm = pe.matmul(OBK[j % 2][0:S, 0:C], HTt[:, half, qa, k, j * S:(j + 1) * S],
                                               MW[:, es % 2, qb, c:c + C], start=(i == 0), stop=(i == 3 * NM - 1))
                                i += 1
                        mm.then_inc(s[f"d_mm_{l}"], 1)
            experts(pe, n, work)

        MN = [2048, 3072]

        def experts_scalar(act, l, n):
            def work(kind, ev, es, half):
                if kind == "cut":
                    act.wait_ge(s[f"m_in{es % 2}_{l}"], (ev + 2 - es % 2) * 8)
                    if es >= 2:
                        act.wait_ge(s[f"d_mm_{l}"], (ev - 1) * 8)
                    act.activation(MW[:, es % 2, 0, 0:MN[l]], ST[:, es % 2, 0:MN[l]], ACT.Copy, scale=WS)\
                       .then_inc(s[f"m_hi_{l}"], 1)
                elif kind == "up":
                    u0, us = (ev * 2 + half) * NM, (es * 2 + half) * NM
                    for m in range(NM):
                        act.wait_ge(s[f"u_mm_{l}"], u0 + m + 1)
                        if us + m >= 2:
                            act.wait_ge(s[f"u_hf_{l}"] if l else s[f"u_lo_{l}"], u0 + m - 1)
                        if l == 0:
                            act.activation(hf[:, m % 2, :], pb[m % 2][:, 0:HT], ACT.Gelu,
                                           bias=bcur[:, es % 2, m:m + 1], scale=1.0 / WS)\
                               .then_inc(s["u_act_0"], 1)
                        else:
                            act.activation(sg[:, m % 2, :], pb[m % 2][:, 0:HT], ACT.Silu, scale=1.0 / WS)\
                               .then_inc(s["u_act_1"], 1)
            experts(act, n, work)

        def experts_vector(dve, l, n, ready):
            def work(kind, ev, es, half):
                if kind == "cut":
                    dve.wait_ge(s[f"m_hi_{l}"], ev + 1)
                    if l == 0:
                        dve.tensor_copy(bcur[:, es % 2, :], b1[:, bass.ds(ev, 1), :].rearrange("p a m -> p (a m)"))
                    dve.scalar_tensor_tensor(MW[:, es % 2, 1, 0:MN[l]], ST[:, es % 2, 0:MN[l]], WS,
                                             MW[:, es % 2, 0, 0:MN[l]], ALU.mult, ALU.subtract)\
                       .then_inc(s[f"m_lo_{l}"], 1)
                elif kind == "up":
                    u0, us = (ev * 2 + half) * NM, (es * 2 + half) * NM
                    for m in range(NM):
                        n_, ns = u0 + m, us + m
                        dve.wait_ge(s[f"u_act_{l}"], n_ + 1)
                        if l == 1:
                            if ns >= 2:
                                dve.wait_ge(s["u_lo_1"], n_ - 1)
                            dve.scalar_tensor_tensor(hf[:, m % 2, :], pb[2 + m % 2][:, 0:HT], HS / WS, sg[:, m % 2, :],
                                                     ALU.mult, ALU.mult).then_inc(s["u_hf_1"], 1)
                            dve.wait_ge(s["u_hf_1"], n_ + 1)
                        if m == 0 and es >= 1:
                            dve.wait_ge(s[f"d_mm_{l}"], ((ev - 1) * 2 + half + 1) * 4)
                        dve.tensor_copy(HTt[:, half, 0, m, :], hf[:, m % 2, :]).then_inc(s[f"u_hi_{l}"], 1)
                        dve.wait_ge(s[f"u_hi_{l}"], n_ + 1)
                        dve.tensor_tensor(HTt[:, half, 1, m, :], hf[:, m % 2, :], HTt[:, half, 0, m, :],
                                          ALU.subtract).then_inc(s[f"u_lo_{l}"], 1)
                else:
                    d0, dst = (ev * 2 + half) * 4, (es * 2 + half) * 4
                    for j in range(4):
                        b = half * 4 + j
                        dve.wait_ge(s[f"d_mm_{l}"], d0 + j + 1)
                        if dst + j >= 8:
                            dve.wait_ge(s[f"acc_done_{l}"], d0 + j - 7)
                        elif dst + j == 0:
                            dve.wait_ge(*ready)
                        dve.scalar_tensor_tensor(Z[:, b, :], OBK[j % 2][0:S, 0:C], wd[:, b, bass.ds(ev, 1)], Z[:, b, :],
                                                 ALU.mult, ALU.add).then_inc(s[f"acc_done_{l}"], 1)
            experts(dve, n, work)

        def experts_sync(sp, l, n):
            for e in range(n):
                if e >= 2:
                    sp.wait_ge(s[f"m_lo_{l}"], e - 1)
                sp.dma_start(ST[:, e % 2, 0:MN[l]], a[f"moe{l}"][e, :, :]).then_inc(s[f"m_in{e % 2}_{l}"], 16)

        def abel_tensor(pe):
            for b in range(B):
                if b >= 2:
                    pe.wait_ge(s["f_act_0"], b - 1)
                i = 0
                for k in range(2):
                    for qa, qb in PARTS:
                        pe.matmul(GB[b % 2][0:S, 0:C], xT[:, qa, k, b * S:(b + 1) * S], w0("abel", qb, k),
                                  start=(i == 0), stop=False)
                        i += 1
                for q in range(2):
                    mm = pe.matmul(GB[b % 2][0:S, 0:C], ones16[:, 0:S], row("abel_b", q), start=False, stop=(q == 1))
                mm.then_inc(s["f_mm_0"], 1)
            pe.wait_ge(s["rt_wd_0"], 1)
            for g in range(2):
                for j in range(4):
                    mm = pe.transpose(pb[4 + g][0:E, j * S:(j + 1) * S], wd[:, 4 * g + j, 0:E], identf[0:S, 0:S])
                mm.then_inc(s["f_mm_0"], 1)
            pe.wait_ge(s["f_dve_0"], 2)
            pe.wait_ge(s["f_act_0"], B)
            for b in range(B):
                if b >= 2:
                    pe.wait_ge(s["f_dve_0"], 2 + b - 1)
                for i, (qa, qb) in enumerate(PARTS):
                    mm = pe.matmul(GB[b % 2][0:S, 0:C], wdT[:, qa, b * S:(b + 1) * S], eb2[:, qb, :],
                                   start=(i == 0), stop=(i == 2))
                mm.then_inc(s["f_mm_0"], 1)

        def abel_scalar(act):
            for b in range(B):
                act.wait_ge(s["f_mm_0"], b + 1)
                act.activation(AB[:, b, :], GB[b % 2][0:S, 0:C], ACT.Gelu, scale=1.0 / WS).then_inc(s["f_act_0"], 1)
            for g in range(2):
                act.wait_ge(s["f_mm_0"], B + g + 1)
                act.activation(wdT[:, 0, g * HT:(g + 1) * HT], pb[4 + g][0:E, 0:HT], ACT.Copy, scale=WS)\
                   .then_inc(s["f_act_0"], 1)

        def abel_vector(dve):
            for g in range(2):
                dve.wait_ge(s["f_act_0"], B + g + 1)
                dve.scalar_tensor_tensor(wdT[:, 1, g * HT:(g + 1) * HT], pb[4 + g][0:E, 0:HT], WS,
                                         wdT[:, 0, g * HT:(g + 1) * HT], ALU.mult, ALU.subtract)\
                   .then_inc(s["f_dve_0"], 1)
            for b in range(B):
                dve.wait_ge(s["f_mm_0"], B + 2 + b + 1)
                dve.tensor_scalar(Z[:, b, :], GB[b % 2][0:S, 0:C], 1.0 / WS, None, ALU.mult)\
                   .then_inc(s["f_dve_0"], 1)

        EU = []
        for t in range(DEG - 1, 0, -1):
            EU += [("horner", g, t) for g in range(3)]
        for _ in range(SQ):
            EU += [("turn", g, 0) for g in range(3)] + [("square", g, 0) for g in range(3)]
        EU += [("turn", 0, 0), ("turn", 1, 0), ("pair", 1, 0), ("pair", 0, 0)]

        def expm_tensor(pe):
            pe.wait_ge(s["e_lo"], 4)
            for n, (kind, g, t) in enumerate(EU):
                bank = pb[n % 3]
                if kind == "pair":
                    pe.wait_ge(s["e_lo"], 4 + n)
                elif n >= 3:
                    pe.wait_ge(s["e_lo"], 4 + n - 2)
                if kind == "turn":
                    for c in range(2):
                        for m in range(2):
                            mm = pe.transpose(bank[:, c * 256 + m * 128:c * 256 + (m + 1) * 128],
                                              RF[:, g, m, c * 128:(c + 1) * 128], identf[:, :])
                else:
                    left = BT if kind == "horner" else RT
                    right = 2 if kind == "pair" else g
                    for m in range(2):
                        i = 0
                        for k in range(2):
                            for qa, qb in PARTS:
                                mm = pe.matmul(bank[:, m * 256:(m + 1) * 256], left[:, qa, g, k, m * 128:(m + 1) * 128],
                                               R16[:, qb, right, k, :], start=(i == 0), stop=(i == 5))
                                i += 1
                mm.then_inc(s["e_mm"], 1)

        flatg = ST[:, :, 0:3 * 512].rearrange("p a (g n) -> p a g n", g=3)

        def expm_scalar(act):
            act.wait_ge(s["e_in"], 32)
            act.activation(BT[:, 0, :, :, :].rearrange("p g k n -> p g (k n)"), flatg[:, 0, :, :], ACT.Copy,
                           scale=WS / 2 ** SQ).then_inc(s["e_hi"], 1)
            for g in range(3):
                act.wait_ge(s["e_f"], 2 + g + 1)
                act.activation(R16[:, 0, g, :, :], RF[:, g, :, :], ACT.Copy).then_inc(s["e_hi"], 1)
            nf = 0
            for n, (kind, g, t) in enumerate(EU):
                dst = (RT if kind == "turn" else R16)[:, 0, 2 if kind == "pair" else g, :, :]
                if kind == "turn":
                    act.wait_ge(s["e_mm"], n + 1)
                    src = pb[n % 3][:, :].rearrange("p (k n) -> p k n", k=2)
                else:
                    nf += 1
                    act.wait_ge(s["e_f"], 5 + nf)
                    src = RF[:, 2 if kind == "pair" else g, :, :]
                act.activation(dst, src, ACT.Copy).then_inc(s["e_hi"], 1)

        def expm_vector(dve):
            dve.memset(eye, 0.0).then_inc(s["e_f"], 1)
            dve.wait_ge(s["e_f"], 1)
            for k in range(2):
                x = dve.tensor_scalar(eye[:, k * 256 + k * 128:k * 256 + (k + 1) * 128], identf[:, :], WS, None, ALU.mult)
            x.then_inc(s["e_f"], 1)
            dve.wait_ge(s["e_f"], 2)
            dve.wait_ge(s["e_in"], 32)
            for g in range(3):
                dve.scalar_tensor_tensor(RF[:, g, :, :].rearrange("p k n -> p (k n)"), flatg[:, 1, g, :],
                                         WS / 2 ** SQ / DEG, eye, ALU.mult, ALU.add).then_inc(s["e_f"], 1)
            dve.wait_ge(s["e_hi"], 1)
            dve.scalar_tensor_tensor(BT[:, 1, :, :, :].rearrange("p g k n -> p g (k n)"), flatg[:, 0, :, :],
                                     WS / 2 ** SQ, BT[:, 0, :, :, :].rearrange("p g k n -> p g (k n)"),
                                     ALU.mult, ALU.subtract).then_inc(s["e_lo"], 1)
            for g in range(3):
                dve.wait_ge(s["e_hi"], 2 + g)
                dve.tensor_tensor(R16[:, 1, g, :, :], RF[:, g, :, :], R16[:, 0, g, :, :], ALU.subtract)\
                   .then_inc(s["e_lo"], 1)
            nf = 0
            for n, (kind, g, t) in enumerate(EU):
                r = 2 if kind == "pair" else g
                src = pb[n % 3][:, :].rearrange("p (k n) -> p k n", k=2)
                if kind == "turn":
                    dst, hi_ = RT[:, 1, g, :, :], RT[:, 0, g, :, :]
                else:
                    nf += 1
                    dve.wait_ge(s["e_mm"], n + 1)
                    if n >= 3:
                        dve.wait_ge(s["e_lo"], 4 + n - 2 if kind != "pair" else 4 + n)
                    if kind == "horner":
                        x = dve.scalar_tensor_tensor(RF[:, g, :, :].rearrange("p k n -> p (k n)"), pb[n % 3][:, :],
                                                     1.0 / (WS * t), eye, ALU.mult, ALU.add)
                    else:
                        x = dve.tensor_scalar(RF[:, r, :, :], src, 1.0 / WS, None, ALU.mult)
                    x.then_inc(s["e_f"], 1)
                    dve.wait_ge(s["e_f"], 5 + nf)
                    src, dst, hi_ = RF[:, r, :, :], R16[:, 1, r, :, :], R16[:, 0, r, :, :]
                dve.wait_ge(s["e_hi"], 4 + n + 1)
                dve.tensor_tensor(dst, src, hi_, ALU.subtract).then_inc(s["e_lo"], 1)

        def mix_tensor(pe, turned):
            pe.wait_ge(s["ln_tlo"], turned)
            pe.wait_ge(s["e_lo"], 4 + len(EU))
            for b in range(B):
                if b >= 2:
                    pe.wait_ge(s["f_dve_0"], 2 + B + b - 1)
                i = 0
                for k in range(2):
                    for qa, qb in PARTS:
                        mm = pe.matmul(GB[b % 2][0:S, 0:C], xT[:, qa, k, b * S:(b + 1) * S], R16[:, qb, 2, k, :],
                                       start=(i == 0), stop=(i == 5))
                        i += 1
                mm.then_inc(s["f_mm_0"], 1)

        def mix_scalar(act):
            act.wait_ge(s["ffn"], 2 + 2 * B + 2)
            act.activation(zz[:, 1, :], zz[:, 0, :], ACT.Sigmoid).then_inc(s["f_act_0"], 1)

        def mix_vector(dve):
            done = 2
            n0 = 2 + B
            for b in range(B):
                dve.wait_ge(s["f_mm_0"], B + 2 + B + b + 1)
                dve.tensor_scalar(Z[:, b, :], GB[b % 2][0:S, 0:C], 1.0 / WS, None, ALU.mult)\
                   .then_inc(s["f_dve_0"], 1)
            dve.wait_ge(s["f_dve_0"], n0 + B)
            for j, src in enumerate((AB, Z)):
                for b in range(B):
                    dve.tensor_tensor_reduce(junk[:, j, b, :], src[:, b, :], gam[:, 2 + j, :], 1.0, 0.0, ALU.mult,
                                             ALU.add, (zz[:, 0, :] if j == 0 else zz[:, 2, :])[:, b:b + 1])\
                       .then_inc(s["ffn"], 1)
            dve.wait_ge(s["ffn"], done + 2 * B)
            dve.tensor_tensor(zz[:, 0, :], zz[:, 0, :], zz[:, 2, :], ALU.add).then_inc(s["ffn"], 1)
            dve.wait_ge(s["ffn"], done + 2 * B + 1)
            dve.tensor_scalar(zz[:, 0, :], zz[:, 0, :], gc_b[:, 0:1], None, ALU.add).then_inc(s["ffn"], 1)
            dve.tensor_tensor(junk[:, 0, :, :], Z[:, :, :], AB[:, :, :], ALU.subtract).then_inc(s["ffn"], 1)
            dve.wait_ge(s["f_act_0"], B + 3)
            dve.wait_ge(s["ffn"], done + 2 * B + 3)
            for b in range(B):
                dve.scalar_tensor_tensor(junk[:, 1, b, :], junk[:, 0, b, :], zz[:, 1, b:b + 1], AB[:, b, :],
                                         ALU.mult, ALU.add).then_inc(s["ffn"], 1)
            dve.wait_ge(s["ffn"], done + 3 * B + 3)
            dve.tensor_tensor(Z[:, :, :], junk[:, 1, :, :], Y[:, :, :], ALU.add).then_inc(s["ffn"], 1)
            dve.wait_ge(s["ffn"], done + 3 * B + 4)
            dve.scalar_tensor_tensor(X[:, :, :].rearrange("p b c -> p (b c)"), Z[:, :, :].rearrange("p b c -> p (b c)"),
                                     tg[:, 1:2], X[:, :, :].rearrange("p b c -> p (b c)"), ALU.mult, ALU.add)\
               .then_inc(s["ffn"], 1)

        FFN0 = 2 + 3 * B + 5
        PHASES = a["phases"]
        G_ALL = [2 * counts(L)[0] + (B - 2) * counts(L)[1] + 2 * len(L.out) for L in layers]
        block = ctx.enter_context(nc.Block())

        @block.sync
        def _(sp):
            sp.dma_start(X[:, :, :], a["x"].rearrange("b s c -> s b c")).then_inc(s["x_in"], 16)
            sp.dma_start(tg[:, :], a["gates"].partition_broadcast(S)).then_inc(s["small_in"], 16)
            sp.dma_start(lora_s[:, :], a["alphas"].partition_broadcast(128)).then_inc(s["small_in"], 16)
            sp.dma_start(gam[:, :, :], a["vecs"].partition_broadcast(S)).then_inc(s["small_in"], 16)
            sp.dma_start(b1[:, :, :], a["eb1"]).then_inc(s["small_in"], 16)
            sp.dma_start(gc_b[:, :], a["gc_b"].partition_broadcast(S)).then_inc(s["small_in"], 16)
            chunks_sync(sp, 0, NC0)
            if PHASES >= 2:
                sp.wait_ge(s["g_free0"], G_ALL[0])
                experts_sync(sp, 0, E)
                sp.wait_ge(s["m_lo_0"], E)
                for j in range(2):
                    sp.dma_start(ST[:, j, 0:3 * 512], a["gens"][j, :, :]).then_inc(s["e_in"], 16)
            if PHASES >= 3:
                sp.wait_ge(s["ffn"], FFN0)
                chunks_sync(sp, NC0, NC1)
                sp.wait_ge(s["ipa_lo"], 10)
                for q, part in enumerate((vi_sb, vi_sb2)):
                    sp.dma_start(vi_dram[:, q, :], part).then_inc(s["ipa_stored"], 16)
                sp.wait_ge(s["ipa_stored"], 32)
                attention_sync(sp, layers[1])
            if PHASES >= 4:
                sp.wait_ge(s["g_free1"], G_ALL[1])
                experts_sync(sp, 1, E + 1)
            if PHASES == 1:
                sp.wait_ge(s["g_free0"], G_ALL[0])
            if PHASES == 2:
                sp.wait_ge(s["ffn"], FFN0)
            if PHASES == 3:
                sp.wait_ge(s["g_free1"], G_ALL[1])
            if PHASES == 4:
                sp.wait_ge(s["ffn"], FFN0 + 1)
            sp.dma_start(out.rearrange("b s c -> s b c"), X[:, :, :]).then_inc(s["x_in"], 16)
            sp.wait_ge(s["x_in"], 32)

        @block.gpsimd
        def _(pool):
            pool.memset(identf[:, :], 0.0).then_inc(s["ident_set"], 1)
            pool.wait_ge(s["ident_set"], 1)
            pool.affine_select(out=identf[:, :], in_=identf[:, :], compare_op=ALU.not_equal, fill=1.0, base=0,
                               pattern=[[-1, 128]], channel_multiplier=1).then_inc(s["ident_set"], 1)
            pool.memset(mask[:, :], 1.0).then_inc(s["ident_set"], 1)
            pool.wait_ge(s["ident_set"], 3)
            pool.affine_select(out=mask[:, :], in_=mask[:, :], compare_op=ALU.is_ge, fill=0.0, base=0,
                               pattern=[[-16, 8]], channel_multiplier=1).then_inc(s["ident_set"], 1)
            pool.wait_ge(s["ident_set"], 4)
            pool.affine_select(out=mask[:, :], in_=mask[:, :], compare_op=ALU.is_ge, fill=0.0, base=15,
                               pattern=[[16, 8]], channel_multiplier=-1).then_inc(s["ident_set"], 1)
            pool.iota(iota8[:, :], [[1, E]], base=0, channel_multiplier=0, allow_small_or_imprecise_dtypes=True)\
                .then_inc(s["ident_set"], 1)
            pool.wait_ge(s["ident_set"], 5)
            attention_gpsimd(pool, layers[0])
            if PHASES >= 3:
                pool.wait_ge(s["ipa_stored"], 32)
                pool.memset(qflat, 0.0).then_inc(s["const_set"], 1)
                attention_gpsimd(pool, layers[1])

        @block.scalar
        def _(act):
            norm_scalar(act, 0)
            act.wait_ge(s["small_in"], 16 * 5)
            act.activation(tg[:, :], tg[:, :], ACT.Tanh).then_inc(s["tanh_done"], 1)
            chunks_scalar(act, 0, NC0)
            turn_scalar(act, 0)
            attention_scalar(act, layers[0])
            if PHASES >= 2:
                norm_scalar(act, 1)
                norm_scalar(act, 2)
                turn_scalar(act, 1)
                router_scalar(act, 0)
                abel_scalar(act)
                experts_scalar(act, 0, E)
                turn_scalar(act, 2)
                expm_scalar(act)
                mix_scalar(act)
            if PHASES >= 3:
                norm_scalar(act, 3)
                chunks_scalar(act, NC0, NC1)
                turn_scalar(act, 3)
                ipa_scalar(act)
                act.wait_ge(s["const_set"], 1)
                attention_scalar(act, layers[1])
            if PHASES >= 4:
                norm_scalar(act, 4)
                turn_scalar(act, 4)
                router_scalar(act, 1)
                experts_scalar(act, 1, E + 1)

        @block.vector
        def _(dve):
            dve.memset(ones16[:, :], 1.0).then_inc(s["ones_set"], 1)
            dve.memset(os16[:, :], OS).then_inc(s["ones_set"], 1)
            dve.memset(cT[KC:KC + 1, 0, 1, :], 1.0).then_inc(s["ones_set"], 1)
            dve.memset(cT[KC:KC + 1, 1, 1, :], 0.0).then_inc(s["ones_set"], 1)
            dve.wait_ge(s["x_in"], 16)
            norm_vector(dve, 0, X, Y)
            chunks_vector(dve, 0, NC0)
            turn_vector(dve, 0)
            dve.wait_ge(s["tanh_done"], 1)
            dve.tensor_scalar(tgs[:, 0:1], tg[:, 0:1], 1.0 / WS, None, ALU.mult).then_inc(s["lora_scale"], 1)
            dve.tensor_scalar(tgs[:, 1:2], tg[:, 2:3], 1.0 / (WS * OS), None, ALU.mult).then_inc(s["lora_scale"], 1)
            dve.tensor_scalar(lora_s[:, :], lora_s[:, :], 1.0 / (RANK * WS * WS), None, ALU.mult)\
               .then_inc(s["lora_scale"], 1)
            dve.wait_ge(s["lora_scale"], 3)
            attention_vector(dve, layers[0])
            if PHASES >= 2:
                dve.wait_ge(s["g_free0"], G_ALL[0])
                norm_vector(dve, 1, X, Y)
                norm_vector(dve, 2, Y, Z)
                dve.wait_ge(s["ln_norm"], 3 * B)
                dve.tensor_tensor(Z[:, :, :], Z[:, :, :], bc(gam[:, 0:1, :], [S, B, C]), ALU.mult).then_inc(s["ffn"], 1)
                dve.wait_ge(s["ffn"], 1)
                dve.tensor_tensor(Z[:, :, :], Z[:, :, :], bc(gam[:, 1:2, :], [S, B, C]), ALU.add).then_inc(s["ffn"], 1)
                turn_vector(dve, 1)
                dve.wait_ge(s["ident_set"], 6)
                router_vector(dve, 0)
                abel_vector(dve)
                experts_vector(dve, 0, E, (s["f_dve_0"], 2 + B))
                turn_vector(dve, 2)
                expm_vector(dve)
                mix_vector(dve)
            if PHASES >= 3:
                dve.wait_ge(s["ffn"], FFN0)
                norm_vector(dve, 3, X, Y)
                chunks_vector(dve, NC0, NC1)
                turn_vector(dve, 3)
                for q in range(2):
                    for k in range(2):
                        dve.tensor_copy(ci_sb[:, q, k, :].rearrange("p (b n) -> p b n", b=B), cI[q][k])\
                           .then_inc(s["ipa_ctx"], 1)
                ipa_vector(dve)
                dve.wait_ge(s["const_set"], 1)
                attention_vector(dve, layers[1])
            if PHASES >= 4:
                dve.wait_ge(s["g_free1"], G_ALL[1])
                norm_vector(dve, 4, X, Y)
                turn_vector(dve, 4)
                router_vector(dve, 1)
                dve.memset(Z[:, :, :], 0.0).then_inc(s["f_dve_1"], 1)
                dve.wait_ge(s["rt_wd_1"], 2)
                experts_vector(dve, 1, E + 1, (s["f_dve_1"], 1))
                dve.wait_ge(s["acc_done_1"], 8 * (E + 1))
                dve.scalar_tensor_tensor(X[:, :, :].rearrange("p b c -> p (b c)"),
                                         Z[:, :, :].rearrange("p b c -> p (b c)"), tg[:, 3:4],
                                         X[:, :, :].rearrange("p b c -> p (b c)"), ALU.mult, ALU.add)\
                   .then_inc(s["ffn"], 1)

        @block.tensor
        def _(pe):
            pe.wait_ge(s["ident_set"], 2)
            pe.wait_ge(s["ln_norm"], B)
            turn_tensor(pe, 0, Y)
            pe.wait_ge(s["ln_tlo"], 4)
            pe.wait_ge(s["chunk_lo"], NC0)
            pe.wait_ge(s["ones_set"], 4)
            attention_tensor(pe, layers[0])
            if PHASES >= 2:
                pe.wait_ge(s["ffn"], 2)
                turn_tensor(pe, 1, Z)
                router_tensor(pe, 0, 8)
                if PHASES >= 3 or True:
                    pe.wait_ge(s["chunk_lo"], NC0)
                abel_tensor(pe)
                experts_tensor(pe, 0, E)
                pe.wait_ge(s["acc_done_0"], 8 * E)
                turn_tensor(pe, 2, Z)
                expm_tensor(pe)
                mix_tensor(pe, 12)
            if PHASES >= 3:
                chunks_tensor(pe, NC0, NC1)
                pe.wait_ge(s["chunk_added"], lora_before[NC1])
                pe.wait_ge(s["ln_norm"], 4 * B)
                turn_tensor(pe, 3, Y)
                pe.wait_ge(s["chunk_lo"], NC1)
                pe.wait_ge(s["ipa_ctx"], 4)
                ipa_tensor(pe)
                pe.wait_ge(s["ln_tlo"], 16)
                pe.wait_ge(s["ipa_lo"], 10)
                pe.wait_ge(s["const_set"], 1)
                attention_tensor(pe, layers[1])
            if PHASES >= 4:
                pe.wait_ge(s["ln_norm"], 5 * B)
                turn_tensor(pe, 4, Y)
                router_tensor(pe, 1, 20)
                experts_tensor(pe, 1, E + 1)


def _layout(inputs, np):
    i = {k: np.asarray(v) for k, v in inputs.items()}
    f = np.float32

    def tiles(w, rows):
        n = w.shape[0] // rows
        return w.reshape(n, rows, -1).transpose(1, 0, 2).reshape(rows, -1)

    def biased(w, b):
        t = w.reshape(2, KC, -1)
        last = np.stack([np.zeros_like(b), b])[:, None, :]
        return np.concatenate([t, last], 1).transpose(1, 0, 2).reshape(KC + 1, -1)

    out = {
        "x": i["x"],
        "ctxT": i["ctx_768"].reshape(B * KV, CKV).T,
        "pa0": np.concatenate([tiles(w, 128) for w in (i["L0_xattn_Wq"], i["L0_xattn_Wo"], i["L0_ffn_abel_w"],
                                                       i["L0_ffn_moe_gate_w"], i["L1_ffn_Wr"].T)], 1),
        "kv0": np.concatenate([biased(i["L0_xattn_Wk"], i["L0_xattn_bk"]),
                               biased(i["L0_xattn_Wv"], i["L0_xattn_bv"])], 1),
        "rows": np.concatenate([i["L0_xattn_bq"], i["L0_xattn_bo"], i["L0_ffn_abel_b"], i["L0_ffn_moe_gate_b"],
                                i["L1_xattn_bo"], i["L1_ffn_rb"]])[None, :],
        "gates": np.stack([i["g_xattn"][0], i["g_ffn"][0], i["g_xattn"][1], i["g_ffn"][1]]),
        "alphas": np.concatenate([i["L1_xattn_q_alpha"], i["L1_xattn_k_alpha"], i["L1_xattn_v_alpha"],
                                  i["L1_xattn_o_alpha"]]),
        "vecs": np.stack([i["L0_ffn_ln_gamma"], i["L0_ffn_ln_beta"], i["L0_ffn_gc_w"][0:C, 0],
                          i["L0_ffn_gc_w"][C:, 0]]),
        "eb1": i["L0_ffn_eb1"].reshape(E, NM, 128).transpose(2, 0, 1),
        "gc_b": i["L0_ffn_gc_b"],
        "eb2": i["L0_ffn_eb2"],
        "moe0": np.stack([np.concatenate([tiles(i["L0_ffn_ew1"][e], 128), tiles(i["L0_ffn_ew2"][e], 128)], 1)
                          for e in range(E)]),
        "moe1": np.stack([np.concatenate([tiles(w.T, 128) for w in (g, u, d)], 1) for g, u, d in
                          [(i["L1_ffn_Wg_s"], i["L1_ffn_Wu_s"], i["L1_ffn_Wd_s"])] +
                          [(i["L1_ffn_Wg"][e], i["L1_ffn_Wu"][e], i["L1_ffn_Wd"][e]) for e in range(E)]]),
        "gens": np.stack([np.concatenate([tiles(m, 128) for m in ms], 1) for ms in
                          (i["L0_ffn_gens"].transpose(0, 2, 1), i["L0_ffn_gens"])]),
        "lora": np.concatenate([i["L1_xattn_q_down"].T, i["L1_xattn_q_up"], i["L1_xattn_k_down"].T,
                                i["L1_xattn_k_up"], i["L1_xattn_v_down"].T, i["L1_xattn_v_up"],
                                i["L1_xattn_o_down"].T, i["L1_xattn_o_up"]], 1),
        "w1q": tiles(i["L1_xattn_Wq"], 128),
        "w1k": tiles(i["L1_xattn_Wk"], KC),
        "w1v": tiles(i["L1_xattn_Wv"], KC),
        "w1o": tiles(i["L1_xattn_Wo"], 128),
        "w1ki": tiles(i["L1_xattn_Wk_ipa"], KC),
        "w1vi": tiles(i["L1_xattn_Wv_ipa"], KC),
    }
    return {k: np.ascontiguousarray(v) for k, v in out.items()}


PHASES = 4


def kernel(**inputs):
    import numpy as _np
    import concourse.bacc as _bacc
    from concourse.bass_utils import run_bass_kernel_spmd as _run

    arrays = _layout(inputs, _np)
    nc = _bacc.Bacc("TRN2", target_bir_lowering=False, num_devices=1)
    args = {n: nc.dram_tensor(f"in_{n}", v.shape, F32, kind="ExternalInput").ap() for n, v in arrays.items()}
    args["phases"] = PHASES
    res = nc.dram_tensor("out_0", (B, S, C), F32, kind="ExternalOutput").ap()
    build(nc, args, res)
    r = _run(nc, [{f"in_{n}": v for n, v in arrays.items()}], core_ids=[0])
    return r.results[0]["out_0"]
```

```python
from contextlib import ExitStack

import concourse.bass as bass
from concourse import mybir

F32 = mybir.dt.float32
F16 = mybir.dt.float16
U32 = mybir.dt.uint32
ALU = mybir.AluOpType
ACT = mybir.ActivationFunctionType
AX = mybir.AxisListType

B, S, C = 8, 112, 256
KV, CKV = 375, 192
H = 16
KC = CKV // 2
CHUNK = 125
NCH = KV // CHUNK
T = B * S
HT = T // 2
E = 8
FF = 512
NM = FF // 128
WS = 64.0
CLAMP = 10000.0
EPS = 1e-5
IPA = 4
ORG = KV - IPA
RANK = 32
HS = 16.0
OS = 16.0
SQ, DEG = 2, 8
PARTS = ((0, 0), (0, 1), (1, 0))

ROW = {}
_at = 0
for _n, _l in (("bq", C), ("bo0", C), ("abel_b", C), ("gate_b", E), ("bo1", C), ("rb", E)):
    ROW[_n] = (_at, _l)
    _at += _l
ROWS = _at

PA0 = {"Wq": (0, C), "Wo": (2 * C, C), "abel": (4 * C, C), "gate": (6 * C, E), "router1": (6 * C + 2 * E, E)}
PA0_N = 6 * C + 4 * E
STAGE_N = 3072
HB = 4
DOWN_N, UP_N = C + 2 * CKV + 1024, 3 * 1024 + C
STAGES, CHUNK_N = 3, 2048

LN_SMALL = 7


class Layer:

    def __init__(self, index, dim):
        self.index, self.dim = index, dim
        self.width = H * dim
        self.tiles = self.width // 128
        self.qt = min(4, self.tiles)
        self.per_tile = 128 // dim
        self.vw = min(512, self.width)
        self.keys = KV if index == 0 else ORG
        nq = self.tiles // self.qt
        self.q_units = [("q", g) for g in range(nq)]
        self.k_units = [("k", t) for t in range(self.tiles)]
        self.v_units = [("v", c, w) for c in range(NCH) for w in range(self.width // self.vw)]
        self.i_units = [("i",)] if index else []
        self.front = self.q_units + self.k_units + self.i_units + self.v_units
        self.out = [("t", g) for g in range(nq)] + [("o",)]
        if index == 0:
            at = {0: 0, 1: 4, 2: 6, 3: 8, 4: 10, 5: 12}
            out_at = {0: 3, 1: 5}
        else:
            at = {n: min(15, n) for n in range(len(self.front))}
            out_at = {0: 4, 1: 5, 2: 8}
        self.steps = [[] for _ in range(H)]
        for n, u in enumerate(self.front):
            self.steps[at[n]].append(("front", u))
        for n, u in enumerate(self.out):
            self.steps[out_at[n]].append(("out", u))

    def units(self, kinds):
        n, found = 0, []
        for h in range(H):
            for kind, u in self.steps[h]:
                if kind in kinds:
                    found.append((h, kind, u, n))
                    n += 1
        return found


def acts(u):
    return u[0] not in ("i", "o")


def build(nc, a, out):
    ctx = ExitStack()
    with ctx:
        def sb(name, shape, dt=F32):
            return ctx.enter_context(nc.sbuf_tensor(name, shape, dt))

        def sem(name):
            return ctx.enter_context(nc.semaphore(name))

        X = sb("X", [S, B, C])
        Y = sb("Y", [S, B, C])
        ZA = sb("Z", [128, B, C])
        Z = ZA[0:S]
        xT = sb("xT", [128, 2, 2, T], F16)
        cT = sb("cT", [KC + 1, 2, 2, B * KV], F16)
        ST = sb("ST", [128, 2, STAGE_N])
        W0 = sb("W0", [128, 2, PA0_N], F16)
        WKV0 = sb("WKV0", [KC + 1, 2, 4 * C], F16)
        RW = sb("RW", [1, 2, ROWS], F16)
        W1 = sb("W1", [128, 2, 8 * 1024], F16)
        qz = sb("qz", [128, 2, 2, H, S], F16)
        KT = sb("KT", [128, 12288], F16)
        V = sb("V", [128, 2, 2, NCH, 1024], F16)
        WI1 = KT[0:KC, 0:8192].rearrange("p (q n) -> p q n", q=2)
        flat = ST[:, :, :].rearrange("p a n -> p (a n)")
        P_ = flat[0:S, 0:2 * KV].rearrange("p (a n) -> p a n", a=2)
        SC = flat[0:S, 768:768 + 2 * KV].rearrange("p (a n) -> p a n", a=2)
        OB = flat[0:S, 1536:1536 + 1024]
        PT = flat[0:CHUNK, 2560:2560 + 2 * NCH * S].bitcast(F16)\
            .rearrange("p (a q c n) -> p a q c n", a=2, q=2, c=NCH)
        OT = flat[:, 3328:3328 + 8 * S].bitcast(F16).rearrange("p (q t n) -> p q t n", q=2, t=8)
        qu = flat[:, 4352:4352 + 4 * S].bitcast(F16).rearrange("p (a q t n) -> p a q t n", a=2, q=2, t=2)
        mask = sb("mask", [128, 8], F16)
        qflat = qz[:, :, :, :, :].rearrange("p a q h n -> p (a q h n)")
        hf = qflat[:, 0:8 * HT].bitcast(F32).rearrange("p (a n) -> p a n", a=HB)
        sg = qflat[:, 8 * HT:16 * HT].bitcast(F32).rearrange("p (a n) -> p a n", a=HB)
        identf = sb("identf", [128, 128])
        ones16 = sb("ones16", [1, 512], F16)
        os16 = sb("os16", [1, S], F16)
        zero16 = sb("zero16", [1, 128], F16)
        iota8 = sb("iota8", [S, E])
        nm = sb("nm", [S, 4])
        sums = sb("sums", [S, 2, H])
        rinv = sb("rinv", [S, H])
        tg = sb("tg", [S, 4])
        tgs = sb("tgs", [S, 4])
        lora_s = sb("lora_s", [128, 4])
        gc_b = sb("gc_b", [S, 1])
        stats = sb("stats", [S, B, 6])
        mv = sb("mv", [S, B, 2])
        lnc = sb("lnc", [S, LN_SMALL, B])
        lg = sb("lg", [S, B, E])
        m8 = sb("m8", [S, B, 8])
        i8 = sb("i8", [S, B, 8], U32)
        i8f = sb("i8f", [S, B, 8])
        oh = sb("oh", [S, 2, B, E])
        w12 = sb("w12", [S, 4, B])
        wd = sb("wd", [S, B, E])
        wdf = sb("wdf", [E, 2, HT])
        wdT = sb("wdT", [E, 2, T], F16)
        gam = sb("gam", [S, 4, C])
        b1 = sb("b1", [128, E, NM])
        bcur = sb("bcur", [128, 2, NM])
        KI = sb("KI", [128, 2, 8, B * IPA], F16)
        zi = sb("zi", [S, 3, H, IPA])
        pn = sb("pn", [S, 2, H, IPA])
        si = sb("si", [S, 3, H])
        eb2 = sb("eb2", [E, 2, C], F16)
        zz = sb("zz", [S, 3, B])

        pb = [ctx.enter_context(nc.psum_tensor(f"pb{i}", [128, 512], F32)) for i in range(8)]
        SB_, TB_, OBK, GB = pb[0:2], pb[2:4], pb[4:6], pb[6:8]

        wdB = ZA[:, :, :].rearrange("p b c -> p (b c)")[:, 0:2 * T].rearrange("p (a n) -> p a n", a=2)
        wd_dram = [nc.dram_tensor(f"wd_scratch{l}", [E, 2, HT], F32).ap() for l in range(2)]
        vi_dram = nc.dram_tensor("vi_scratch", [B * IPA, 2, 1024], F16).ap()

        kT = [[KT[:, (2 * p + q) * 3000:(2 * p + q + 1) * 3000].rearrange("p (t k) -> p t k", t=8)
               for q in range(2)] for p in range(2)]
        MW = KT[:, :].rearrange("p (u q n) -> p u q n", u=2, q=2)
        VF = V[:, :, :, :, :].rearrange("p a b c d -> p (a b c d)")
        HTt = VF[:, 0:2 * 2 * NM * HT].rearrange("p (u q m n) -> p u q m n", u=2, q=2, m=NM)

        AB = VF[0:S, 7168:7168 + 2 * B * C].bitcast(F32).rearrange("p (b c) -> p b c", b=B)
        junk = VF[0:S, 0:2 * B * C].bitcast(F32).rearrange("p (b c) -> p b c", b=B)
        KF = KT[:, :].rearrange("p (u n) -> p u n", u=4)
        BT = KF[:, 0, :].rearrange("p (q g k n) -> p q g k n", q=2, g=3, k=2)
        R16 = KF[:, 1, :].rearrange("p (q g k n) -> p q g k n", q=2, g=3, k=2)
        RT = KF[:, 2, :].rearrange("p (q g k n) -> p q g k n", q=2, g=3, k=2)
        RF = KF[:, 3, :].bitcast(F32).rearrange("p (g k n) -> p g k n", g=3, k=2)
        eye = sg[:, :, :].rearrange("p a b -> p (a b)")[:, 0:512]

        def w0(name, q, k):
            o, n = PA0[name]
            return W0[:, q, o + k * n:o + (k + 1) * n]

        def row(name, q):
            o, n = ROW[name]
            return RW[0:1, q, o:o + n]

        def bc(ap, shape):
            return ap.broadcast_to(shape)

        names = """x_in small_in ident_set const_set ones_set
            tanh_done lora_scale
            chunk_lora_mm chunk_added chunk_hi chunk_lo
            ln_stats ln_aggr ln_small ln_sqrt ln_norm ln_tmm ln_thi ln_tlo
            ipa_mm ipa_hi ipa_lo ipa_stored ipa_ctx ffn mix halves""".split()
        s = {n: sem(n) for n in names}
        s["chunk_in"] = [sem(f"chunk_in{i}") for i in range(STAGES)]
        for L in range(2):
            for n in """s_mm clip_done mx_done exp_done t_mm hi_done lo_done pv_mm g_mm g_hi g_free
                    qz_done o_rd r_done x_up ipa_patch ipa_z ipa_m ipa_e ipa_s ipa_r ipa_pn vi_in""".split():
                s[f"{n}{L}"] = sem(f"{n}{L}")
            for n in """m_in0 m_in1 m_hi m_lo u_mm u_act u_wt u_hf u_hi u_lo d_mm wd_mm wd_act wd_lo wd_out
                    w_in0 w_in1 moved rt_mm rt_lg rt_m8 rt_i8 rt_sm rt_wd rt_act f_mm f_act f_dve""".split():
                s[f"{n}_{L}"] = sem(f"{n}_{L}")
        for n in "e_mm e_hi e_lo e_f e_in".split():
            s[n] = sem(n)

        layers = [Layer(0, 16), Layer(1, 64)]

        LD = VF[0:3 * RANK, 0:DOWN_N + UP_N]
        LO, at = {}, 0
        for factor, length in (("qd", C), ("kd", CKV), ("vd", CKV), ("od", 1024),
                               ("qu", 1024), ("ku", 1024), ("vu", 1024), ("ou", C)):
            LO[factor] = at
            at += length

        def lo_(name, c0, n):
            return LD[:, LO[name] + c0:LO[name] + c0 + n]

        chunks0 = [
            (128, PA0_N, a["pa0"], W0[:, 0, :], W0[:, 1, :], []),
            (KC + 1, 4 * C, a["kv0"], WKV0[:, 0, :], WKV0[:, 1, :], []),
            (1, ROWS, a["rows"], RW[:, 0, :], RW[:, 1, :], []),
            (E, C, a["eb2"], eb2[:, 0, :], eb2[:, 1, :], []),
        ]
        for k in range(2):
            for g in range(2):
                c0, c1 = g * 4 * KV, (g + 1) * 4 * KV
                chunks0.append((KC, 4 * KV, a["ctxT"][k * KC:(k + 1) * KC, c0:c1],
                                cT[0:KC, 0, k, c0:c1], cT[0:KC, 1, k, c0:c1], []))
        half = UP_N // 2
        lora_cols = [(0, DOWN_N), (DOWN_N, half), (DOWN_N + half, half)]
        LORA_CHUNKS = len(lora_cols)
        lo_rows = {len(chunks0) + j: slice(2 * RANK, 3 * RANK) if j == 0 else slice(RANK, 2 * RANK)
                   for j in range(LORA_CHUNKS)}
        chunks1 = [(3 * RANK, w, a["lora"][:, c0:c0 + w], LD[:, c0:c0 + w],
                    LD[lo_rows[len(chunks0) + j], c0:c0 + w], []) for j, (c0, w) in enumerate(lora_cols)]
        specs = [("q", 0, 128, C, 1024, "qd", "qu"), ("k", 1, KC, CKV, 1024, "kd", "ku"),
                 ("v", 2, KC, CKV, 1024, "vd", "vu"), ("o", 3, 128, 1024, C, "od", "ou")]
        for name, j, rows, kk, cols, dn, up in specs:
            lora = []
            for kt in range(kk // rows):
                for c0 in range(0, cols, 512):
                    w = min(512, cols)
                    lora.append((kt * cols + c0, w, rows,
                                 lo_(dn, kt * rows, rows), lo_(up, c0, w), j))
            chunks1.append((rows, 2048, a["w1" + name], W1[0:rows, 0, j * 2048:(j + 1) * 2048],
                            W1[0:rows, 1, j * 2048:(j + 1) * 2048], lora))
        for j, name in enumerate(("ki", "vi")):
            chunks1.append((KC, 2048, a["w1" + name], WI1[:, 0, j * 2048:(j + 1) * 2048],
                            WI1[:, 1, j * 2048:(j + 1) * 2048], []))
        chunks = chunks0 + chunks1
        lora_before = [sum(len(c[5]) for c in chunks[:n]) for n in range(len(chunks) + 1)]

        def staged(n, c0, w):
            o = (n % STAGES) * CHUNK_N + c0
            return flat[0:chunks[n][0], o:o + w]

        def chunks_sync(sp, first, last):
            for n in range(first, last):
                if n >= STAGES:
                    sp.wait_ge(s["chunk_lo"], n - STAGES + 1)
                sp.dma_start(staged(n, 0, chunks[n][1]), chunks[n][2]).then_inc(s["chunk_in"][n % STAGES], 16)

        def chunk_arrived(eng, n):
            eng.wait_ge(s["chunk_in"][n % STAGES], 16 * (n // STAGES + 1))

        def chunks_tensor(pe, first, last):
            for n in range(first, last):
                for j, (c0, w, rows, dn, up, _) in enumerate(chunks[n][5]):
                    k = lora_before[n] + j
                    if j == 0 and k == 0:
                        pe.wait_ge(s["chunk_lo"], len(chunks0) + LORA_CHUNKS)
                    if k >= 2:
                        pe.wait_ge(s["chunk_added"], k - 1)
                    pe.matmul(GB[k % 2][0:rows, 0:w], dn, up, start=True, stop=True)\
                      .then_inc(s["chunk_lora_mm"], 1)

        def chunks_vector(dve, first, last):
            def adds(n):
                rows, lora = chunks[n][0], chunks[n][5]
                for j, (c0, w, r, dn, up, which) in enumerate(lora):
                    k = lora_before[n] + j
                    if j == 0:
                        chunk_arrived(dve, n)
                    if k == 0:
                        dve.wait_ge(s["lora_scale"], 3)
                    dve.wait_ge(s["chunk_lora_mm"], k + 1)
                    dve.scalar_tensor_tensor(staged(n, c0, w), GB[k % 2][0:rows, 0:w], lora_s[0:rows, which:which + 1],
                                             staged(n, c0, w), ALU.mult, ALU.add).then_inc(s["chunk_added"], 1)

            def cut(n):
                rows, cols, src, hi, lo, lora = chunks[n]
                dve.wait_ge(s["chunk_hi"], n + 1)
                part = lo_rows.get(n, slice(0, rows))
                dve.scalar_tensor_tensor(lo, staged(n, 0, cols)[part], WS if n not in plain else 1.0, hi[part],
                                         ALU.mult, ALU.subtract).then_inc(s["chunk_lo"], 1)

            for n in range(first, last):
                if n == first or (chunks[n][5] and not chunks[n - 1][5]):
                    adds(n)
                if n + 1 < last and chunks[n][5]:
                    adds(n + 1)
                cut(n)

        def chunks_scalar(act, first, last):
            for n in range(first, last):
                rows, cols, src, hi, lo, lora = chunks[n]
                chunk_arrived(act, n)
                if lora:
                    act.wait_ge(s["chunk_added"], lora_before[n + 1])
                act.activation(hi, staged(n, 0, cols), ACT.Copy,
                               scale=WS if n not in plain else 1.0).then_inc(s["chunk_hi"], 1)

        plain = set(range(4, 8))
        NC0, NC1 = len(chunks0), len(chunks)

        def norm_vector(dve, r, src, dst):
            st_, ag_, sm_, nn_ = s["ln_stats"], s["ln_aggr"], s["ln_small"], s["ln_norm"]
            if r:
                dve.wait_ge(nn_, B * r)
            for b in range(B):
                dve.bn_stats(stats[:, b, :], src[:, b, :]).then_inc(st_, 1)
            dve.wait_ge(st_, B * (r + 1))
            for b in range(B):
                dve.bn_aggr(mv[:, b, :], stats[:, b, :]).then_inc(ag_, 1)
            dve.wait_ge(ag_, B * (r + 1))
            k = 6 * r
            dve.tensor_scalar(lnc[:, 0, :], mv[:, :, 1], EPS, None, ALU.add).then_inc(sm_, 1)
            dve.wait_ge(s["ln_sqrt"], r + 1)
            dve.reciprocal(lnc[:, 2, :], lnc[:, 1, :]).then_inc(sm_, 1)
            dve.wait_ge(sm_, k + 2)
            dve.tensor_tensor(lnc[:, 3, :], lnc[:, 2, :], lnc[:, 2, :], ALU.mult).then_inc(sm_, 1)
            dve.wait_ge(sm_, k + 3)
            dve.tensor_tensor(lnc[:, 4, :], lnc[:, 3, :], lnc[:, 0, :], ALU.mult).then_inc(sm_, 1)
            dve.wait_ge(sm_, k + 4)
            dve.tensor_scalar(lnc[:, 5, :], lnc[:, 4, :], -0.5, 1.5, ALU.mult, ALU.add).then_inc(sm_, 1)
            dve.wait_ge(sm_, k + 5)
            dve.tensor_tensor(lnc[:, 6, :], lnc[:, 5, :], lnc[:, 2, :], ALU.mult).then_inc(sm_, 1)
            dve.wait_ge(sm_, k + 6)
            for b in range(B):
                dve.tensor_scalar(dst[:, b, :], src[:, b, :], mv[:, b, 0:1], lnc[:, 6, b:b + 1],
                                  ALU.subtract, ALU.mult).then_inc(nn_, 1)

        def norm_scalar(act, r):
            act.wait_ge(s["ln_small"], 6 * r + 1)
            act.activation(lnc[:, 1, :], lnc[:, 0, :], ACT.Sqrt).then_inc(s["ln_sqrt"], 1)

        GROUPS = [(k, g) for g in range(2) for k in range(2)]

        def turn_tensor(pe, r, src):
            for n, (k, g) in enumerate(GROUPS):
                i = 4 * r + n
                if i >= 2:
                    pe.wait_ge(s["ln_tlo"], i - 1)
                for j in range(4):
                    mm = pe.transpose(GB[i % 2][:, j * S:(j + 1) * S], src[:, 4 * g + j, k * 128:(k + 1) * 128],
                                      identf[0:S, 0:S])
                mm.then_inc(s["ln_tmm"], 1)

        def turn_scalar(act, r):
            for n, (k, g) in enumerate(GROUPS):
                i = 4 * r + n
                act.wait_ge(s["ln_tmm"], i + 1 - (4 if r > 2 else 0))
                act.activation(xT[:, 0, k, g * HT:(g + 1) * HT], GB[i % 2][:, 0:HT], ACT.Copy)\
                   .then_inc(s["ln_thi"], 1)

        def turn_vector(dve, r):
            for n, (k, g) in enumerate(GROUPS):
                i = 4 * r + n
                dve.wait_ge(s["ln_thi"], i + 1)
                dve.scalar_tensor_tensor(xT[:, 1, k, g * HT:(g + 1) * HT], GB[i % 2][:, 0:HT], 1.0,
                                         xT[:, 0, k, g * HT:(g + 1) * HT], ALU.mult, ALU.subtract)\
                   .then_inc(s["ln_tlo"], 1)

        def psum_out(L, h):
            if L.index == 0:
                return OBK[0][0:S, 2 * h * L.dim:2 * (h + 1) * L.dim].rearrange("p (q d) -> p q d", q=2)
            per = 512 // L.dim
            return OBK[h // per][0:S, (h % per) * L.dim:(h % per + 1) * L.dim]

        def counts(L):
            F, U = len(L.front), len(L.front) + len(L.out)
            hiF = sum(acts(u) for u in L.front)
            hiU = hiF + sum(acts(u) for u in L.out)
            return F, U, hiF, hiU

        def unit_numbers(L, where, bv, bs):
            F, U, hiF, hiU = counts(L)
            if where == "first":
                kinds, n0, s0, h0 = ("front",), F, F, hiF
            elif where == "last":
                kinds, n0, h0 = ("out",), 2 * F + (bv - 1) * U, 2 * hiF + (bv - 1) * hiU
                s0 = 2 * F + (bs - 1) * U
            else:
                kinds, n0, h0 = ("front", "out"), 2 * F + (bv - 1) * U, 2 * hiF + (bv - 1) * hiU
                s0 = 2 * F + (bs - 1) * U
            found, done = [], 0
            for h, kind, u, n in L.units(kinds):
                found.append((h, kind, u, n0 + n, s0 + n, h0 + done))
                done += acts(u)
            return found

        def prologue_units(L):
            found, done = [], 0
            for n, u in enumerate(L.front):
                found.append((0, "front", u, n, n, done))
                done += acts(u)
            return found

        def tail_units(L):
            F, U, hiF, hiU = counts(L)
            n0, h0 = 2 * F + (B - 2) * U + len(L.out), 2 * hiF + (B - 2) * hiU + (hiU - hiF)
            found, done = [], 0
            for n, u in enumerate(L.out):
                found.append((0, "out", u, n0 + n, n0 + n, h0 + done))
                done += acts(u)
            return found

        def front_done(L, bv, bs, which):
            F, U, _, _ = counts(L)
            last = {"q": len(L.q_units), "k": len(L.q_units) + len(L.k_units),
                    "i": len(L.q_units) + len(L.k_units) + len(L.i_units), "v": len(L.front)}[which]
            if isinstance(bs, int) and bs == 0:
                return last
            if bs == 1 and isinstance(bv, int):
                return F + last
            number = {("front", u) if kind == "front" else ("out", u): n
                      for _, kind, u, n in L.units(("front", "out"))}
            u = L.front[last - 1]
            inner = number[("front", u)] + 1
            return 2 * F + (bv - 2) * U + inner

        def attention_tensor(pe, L):
            l = L.index
            g_mm, g_free = s[f"g_mm{l}"], s[f"g_free{l}"]
            dq = C if l == 0 else 1024

            def wq(q, k, t):
                return w0("Wq", q, k)[:, t * 128:(t + 1) * 128] if l == 0 else \
                    W1[:, q, k * 1024 + t * 128:k * 1024 + (t + 1) * 128]

            def wk(q, k, t):
                if l == 0:
                    return WKV0[0:KC + k, q, k * C + t * 128:k * C + (t + 1) * 128]
                return W1[0:KC, q, 2048 + k * 1024 + t * 128:2048 + k * 1024 + (t + 1) * 128]

            def wv(q, k, w):
                if l == 0:
                    return WKV0[0:KC + k, q, 2 * C + k * C:2 * C + (k + 1) * C]
                return W1[0:KC, q, 4096 + k * 1024 + w * 512:4096 + k * 1024 + (w + 1) * 512]

            def wo(q, t):
                return w0("Wo", q, t) if l == 0 else W1[:, q, 6144 + t * C:6144 + (t + 1) * C]

            def unit(kind, u, n, ns, bv, bs, behind=1):
                bank = GB[ns % 2]
                if ns >= 2:
                    pe.wait_ge(g_free, n - 1)
                rows = KC + 1 if l == 0 else KC
                if u[0] == "q":
                    for t in range(L.qt):
                        i = 0
                        for k in range(2):
                            for qa, qb in PARTS:
                                mm = pe.matmul(bank[:, t * S:(t + 1) * S], wq(qa, k, u[1] * 4 + t),
                                               xT[:, qb, k, bass.ds(bv * S, S)], start=(i == 0),
                                               stop=(i == 5 and l == 1))
                                i += 1
                        if l == 0:
                            for q in range(2):
                                mm = pe.matmul(bank[:, t * S:(t + 1) * S], row("bq", q)[:, t * 128:(t + 1) * 128],
                                               ones16[:, 0:S], start=False, stop=(q == 1))
                elif u[0] == "k":
                    i = 0
                    for k in range(2):
                        for qa, qb in PARTS:
                            kr = KC + (k if l == 0 else 0)
                            mm = pe.matmul(bank[:, 0:L.keys], wk(qa, k, u[1]),
                                           cT[0:kr, qb, k, bass.ds(bv * KV, L.keys)], start=(i == 0), stop=(i == 5))
                            i += 1
                elif u[0] == "v":
                    m = min(CHUNK, L.keys - u[1] * CHUNK)
                    i = 0
                    for k in range(2):
                        for qa, qb in PARTS:
                            kr = KC + (k if l == 0 else 0)
                            mm = pe.matmul(bank[0:m, 0:L.vw], cT[0:kr, qa, k, bass.ds(bv * KV + u[1] * CHUNK, m)],
                                           wv(qb, k, u[2]), start=(i == 0), stop=(i == 5))
                            i += 1
                elif u[0] == "i":
                    pe.wait_ge(g_free, front_done(L, bv, bs, "q"))
                    for h in range(H):
                        for i, (qa, qb) in enumerate(PARTS):
                            mm = pe.matmul(bank[0:S, h * IPA:(h + 1) * IPA], qz[:, bs % 2, qa, h, :],
                                           KI[:, qb, h // 2, bass.ds(bv * IPA, IPA)], start=(i == 0), stop=(i == 2))
                elif u[0] == "t":
                    if u[1] == 0:
                        pe.wait_ge(s[f"o_rd{l}"], bv + 1)
                    for j in range(L.qt):
                        c0 = (u[1] * 4 + j) * 128
                        mm = pe.transpose(bank[:, j * S:(j + 1) * S], OB[:, c0:c0 + 128], identf[0:S, 0:S])
                else:
                    pe.wait_ge(g_free, n - behind + 1)
                    i, last = 0, 3 * L.tiles - 1
                    for t in range(L.tiles):
                        for qa, qb in PARTS:
                            pe.matmul(bank[0:S, 0:C], OT[:, qa, t, :], wo(qb, t), start=(i == 0), stop=False)
                            i += 1
                    for q in range(2):
                        mm = pe.matmul(bank[0:S, 0:C], (os16 if l else ones16)[:, 0:S], row(f"bo{l}", q), start=False, stop=(q == 1))
                mm.then_inc(g_mm, 1)

            def scores(bv, bs, h):
                i, st = bv * H + h, bs * H + h
                if h == 0:
                    pe.wait_ge(g_free, front_done(L, bv, bs, "k"))
                    if l == 0:
                        pe.wait_ge(s["qz_done0"], 4 * bv + 4)
                if st >= 2:
                    pe.wait_ge(s["mx_done0"] if l == 0 else s["exp_done1"], i - 1)
                for n, (qa, qb) in enumerate(PARTS):
                    mm = pe.matmul(SB_[st % 2][0:S, 0:L.keys], qz[:, bs % 2, qa, h, :],
                                   kT[bs % 2][qb][:, h // L.per_tile, 0:L.keys], start=(n == 0), stop=(n == 2))
                mm.then_inc(s[f"s_mm{l}"], 1)

            def turn(i, st):
                pe.wait_ge(s["exp_done0"] if l == 0 else s["ipa_patch1"], i + 1)
                if st >= 2:
                    pe.wait_ge(s[f"lo_done{l}"], i - 1)
                for c in range(NCH):
                    mm = pe.transpose(TB_[st % 2][0:CHUNK, c * S:(c + 1) * S],
                                      P_[:, st % 2, c * CHUNK:(c + 1) * CHUNK], identf[0:S, 0:S])
                mm.then_inc(s[f"t_mm{l}"], 1)

            def weigh(bv, bs, h):
                i, st = bv * H + h, bs * H + h
                if h == 0:
                    pe.wait_ge(g_free, front_done(L, bv, bs, "v"))
                    if l == 1:
                        pe.wait_ge(s[f"vi_in{bs % 2}"], (bv - bs % 2) * 16 + 32)
                    if bs >= 1:
                        pe.wait_ge(s[f"o_rd{l}"], bv)
                pe.wait_ge(s[f"lo_done{l}"], i + 1)
                n = 0
                for c in range(NCH):
                    if l == 0:
                        for qa in range(2):
                            mm = pe.matmul(psum_out(L, h), PT[:, st % 2, qa, c, :],
                                           V[0:CHUNK, bs % 2, :, c, h * L.dim:(h + 1) * L.dim],
                                           start=(n == 0), stop=(n == 5))
                            n += 1
                        continue
                    for qa, qb in PARTS:
                        mm = pe.matmul(psum_out(L, h), PT[:, st % 2, qa, c, :],
                                       V[0:CHUNK, bs % 2, qb, c, h * L.dim:(h + 1) * L.dim],
                                       start=(n == 0), stop=(n == 8))
                        n += 1
                mm.then_inc(s[f"pv_mm{l}"], 1)

            def batch(where, bv, bs):
                todo = unit_numbers(L, where, bv, bs)
                at = {u: ns for _, kind, u, n, ns, _ in todo if kind == "out"}
                behind = at[L.out[-1]] - at[L.out[-2]] if at else 1
                for h in range(H):
                    scores(bv, bs, h)
                    if bs or h >= 2:
                        turn(bv * H + h - 2, bs * H + h - 2)
                    if bs or h >= 3:
                        if h >= 3:
                            weigh(bv, bs, h - 3)
                        else:
                            weigh(bv - 1, bs - 1, H + h - 3)
                    for hh, kind, u, n, ns, _ in todo:
                        if hh == h:
                            d = 1 if kind == "front" else -1
                            unit(kind, u, n, ns, bv + d, bs + d, behind)

            for _, kind, u, n, ns, _ in prologue_units(L):
                unit(kind, u, n, ns, 0, 0)
            batch("first", 0, 0)
            with pe.Fori(0, (B - 2) // 2) as r:
                b = r * 2 + 1
                batch("middle", b, 1)
                batch("middle", b + 1, 2)
            batch("last", B - 1, B - 1)
            for i in range(B * H - 2, B * H):
                turn(i, i)
                weigh(B - 1, B - 1, i - 1 - (B - 1) * H)
            weigh(B - 1, B - 1, H - 1)
            for _, kind, u, n, ns, _ in tail_units(L):
                unit(kind, u, n, ns, B - 1, B - 1)

        QSCALE = {0: -0.25 / WS, 1: 0.125 / WS}

        def q_cuts(L, u, bs):
            for side in range(2):
                r = slice(64 * side, 64 * side + 64)
                h0 = 8 * u[1] + side
                yield (r, lambda q, r=r, h0=h0: qz[r, bs % 2, q, h0:h0 + 7:2, :])

        def attention_scalar(act, L):
            l = L.index
            g_mm, g_hi = s[f"g_mm{l}"], s[f"g_hi{l}"]

            def unit(kind, u, n, ns, bv, bs):
                if not acts(u):
                    return
                bank = GB[ns % 2]
                act.wait_ge(g_mm, n + 1)
                if u[0] == "q" and l == 0:
                    act.activation(qu[:, bs % 2, 0, :, :], bank[:, 0:2 * S].rearrange("p (t n) -> p t n", t=2),
                                   ACT.Copy, scale=QSCALE[0]).then_inc(g_hi, 1)
                elif u[0] == "q":
                    for side, (r, dst) in enumerate(q_cuts(L, u, bs)):
                        x = act.activation(dst(0), bank[r, 0:4 * S].rearrange("p (t n) -> p t n", t=4),
                                           ACT.Copy, scale=QSCALE[1])
                        if side:
                            x.then_inc(g_hi, 1)
                elif u[0] == "k":
                    act.activation(kT[bs % 2][0][:, u[1], 0:L.keys], bank[:, 0:L.keys], ACT.Copy,
                                   scale=1.0 / WS).then_inc(g_hi, 1)
                elif u[0] == "v":
                    m = min(CHUNK, L.keys - u[1] * CHUNK)
                    act.activation(V[0:m, bs % 2, 0, u[1], u[2] * 512:u[2] * 512 + L.vw], bank[0:m, 0:L.vw],
                                   ACT.Copy, scale=1.0 / WS).then_inc(g_hi, 1)
                else:
                    g = u[1]
                    act.activation(OT[:, 0, g * L.qt:(g + 1) * L.qt, :],
                                   bank[:, 0:L.qt * S].rearrange("p (t n) -> p t n", t=L.qt), ACT.Copy)\
                       .then_inc(g_hi, 1)

            def exps(bv, bs, h):
                i, st = bv * H + h, bs * H + h
                act.wait_ge(s["mx_done1"] if l else s["clip_done0"], i + 1)
                if st >= 2:
                    act.wait_ge(s[f"t_mm{l}"], i - 1)
                if h == 0 and bs >= 2:
                    act.wait_ge(s[f"o_rd{l}"], bv - 1)
                src = SC[:, st % 2, :] if l == 0 else SB_[st % 2][0:S, 0:L.keys]
                act.activation(P_[:, st % 2, 0:L.keys], src, ACT.Exp, bias=nm[:, st % 4:st % 4 + 1],
                               scale=1.0 if l else -1.0,
                               accum_out=sums[:, bs % 2, h:h + 1]).then_inc(s[f"exp_done{l}"], 1)

            def hi(i, st):
                act.wait_ge(s[f"t_mm{l}"], i + 1)
                if st >= 2:
                    act.wait_ge(s[f"pv_mm{l}"], i - 1)
                act.activation(PT[:, st % 2, 0, :, :], TB_[st % 2][0:CHUNK, 0:NCH * S]
                               .rearrange("p (c n) -> p c n", c=NCH), ACT.Copy).then_inc(s[f"hi_done{l}"], 1)

            def ipa_exp(bv, bs):
                act.wait_ge(s["ipa_z1"], bv + 1)
                act.activation(zi[:, 1, :, :], zi[:, 0, :, :], ACT.Exp).then_inc(s["ipa_e1"], 1)

            def batch(where, bv, bs):
                todo = unit_numbers(L, where, bv, bs)
                for h in range(H):
                    if bs or h >= 2:
                        hi(bv * H + h - 2, bs * H + h - 2)
                    exps(bv, bs, h)
                    for hh, kind, u, n, ns, nh in todo:
                        if hh == h:
                            d = 1 if kind == "front" else -1
                            unit(kind, u, n, ns, bv + d, bs + d)
                            if u[0] == "i":
                                ipa_exp(bv + d, bs + d)

            for _, kind, u, n, ns, nh in prologue_units(L):
                unit(kind, u, n, ns, 0, 0)
                if u[0] == "i":
                    ipa_exp(0, 0)
            batch("first", 0, 0)
            with act.Fori(0, (B - 2) // 2) as r:
                b = r * 2 + 1
                batch("middle", b, 1)
                batch("middle", b + 1, 2)
            batch("last", B - 1, B - 1)
            for i in range(B * H - 2, B * H):
                hi(i, i)
            for _, kind, u, n, ns, nh in tail_units(L):
                unit(kind, u, n, ns, B - 1, B - 1)

        def attention_vector(dve, L):
            l = L.index
            g_mm, g_hi, g_free = s[f"g_mm{l}"], s[f"g_hi{l}"], s[f"g_free{l}"]
            step = ALU.mult, ALU.subtract

            def unit(kind, u, n, ns, nh, bv, bs):
                bank = GB[ns % 2]
                if acts(u):
                    dve.wait_ge(g_hi, nh + 1)
                else:
                    dve.wait_ge(g_mm, n + 1)
                if u[0] == "q" and l == 0:
                    x = dve.scalar_tensor_tensor(qu[:, bs % 2, 1, :, :],
                                                 bank[:, 0:2 * S].rearrange("p (t n) -> p t n", t=2), QSCALE[0],
                                                 qu[:, bs % 2, 0, :, :], *step)
                elif u[0] == "q":
                    for r, dst in q_cuts(L, u, bs):
                        x = dve.scalar_tensor_tensor(dst(1), bank[r, 0:4 * S].rearrange("p (t n) -> p t n", t=4),
                                                     QSCALE[1], dst(0), *step)
                elif u[0] == "k":
                    x = dve.scalar_tensor_tensor(kT[bs % 2][1][:, u[1], 0:L.keys], bank[:, 0:L.keys], 1.0 / WS,
                                                 kT[bs % 2][0][:, u[1], 0:L.keys], *step)
                elif u[0] == "v":
                    m = min(CHUNK, L.keys - u[1] * CHUNK)
                    c = slice(u[2] * 512, u[2] * 512 + L.vw)
                    x = dve.scalar_tensor_tensor(V[0:m, bs % 2, 1, u[1], c], bank[0:m, 0:L.vw], 1.0 / WS,
                                                 V[0:m, bs % 2, 0, u[1], c], *step)
                elif u[0] == "t":
                    t = slice(u[1] * L.qt, (u[1] + 1) * L.qt)
                    x = dve.scalar_tensor_tensor(OT[:, 1, t, :],
                                                 bank[:, 0:L.qt * S].rearrange("p (t n) -> p t n", t=L.qt), 1.0,
                                                 OT[:, 0, t, :], *step)
                elif u[0] == "o":
                    xb = X[:, bass.ds(bv, 1), :]
                    x = dve.scalar_tensor_tensor(xb, bank[0:S, 0:C].rearrange("p (a n) -> p a n", a=1),
                                                 tgs[:, l:l + 1], xb, ALU.mult, ALU.add)
                else:
                    sc = bank[0:S, 0:H * IPA].rearrange("p (h j) -> p h j", h=H)
                    if bs >= 1:
                        dve.wait_ge(s["ipa_pn1"], bv)
                    dve.tensor_reduce(si[:, 0, :], sc, AX.X, ALU.max).then_inc(s["ipa_m1"], 1)
                    dve.wait_ge(s["ipa_m1"], bv + 1)
                    dve.tensor_tensor(zi[:, 0, :, :], sc, bc(si[:, 0, :].unsqueeze(2), [S, H, IPA]),
                                      ALU.subtract).then_inc(s["ipa_z1"], 1)
                    dve.wait_ge(s["ipa_z1"], bv + 1)
                    x = dve.tensor_copy(si[:, 0, 0:1], si[:, 0, 1:2])
                x.then_inc(g_free, 1)

            def ipa_rest(bv, bs):
                dve.wait_ge(s["ipa_e1"], bv + 1)
                dve.tensor_reduce(si[:, 1, :], zi[:, 1, :, :], AX.X, ALU.add).then_inc(s["ipa_s1"], 1)
                dve.wait_ge(s["ipa_s1"], bv + 1)
                dve.reciprocal(si[:, 2, :], si[:, 1, :]).then_inc(s["ipa_r1"], 1)
                dve.wait_ge(s["ipa_r1"], bv + 1)
                if bs >= 2:
                    dve.wait_ge(s["ipa_patch1"], (bv - 1) * H)
                dve.tensor_tensor(pn[:, bs % 2, :, :], zi[:, 1, :, :], bc(si[:, 2, :].unsqueeze(2), [S, H, IPA]),
                                  ALU.mult).then_inc(s["ipa_pn1"], 1)

            def maxima(bv, bs, h):
                i, st = bv * H + h, bs * H + h
                dve.wait_ge(s[f"s_mm{l}"], i + 1)
                src = SB_[st % 2][0:S, 0:L.keys]
                if l == 0:
                    if st >= 2:
                        dve.wait_ge(s["exp_done0"], i - 1)
                    dve.tensor_scalar(SC[:, st % 2, :], src, -CLAMP, CLAMP, ALU.max, ALU.min,
                                      accum_out=nm[:, st % 4:st % 4 + 1]).then_inc(s["mx_done0"], 1)
                    dve.wait_ge(s["mx_done0"], i + 1)
                    dve.tensor_scalar(SC[:, st % 2, :], SC[:, st % 2, :], CLAMP, None, ALU.min)\
                       .then_inc(s["clip_done0"], 1)
                    return
                dve.tensor_reduce(nm[:, st % 4:st % 4 + 1], src, AX.X, ALU.max, negate=True)\
                   .then_inc(s[f"mx_done{l}"], 1)

            def lo(i, st):
                dve.wait_ge(s[f"hi_done{l}"], i + 1)
                dve.scalar_tensor_tensor(PT[:, st % 2, 1, :, :], TB_[st % 2][0:CHUNK, 0:NCH * S]
                                         .rearrange("p (c n) -> p c n", c=NCH), 1.0, PT[:, st % 2, 0, :, :],
                                         *step).then_inc(s[f"lo_done{l}"], 1)

            def normalise(bv, bs):
                dve.wait_ge(s[f"pv_mm{l}"], bv * H + H)
                if bs >= 1:
                    dve.wait_ge(s[f"o_rd{l}"], bv)
                dve.reciprocal(rinv[:, :], sums[:, bs % 2, :]).then_inc(s[f"r_done{l}"], 1)
                dve.wait_ge(s[f"r_done{l}"], bv + 1)
                if l == 0:
                    halves = OBK[0][0:S, :].rearrange("p (h q d) -> p h q d", h=H, q=2)
                    ob = OB[:, 0:C].rearrange("p (h d) -> p h d", h=H)
                    dve.tensor_copy(ob, halves[:, :, 0, :]).then_inc(s["halves"], 1)
                    dve.wait_ge(s["halves"], 2 * bv + 1)
                    dve.tensor_tensor(ob, ob, halves[:, :, 1, :], ALU.add).then_inc(s["halves"], 1)
                    dve.wait_ge(s["halves"], 2 * bv + 2)
                    dve.tensor_tensor(ob, ob, bc(rinv[:, :].unsqueeze(2), [S, H, L.dim]), ALU.mult)\
                       .then_inc(s["o_rd0"], 1)
                    return
                per = min(H, 512 // L.dim)
                for n in range(H // per):
                    w = per * L.dim
                    x = dve.scalar_tensor_tensor(
                        OB[:, n * w:(n + 1) * w].rearrange("p (h d) -> p h d", h=per),
                        OBK[n][0:S, 0:w].rearrange("p (h d) -> p h d", h=per), OS if l else 1.0,
                        bc(rinv[:, n * per:(n + 1) * per].unsqueeze(2), [S, per, L.dim]), ALU.mult, ALU.mult)
                x.then_inc(s[f"o_rd{l}"], 1)

            def batch(where, bv, bs):
                todo = unit_numbers(L, where, bv, bs)
                for h in range(H):
                    maxima(bv, bs, h)
                    if bs or h >= 2:
                        lo(bv * H + h - 2, bs * H + h - 2)
                    if bs and h == 2:
                        normalise(bv - 1, bs - 1)
                    for hh, kind, u, n, ns, nh in todo:
                        if hh == h:
                            d = 1 if kind == "front" else -1
                            unit(kind, u, n, ns, nh, bv + d, bs + d)
                            if u[0] == "i":
                                ipa_rest(bv + d, bs + d)

            for _, kind, u, n, ns, nh in prologue_units(L):
                unit(kind, u, n, ns, nh, 0, 0)
                if u[0] == "i":
                    ipa_rest(0, 0)
            batch("first", 0, 0)
            with dve.Fori(0, (B - 2) // 2) as r:
                b = r * 2 + 1
                batch("middle", b, 1)
                batch("middle", b + 1, 2)
            batch("last", B - 1, B - 1)
            for i in range(B * H - 2, B * H):
                lo(i, i)
            normalise(B - 1, B - 1)
            for _, kind, u, n, ns, nh in tail_units(L):
                unit(kind, u, n, ns, nh, B - 1, B - 1)

        def attention_gpsimd(pool, L):
            l = L.index
            if l == 0:
                def masks(bv, bs):
                    pool.wait_ge(s["g_free0"], front_done(L, bv, bs, "q"))
                    for q in range(2):
                        for t in range(2):
                            pool.tensor_tensor(qz[:, bs % 2, q, 8 * t:8 * t + 8, :],
                                               bc(qu[:, bs % 2, q, t, :].unsqueeze(1), [128, 8, S]),
                                               bc(mask[:, :].unsqueeze(2), [128, 8, S]), ALU.mult)\
                                .then_inc(s["qz_done0"], 1)
                masks(0, 0)
                masks(1, 1)
                with pool.Fori(1, B // 2) as r:
                    b = r * 2
                    masks(b, 2)
                    masks(b + 1, 3)
                return

            def patches(bv, bs):
                pool.wait_ge(s["ipa_pn1"], bv + 1)
                for h in range(H):
                    i, st = bv * H + h, bs * H + h
                    pool.wait_ge(s["exp_done1"], i + 1)
                    pool.tensor_tensor(P_[:, st % 2, ORG:KV], pn[:, bs % 2, h, :],
                                       bc(sums[:, bs % 2, h:h + 1], [S, IPA]), ALU.mult)\
                        .then_inc(s["ipa_patch1"], 1)
            patches(0, 0)
            with pool.Fori(0, (B - 2) // 2) as r:
                b = r * 2 + 1
                patches(b, 1)
                patches(b + 1, 2)
            patches(B - 1, B - 1)

        def attention_sync(sp, L):
            for b in range(B):
                if b >= 2:
                    sp.wait_ge(s["pv_mm1"], (b - 1) * H)
                for q in range(2):
                    sp.dma_start(V[CHUNK - IPA:CHUNK, b % 2, q, NCH - 1, :],
                                 vi_dram[b * IPA:(b + 1) * IPA, q, :]).then_inc(s[f"vi_in{b % 2}"], 16)

        cI = [[cT[0:KC, q, k, :].rearrange("p (b n) -> p b n", b=B)[:, :, ORG:KV] for k in range(2)] for q in range(2)]
        vi_sb = flat[0:B * IPA, 4352:4864].bitcast(F16)
        vi_sb2 = flat[0:B * IPA, 4864:5376].bitcast(F16)
        ci_sb = KT[0:KC, 8192:8192 + 4 * B * IPA].rearrange("p (q k n) -> p q k n", q=2, k=2)

        def ipa_tensor(pe):
            for t in range(8):
                i = 0
                for k in range(2):
                    for qa, qb in PARTS:
                        mm = pe.matmul(GB[0][:, t * B * IPA:(t + 1) * B * IPA],
                                       WI1[:, qa, k * 1024 + t * 128:k * 1024 + (t + 1) * 128],
                                       ci_sb[:, qb, k, :], start=(i == 0), stop=(i == 5))
                        i += 1
            mm.then_inc(s["ipa_mm"], 1)
            for w in range(2):
                if w:
                    pe.wait_ge(s["ipa_lo"], 1)
                i = 0
                for k in range(2):
                    for qa, qb in PARTS:
                        mm = pe.matmul(GB[1 - w][0:B * IPA, :], ci_sb[:, qa, k, :],
                                       WI1[:, qb, 2048 + k * 1024 + w * 512:2048 + k * 1024 + (w + 1) * 512],
                                       start=(i == 0), stop=(i == 5))
                        i += 1
                mm.then_inc(s["ipa_mm"], 1)

        def ipa_scalar(act):
            act.wait_ge(s["ipa_mm"], 1)
            act.activation(KI[:, 0, :, :].rearrange("p t n -> p (t n)"), GB[0][:, 0:8 * B * IPA], ACT.Copy,
                           scale=1.0 / WS).then_inc(s["ipa_hi"], 1)
            for w in range(2):
                act.wait_ge(s["ipa_mm"], 2 + w)
                act.activation(vi_sb[:, w * 512:(w + 1) * 512], GB[1 - w][0:B * IPA, :], ACT.Copy, scale=1.0 / WS)\
                   .then_inc(s["ipa_hi"], 1)

        def ipa_vector(dve):
            dve.wait_ge(s["ipa_hi"], 1)
            dve.scalar_tensor_tensor(KI[:, 1, :, :].rearrange("p t n -> p (t n)"), GB[0][:, 0:8 * B * IPA], 1.0 / WS,
                                     KI[:, 0, :, :].rearrange("p t n -> p (t n)"),
                                     ALU.mult, ALU.subtract).then_inc(s["ipa_lo"], 1)
            for w in range(2):
                dve.wait_ge(s["ipa_hi"], 2 + w)
                dve.scalar_tensor_tensor(vi_sb2[:, w * 512:(w + 1) * 512], GB[1 - w][0:B * IPA, :], 1.0 / WS,
                                         vi_sb[:, w * 512:(w + 1) * 512], ALU.mult, ALU.subtract)\
                   .then_inc(s["ipa_lo"], 1)

        def router_tensor(pe, l, turned):
            name, bias = ("gate", "gate_b") if l == 0 else ("router1", "rb")
            pe.wait_ge(s["ln_tlo"], turned)
            for b in range(B):
                dst = pb[4][0:S, b * E:(b + 1) * E]
                i = 0
                for k in range(2):
                    for qa, qb in PARTS:
                        pe.matmul(dst, xT[:, qa, k, b * S:(b + 1) * S], w0(name, qb, k), start=(i == 0), stop=False)
                        i += 1
                for q in range(2):
                    mm = pe.matmul(dst, ones16[:, 0:S], row(bias, q), start=False, stop=(q == 1))
            mm.then_inc(s[f"rt_mm_{l}"], 1)

        def router_scalar(act, l):
            if l == 0:
                act.wait_ge(s["rt_sm_0"], 1)
                act.activation(w12[:, 0, :], w12[:, 2, :], ACT.Sigmoid).then_inc(s["rt_act_0"], 1)
            else:
                act.wait_ge(s["rt_mm_1"], 1)
                act.activation(lg[:, :, :], pb[4][0:S, 0:B * E].rearrange("p (b e) -> p b e", b=B), ACT.Sigmoid,
                               scale=1.0 / WS).then_inc(s["rt_lg_1"], 1)

        def router_vector(dve, l):
            sm, n = s[f"rt_sm_{l}"], 0
            if l == 0:
                dve.wait_ge(s["rt_mm_0"], 1)
                dve.tensor_scalar(lg[:, :, :], pb[4][0:S, 0:B * E].rearrange("p (b e) -> p b e", b=B), 1.0 / WS,
                                  None, ALU.mult).then_inc(s["rt_lg_0"], 1)
            dve.wait_ge(s[f"rt_lg_{l}"], 1)
            for b in range(B):
                dve.max(m8[:, b, :], lg[:, b, :]).then_inc(s[f"rt_m8_{l}"], 1)
            for b in range(B):
                dve.wait_ge(s[f"rt_m8_{l}"], b + 1)
                dve.max_index(i8[:, b, :], m8[:, b, :], lg[:, b, :]).then_inc(s[f"rt_i8_{l}"], 1)
            dve.wait_ge(s[f"rt_i8_{l}"], B)
            if l == 0:
                dve.tensor_tensor(w12[:, 2, :], m8[:, :, 0], m8[:, :, 1], ALU.subtract).then_inc(sm, 1)
            else:
                dve.tensor_copy(w12[:, 0, :], m8[:, :, 0]).then_inc(sm, 1)
            dve.tensor_copy(i8f[:, :, :], i8[:, :, :]).then_inc(sm, 1)
            dve.wait_ge(sm, 2)
            for j in range(2):
                dve.tensor_tensor(oh[:, j, :, :], bc(iota8[:, :].unsqueeze(1), [S, B, E]),
                                  bc(i8f[:, :, j:j + 1], [S, B, E]), ALU.is_equal).then_inc(sm, 1)
            if l == 0:
                dve.wait_ge(s["rt_act_0"], 1)
                dve.tensor_scalar(w12[:, 1, :], w12[:, 0, :], -1.0, 1.0, ALU.mult, ALU.add).then_inc(sm, 1)
            else:
                dve.tensor_copy(w12[:, 1, :], m8[:, :, 1]).then_inc(sm, 1)
            dve.wait_ge(sm, 5)
            for j in range(2):
                dve.tensor_tensor(oh[:, j, :, :], oh[:, j, :, :], bc(w12[:, j, :].unsqueeze(2), [S, B, E]),
                                  ALU.mult).then_inc(sm, 1)
            dve.wait_ge(sm, 7)
            dve.tensor_tensor(wd[:, :, :], oh[:, 0, :, :], oh[:, 1, :, :], ALU.add).then_inc(s[f"rt_wd_{l}"], 1)

        def expert_order(e, first, last_split):
            todo = [("up", 0, 0)]
            if not last_split:
                todo.append(("cut", 1, 0))
            if not first:
                todo.append(("down", -1, 1))
            if not last_split:
                todo.append(("cut", 1, 1))
            return todo + [("up", 0, 1), ("down", 0, 0)]

        def experts(n, work, stage, eng):
            if stage == "first":
                work("cut", 0, 0, 0)
                work("cut", 0, 0, 1)
                return
            def turn(ev, es, first, last):
                for kind, d, half in expert_order(es, first, last):
                    work(kind, ev + d, es + d, half)
            turn(0, 0, True, False)
            pairs = (n - 2) // 2
            with eng.Fori(0, pairs) as r:
                turn(r * 2 + 1, 1, False, False)
                turn(r * 2 + 2, 2, False, False)
            for e in range(1 + 2 * pairs, n):
                turn(e, e, False, e == n - 1)
            work("down", n - 1, n - 1, 1)

        def up_col(l, part, k, m):
            if part == 2:
                return (2 if l else 1) * 1024 + k * C
            return part * 1024 + k * FF + m * 128

        UP_BANKS = [[pb[0:4]], [pb[0:2], pb[2:4]]]
        SUM = [pb[4:6], pb[6:8]]

        def experts_tensor(pe, l, n, stage="rest"):
            def work(kind, ev, es, half):
                if kind == "up":
                    u0, us = (ev * 2 + half) * NM, (es * 2 + half) * NM
                    if half == 0:
                        pe.wait_ge(s[f"m_lo_{l}"], 2 * ev + 2)
                    for m in range(NM):
                        for part in range(1 + l):
                            banks = UP_BANKS[l][part]
                            if us + m >= len(banks):
                                pe.wait_ge(s["u_hf_1"] if part else s[f"u_act_{l}"], u0 + m - len(banks) + 1)
                            i = 0
                            for k in range(2):
                                for qa, qb in PARTS:
                                    c = up_col(l, part, k, m)
                                    mm = pe.matmul(banks[m % len(banks)][:, 0:HT], MW[:, es % 2, qa, c:c + 128],
                                                   xT[:, qb, k, half * HT:(half + 1) * HT],
                                                   start=(i == 0), stop=(i == 5))
                                    i += 1
                        mm.then_inc(s[f"u_mm_{l}"], 1)
                    if es == 0 and half == 0:
                        biases_tensor(pe, l)
                elif kind == "down":
                    pe.wait_ge(s[f"u_lo_{l}"], (ev * 2 + half + 1) * NM)
                    for c in range(2):
                        i, last = 0, 3 * NM - 1
                        for k in range(NM):
                            for qa, qb in PARTS:
                                c0 = up_col(l, 2, k, 0) + c * 128
                                mm = pe.matmul(SUM[half][c][:, 0:HT], MW[:, es % 2, qa, c0:c0 + 128],
                                               HTt[:, half, qb, k, :],
                                               start=False,
                                               stop=(es == n - 1 and i == last))
                                i += 1
                    mm.then_inc(s[f"d_mm_{l}"], 1)
            experts(n, work, stage, pe)

        MN = [2048, 3072]

        def experts_scalar(act, l, n, stage):
            def work(kind, ev, es, half):
                if kind == "cut":
                    c = slice(0, 1024) if half == 0 else slice(1024, MN[l])
                    act.wait_ge(s[f"m_in{es % 2}_{l}"], (ev + 2 - es % 2) * 8)
                    if es >= 2:
                        act.wait_ge(s[f"d_mm_{l}"], 2 * ev - 3 + half)
                    act.activation(MW[:, es % 2, 0, c], ST[:, es % 2, c], ACT.Copy, scale=WS)\
                       .then_inc(s[f"m_hi_{l}"], 1)
                elif kind == "up":
                    u0, us = (ev * 2 + half) * NM, (es * 2 + half) * NM
                    for m in range(NM):
                        act.wait_ge(s[f"u_mm_{l}"], u0 + m + 1)
                        if us + m >= HB:
                            act.wait_ge(s[f"u_hf_{l}"] if l else s[f"u_lo_{l}"], u0 + m - HB + 1)
                        if l == 0:
                            act.activation(hf[:, m % HB, :], pb[m % 4][:, 0:HT], ACT.Gelu,
                                           bias=bcur[:, es % 2, m:m + 1], scale=1.0 / WS)\
                               .then_inc(s["u_act_0"], 1)
                        else:
                            act.activation(sg[:, m % HB, :], pb[m % 2][:, 0:HT], ACT.Silu, scale=1.0 / WS)\
                               .then_inc(s["u_act_1"], 1)
                    if l == 1 and es == 0 and half == 0:
                        weights_scalar(act, 1)
            experts(n, work, stage, act)

        def experts_vector(dve, l, n, stage):
            def work(kind, ev, es, half):
                if kind == "cut":
                    c = slice(0, 1024) if half == 0 else slice(1024, MN[l])
                    dve.wait_ge(s[f"m_hi_{l}"], 2 * ev + half + 1)
                    if l == 0 and half == 0:
                        dve.tensor_copy(bcur[:, es % 2, :], b1[:, bass.ds(ev, 1), :].rearrange("p a m -> p (a m)"))
                    dve.scalar_tensor_tensor(MW[:, es % 2, 1, c], ST[:, es % 2, c], WS,
                                             MW[:, es % 2, 0, c], ALU.mult, ALU.subtract)\
                       .then_inc(s[f"m_lo_{l}"], 1)
                elif kind == "up":
                    u0, us = (ev * 2 + half) * NM, (es * 2 + half) * NM
                    for m in range(NM):
                        n_, ns = u0 + m, us + m
                        if l == 0:
                            dve.wait_ge(s["u_wt_0"], n_ + 1)
                        elif es == 0:
                            dve.wait_ge(s["u_act_1"], n_ + 1)
                        else:
                            dve.wait_ge(s["u_wt_1"], n_ - 2 * NM + 1)
                        if l == 1:
                            if ns >= HB:
                                dve.wait_ge(s["u_lo_1"], n_ - HB + 1)
                            dve.scalar_tensor_tensor(hf[:, m % HB, :], UP_BANKS[1][1][m % 2][:, 0:HT], HS / WS,
                                                     sg[:, m % HB, :],
                                                     ALU.mult, ALU.mult).then_inc(s["u_hf_1"], 1)
                            dve.wait_ge(s["u_hf_1"], n_ + 1)
                        if m == 0 and es >= 1:
                            dve.wait_ge(s[f"d_mm_{l}"], (ev - 1) * 2 + half + 1)
                        dve.tensor_copy(HTt[:, half, 0, m, :], hf[:, m % HB, :]).then_inc(s[f"u_hi_{l}"], 1)
                        dve.wait_ge(s[f"u_hi_{l}"], n_ + 1)
                        dve.tensor_tensor(HTt[:, half, 1, m, :], hf[:, m % HB, :], HTt[:, half, 0, m, :],
                                          ALU.subtract).then_inc(s[f"u_lo_{l}"], 1)
                else:
                    if l == 0 and half == 0 and es == 0:
                        gate_abel_vector(dve)
                    if l == 0 and half == 0 and es == n - 1:
                        residual_abel_vector(dve)
            experts(n, work, stage, dve)

        def experts_gpsimd(pool, l, n):
            def work(kind, ev, es, half):
                if kind != "up" or es < l:
                    return
                if half == 0:
                    pool.wait_ge(s[f"w_in{es % 2}_{l}"], (ev + 2 - es % 2) * 8 if l == 0 else (ev + es % 2) * 8)
                for m in range(NM):
                    n_ = (ev * 2 + half) * NM + m
                    tile = (sg if l else hf)[:, m % HB, :]
                    pool.wait_ge(s[f"u_act_{l}"], n_ + 1)
                    pool.tensor_tensor(tile, tile, wdB[:, es % 2, half * HT:(half + 1) * HT], ALU.mult)\
                        .then_inc(s[f"u_wt_{l}"], 1)
            experts(n, work, "rest", pool)

        def experts_sync(sp, l, n):
            def weights(e):
                if e >= 2:
                    sp.wait_ge(s[f"u_lo_{l}"], (e - 1) * 2 * NM)
                sp.dma_start(wdB[:, e % 2, :], wd_dram[l][e - l:e - l + 1, :, :].rearrange("a g n -> a (g n)")[0, :]
                             .partition_broadcast(128)).then_inc(s[f"w_in{e % 2}_{l}"], 16)
            for e in range(n):
                if e == 2:
                    sp.wait_ge(s[f"wd_act_{l}"], 2)
                    sp.dma_start(wd_dram[l], wdf[:, :, :]).then_inc(s[f"wd_out_{l}"], 16)
                    sp.wait_ge(s[f"wd_out_{l}"], 16)
                    for e0 in range(l, 2):
                        weights(e0)
                if e >= 2:
                    sp.wait_ge(s[f"m_lo_{l}"], 2 * (e - 1))
                sp.dma_start(ST[:, e % 2, 0:MN[l]], a[f"moe{l}"][e, :, :]).then_inc(s[f"m_in{e % 2}_{l}"], 16)
                if e >= 2:
                    weights(e)

        def weights_tensor(pe, l):
            pe.wait_ge(s[f"rt_wd_{l}"], 1)
            for g in range(2):
                for j in range(4):
                    mm = pe.transpose(pb[4 + g][0:E, j * S:(j + 1) * S], wd[:, 4 * g + j, :], identf[0:S, 0:S])
                mm.then_inc(s[f"wd_mm_{l}"], 1)

        def weights_scalar(act, l):
            for g in range(2):
                act.wait_ge(s[f"wd_mm_{l}"], g + 1)
                act.activation(wdf[:, g, :], pb[4 + g][0:E, 0:HT], ACT.Copy, scale=1.0 if l else HS)\
                   .then_inc(s[f"wd_act_{l}"], 1)

        def abel_tensor(pe):
            for b in range(B):
                if b == B // 2:
                    weights_tensor(pe, 0)
                if b >= 2:
                    pe.wait_ge(s["f_act_0"], b - 1)
                i = 0
                for k in range(2):
                    for qa, qb in PARTS:
                        pe.matmul(GB[b % 2][0:S, 0:C], xT[:, qa, k, b * S:(b + 1) * S], w0("abel", qb, k),
                                  start=(i == 0), stop=False)
                        i += 1
                for q in range(2):
                    mm = pe.matmul(GB[b % 2][0:S, 0:C], ones16[:, 0:S], row("abel_b", q), start=False, stop=(q == 1))
                mm.then_inc(s["f_mm_0"], 1)

        def abel_scalar(act):
            for b in range(B):
                if b == B // 2:
                    weights_scalar(act, 0)
                act.wait_ge(s["f_mm_0"], b + 1)
                act.activation(AB[:, b, :], GB[b % 2][0:S, 0:C], ACT.Gelu, scale=1.0 / WS).then_inc(s["f_act_0"], 1)
            act.wait_ge(s["wd_act_0"], 2)
            act.activation(wdT[:, 0, :], wdf[:, :, :].rearrange("p g n -> p (g n)"), ACT.Copy).then_inc(s["wd_act_0"], 1)

        def biases_vector(dve):
            dve.wait_ge(s["wd_act_0"], 3)
            dve.tensor_tensor(wdT[:, 1, :], wdf[:, :, :].rearrange("p g n -> p (g n)"), wdT[:, 0, :], ALU.subtract)\
               .then_inc(s["wd_lo_0"], 1)

        def biases_tensor(pe, l):
            if l:
                weights_tensor(pe, 1)
                pe.wait_ge(s["wd_act_1"], 2)
                for half in range(2):
                    for c in range(2):
                        pe.matmul(SUM[half][c][:, 0:HT], zero16[:, :], ones16[:, 0:HT], start=True, stop=False)
                return
            pe.wait_ge(s["f_act_0"], B)
            pe.wait_ge(s["wd_lo_0"], 1)
            for half in range(2):
                for c in range(2):
                    for i, (qa, qb) in enumerate(PARTS):
                        pe.matmul(SUM[half][c][:, 0:HT], eb2[:, qa, c * 128:(c + 1) * 128],
                                  wdT[:, qb, half * HT:(half + 1) * HT], start=(i == 0), stop=False)

        def moved_scalar(act):
            act.wait_ge(s["d_mm_0"], 2 * E)
            for k, g in GROUPS:
                act.activation(xT[:, 0, k, g * HT:(g + 1) * HT], SUM[g][k][:, 0:HT], ACT.Copy, scale=1.0 / (WS * HS))\
                   .then_inc(s["ln_thi"], 1)

        def moved_vector(dve):
            for n, (k, g) in enumerate(GROUPS):
                dve.wait_ge(s["ln_thi"], 8 + n + 1)
                dve.scalar_tensor_tensor(xT[:, 1, k, g * HT:(g + 1) * HT], SUM[g][k][:, 0:HT], 1.0 / (WS * HS),
                                         xT[:, 0, k, g * HT:(g + 1) * HT], ALU.mult, ALU.subtract)\
                   .then_inc(s["ln_tlo"], 1)

        RES = flat[:, 0:4 * HT].rearrange("p (g k n) -> p g k n", g=2, k=2)

        def result_vector(dve, g):
            dve.wait_ge(s["d_mm_1"], 2 * E + g + 1)
            for k in range(2):
                dve.tensor_scalar(RES[:, g, k, :], SUM[g][k][:, 0:HT], 1.0 / (WS * HS), None, ALU.mult)\
                   .then_inc(s["moved_1"], 1)

        def result_tensor(pe, g):
            pe.wait_ge(s["moved_1"], 2 * g + 2)
            pe.wait_ge(s["u_act_1"], (E + 1) * 2 * NM)
            pe.wait_ge(s["u_hf_1"], (E + 1) * 2 * NM)
            for j in range(2):
                for b in range(2):
                    for k in range(2):
                        mm = pe.transpose(pb[2 * g + j][0:S, b * C + k * 128:b * C + (k + 1) * 128],
                                          RES[:, g, k, (2 * j + b) * S:(2 * j + b + 1) * S], identf[:, :])
                mm.then_inc(s["f_mm_1"], 1)

        def result_add_vector(dve, g):
            for j in range(2):
                dve.wait_ge(s["f_mm_1"], 2 * g + j + 1)
                xb = X[:, 4 * g + 2 * j:4 * g + 2 * j + 2, :].rearrange("p b c -> p (b c)")
                dve.scalar_tensor_tensor(xb, pb[2 * g + j][0:S, 0:2 * C], tg[:, 3:4], xb, ALU.mult, ALU.add)\
                   .then_inc(s["ffn"], 1)

        EU = []
        for t in range(DEG - 1, 0, -1):
            EU += [("horner", g, t) for g in range(3)]
        for _ in range(SQ):
            EU += [("turn", g, 0) for g in range(3)] + [("square", g, 0) for g in range(3)]
        EU += [("turn", 0, 0), ("turn", 1, 0), ("pair", 1, 0), ("pair", 0, 0)]

        def expm_tensor(pe):
            pe.wait_ge(s["e_lo"], 4)
            for n, (kind, g, t) in enumerate(EU):
                bank = pb[n % 3]
                if kind == "pair":
                    pe.wait_ge(s["e_lo"], 4 + n)
                elif n >= 3:
                    pe.wait_ge(s["e_lo"], 4 + n - 2)
                if kind == "turn":
                    for c in range(2):
                        for m in range(2):
                            mm = pe.transpose(bank[:, c * 256 + m * 128:c * 256 + (m + 1) * 128],
                                              RF[:, g, m, c * 128:(c + 1) * 128], identf[:, :])
                else:
                    left = BT if kind == "horner" else RT
                    right = 2 if kind == "pair" else g
                    for m in range(2):
                        i = 0
                        for k in range(2):
                            for qa, qb in PARTS:
                                mm = pe.matmul(bank[:, m * 256:(m + 1) * 256], left[:, qa, g, k, m * 128:(m + 1) * 128],
                                               R16[:, qb, right, k, :], start=(i == 0), stop=(i == 5))
                                i += 1
                mm.then_inc(s["e_mm"], 1)

        flatg = ST[:, :, 0:3 * 512].rearrange("p a (g n) -> p a g n", g=3)

        def expm_scalar(act):
            act.wait_ge(s["e_in"], 32)
            act.activation(BT[:, 0, :, :, :].rearrange("p g k n -> p g (k n)"), flatg[:, 0, :, :], ACT.Copy,
                           scale=WS / 2 ** SQ).then_inc(s["e_hi"], 1)
            for g in range(3):
                act.wait_ge(s["e_f"], 2 + g + 1)
                act.activation(R16[:, 0, g, :, :], RF[:, g, :, :], ACT.Copy).then_inc(s["e_hi"], 1)
            nf = 0
            for n, (kind, g, t) in enumerate(EU):
                dst = (RT if kind == "turn" else R16)[:, 0, 2 if kind == "pair" else g, :, :]
                if kind == "turn":
                    act.wait_ge(s["e_mm"], n + 1)
                    src = pb[n % 3][:, :].rearrange("p (k n) -> p k n", k=2)
                else:
                    nf += 1
                    act.wait_ge(s["e_f"], 5 + nf)
                    src = RF[:, 2 if kind == "pair" else g, :, :]
                act.activation(dst, src, ACT.Copy).then_inc(s["e_hi"], 1)

        def expm_vector(dve):
            dve.memset(eye, 0.0).then_inc(s["e_f"], 1)
            dve.wait_ge(s["e_f"], 1)
            for k in range(2):
                x = dve.tensor_scalar(eye[:, k * 256 + k * 128:k * 256 + (k + 1) * 128], identf[:, :], WS, None, ALU.mult)
            x.then_inc(s["e_f"], 1)
            dve.wait_ge(s["e_f"], 2)
            dve.wait_ge(s["e_in"], 32)
            for g in range(3):
                dve.scalar_tensor_tensor(RF[:, g, :, :].rearrange("p k n -> p (k n)"), flatg[:, 1, g, :],
                                         WS / 2 ** SQ / DEG, eye, ALU.mult, ALU.add).then_inc(s["e_f"], 1)
            dve.wait_ge(s["e_hi"], 1)
            dve.scalar_tensor_tensor(BT[:, 1, :, :, :].rearrange("p g k n -> p g (k n)"), flatg[:, 0, :, :],
                                     WS / 2 ** SQ, BT[:, 0, :, :, :].rearrange("p g k n -> p g (k n)"),
                                     ALU.mult, ALU.subtract).then_inc(s["e_lo"], 1)
            for g in range(3):
                dve.wait_ge(s["e_hi"], 2 + g)
                dve.tensor_tensor(R16[:, 1, g, :, :], RF[:, g, :, :], R16[:, 0, g, :, :], ALU.subtract)\
                   .then_inc(s["e_lo"], 1)

            def cut(n):
                kind, g, t = EU[n]
                if kind == "turn":
                    src, dst, hi_ = pb[n % 3][:, :].rearrange("p (k n) -> p k n", k=2), RT[:, 1, g, :, :], \
                        RT[:, 0, g, :, :]
                else:
                    r = 2 if kind == "pair" else g
                    src, dst, hi_ = RF[:, r, :, :], R16[:, 1, r, :, :], R16[:, 0, r, :, :]
                dve.wait_ge(s["e_hi"], 4 + n + 1)
                dve.tensor_tensor(dst, src, hi_, ALU.subtract).then_inc(s["e_lo"], 1)

            nf = 0
            for n, (kind, g, t) in enumerate(EU):
                if kind == "pair":
                    cut(n - 1)
                r = 2 if kind == "pair" else g
                src = pb[n % 3][:, :].rearrange("p (k n) -> p k n", k=2)
                if kind != "turn":
                    nf += 1
                    dve.wait_ge(s["e_mm"], n + 1)
                    if n >= 3:
                        dve.wait_ge(s["e_lo"], 4 + n - 2 if kind != "pair" else 4 + n)
                    if kind == "horner":
                        x = dve.scalar_tensor_tensor(RF[:, g, :, :].rearrange("p k n -> p (k n)"), pb[n % 3][:, :],
                                                     1.0 / (WS * t), eye, ALU.mult, ALU.add)
                    else:
                        x = dve.tensor_scalar(RF[:, r, :, :], src, 1.0 / WS, None, ALU.mult)
                    x.then_inc(s["e_f"], 1)
                if n >= 1 and kind != "pair":
                    cut(n - 1)
            dve.wait_ge(s["e_f"], 5 + nf)
            cut(len(EU) - 1)

        def mix_tensor(pe, turned):
            pe.wait_ge(s["ln_tlo"], turned)
            pe.wait_ge(s["e_lo"], 4 + len(EU))
            for b in range(B):
                if b >= 2:
                    pe.wait_ge(s["f_dve_0"], b - 1)
                i = 0
                for k in range(2):
                    for qa, qb in PARTS:
                        mm = pe.matmul(GB[b % 2][0:S, 0:C], xT[:, qa, k, b * S:(b + 1) * S], R16[:, qb, 2, k, :],
                                       start=(i == 0), stop=(i == 5))
                        i += 1
                mm.then_inc(s["f_mm_0"], 1)

        def gate_abel_vector(dve):
            dve.tensor_tensor(gam[:, 2, :], gam[:, 2, :], gam[:, 3, :], ALU.add).then_inc(s["mix"], 1)
            dve.wait_ge(s["mix"], 1)
            dve.wait_ge(s["f_act_0"], B)
            for b in range(B):
                if b >= HB:
                    dve.wait_ge(s["mix"], 1 + b - HB + 1)
                dve.tensor_tensor_reduce(sg[0:S, b % HB, 0:C], AB[:, b, :], gam[:, 2, :], 1.0, 0.0, ALU.mult,
                                         ALU.add, zz[:, 0, b:b + 1]).then_inc(s["mix"], 1)

        def residual_abel_vector(dve):
            dve.tensor_tensor(Y[:, :, :], Y[:, :, :], AB[:, :, :], ALU.add).then_inc(s["mix"], 1)
            dve.wait_ge(s["mix"], B + 2)
            dve.scalar_tensor_tensor(X[:, :, :].rearrange("p b c -> p (b c)"), Y[:, :, :].rearrange("p b c -> p (b c)"),
                                     tg[:, 1:2], X[:, :, :].rearrange("p b c -> p (b c)"), ALU.mult, ALU.add)\
               .then_inc(s["mix"], 1)
            dve.wait_ge(s["mix"], B + 3)

        def mix_scalar(act):
            act.wait_ge(s["mix"], 2 * B + 4)
            act.activation(zz[:, 1, :], zz[:, 0, :], ACT.Sigmoid, bias=gc_b[:, 0:1], scale=1.0)\
               .then_inc(s["f_act_0"], 1)

        def mix_vector(dve):
            done = B + 3

            def gate(b):
                dve.wait_ge(s["f_dve_0"], b + 1)
                dve.tensor_tensor_reduce(junk[:, b, :], Z[:, b, :], gam[:, 3, :], 1.0, 0.0, ALU.mult,
                                         ALU.add, zz[:, 2, b:b + 1]).then_inc(s["mix"], 1)

            for b in range(B):
                dve.wait_ge(s["f_mm_0"], B + b + 1)
                dve.scalar_tensor_tensor(Z[:, b, :], GB[b % 2][0:S, 0:C], 1.0 / WS, AB[:, b, :], ALU.mult,
                                         ALU.subtract).then_inc(s["f_dve_0"], 1)
                if b >= 1:
                    gate(b - 1)
            gate(B - 1)
            dve.wait_ge(s["mix"], done + B)
            dve.tensor_tensor(zz[:, 0, :], zz[:, 0, :], zz[:, 2, :], ALU.add).then_inc(s["mix"], 1)
            dve.wait_ge(s["f_act_0"], B + 1)
            dve.tensor_scalar(zz[:, 2, :], zz[:, 1, :], tg[:, 1:2], None, ALU.mult).then_inc(s["mix"], 1)
            dve.wait_ge(s["mix"], done + B + 2)
            for b in range(B):
                dve.scalar_tensor_tensor(X[:, b, :], Z[:, b, :], zz[:, 2, b:b + 1], X[:, b, :], ALU.mult,
                                         ALU.add).then_inc(s["ffn"], 1)

        FFN0 = 2 + B
        PHASES = a["phases"]
        G_ALL = [2 * counts(L)[0] + (B - 2) * counts(L)[1] + 2 * len(L.out) for L in layers]
        block = ctx.enter_context(nc.Block())

        @block.sync
        def _(sp):
            sp.dma_start(X[:, :, :], a["x"].rearrange("b s c -> s b c")).then_inc(s["x_in"], 16)
            sp.dma_start(tg[:, :], a["gates"].partition_broadcast(S)).then_inc(s["small_in"], 16)
            sp.dma_start(lora_s[:, :], a["alphas"].partition_broadcast(128)).then_inc(s["small_in"], 16)
            sp.dma_start(gam[:, :, :], a["vecs"].partition_broadcast(S)).then_inc(s["small_in"], 16)
            sp.dma_start(b1[:, :, :], a["eb1"]).then_inc(s["small_in"], 16)
            sp.dma_start(gc_b[:, :], a["gc_b"].partition_broadcast(S)).then_inc(s["small_in"], 16)
            chunks_sync(sp, 0, NC0)
            if PHASES >= 2:
                sp.wait_ge(s["g_free0"], G_ALL[0])
                experts_sync(sp, 0, E)
                sp.wait_ge(s["m_lo_0"], 2 * E)
                for j in range(2):
                    sp.dma_start(ST[:, j, 0:3 * 512], a["gens"][j, :, :]).then_inc(s["e_in"], 16)
            if PHASES >= 3:
                sp.wait_ge(s["e_f"], 5)
                sp.wait_ge(s["e_lo"], 1)
                sp.wait_ge(s["chunk_lo"], NC0)
                chunks_sync(sp, NC0, NC1)
                sp.wait_ge(s["ipa_lo"], 3)
                for q, part in enumerate((vi_sb, vi_sb2)):
                    sp.dma_start(vi_dram[:, q, :], part).then_inc(s["ipa_stored"], 16)
                sp.wait_ge(s["ipa_stored"], 32)
                attention_sync(sp, layers[1])
            if PHASES >= 4:
                sp.wait_ge(s["g_free1"], G_ALL[1])
                experts_sync(sp, 1, E + 1)
            if PHASES == 1:
                sp.wait_ge(s["g_free0"], G_ALL[0])
            if PHASES == 2:
                sp.wait_ge(s["ffn"], FFN0)
            if PHASES == 3:
                sp.wait_ge(s["g_free1"], G_ALL[1])
            if PHASES == 4:
                sp.wait_ge(s["ffn"], FFN0 + 4)
            sp.dma_start(out.rearrange("b s c -> s b c"), X[:, :, :]).then_inc(s["x_in"], 16)
            sp.wait_ge(s["x_in"], 32)

        @block.gpsimd
        def _(pool):
            pool.memset(identf[:, :], 0.0).then_inc(s["ident_set"], 1)
            pool.wait_ge(s["ident_set"], 1)
            pool.affine_select(out=identf[:, :], in_=identf[:, :], compare_op=ALU.not_equal, fill=1.0, base=0,
                               pattern=[[-1, 128]], channel_multiplier=1).then_inc(s["ident_set"], 1)
            pool.memset(mask[:, :], 1.0).then_inc(s["ident_set"], 1)
            pool.wait_ge(s["ident_set"], 3)
            pool.affine_select(out=mask[:, :], in_=mask[:, :], compare_op=ALU.is_ge, fill=0.0, base=0,
                               pattern=[[-16, 8]], channel_multiplier=1).then_inc(s["ident_set"], 1)
            pool.wait_ge(s["ident_set"], 4)
            pool.affine_select(out=mask[:, :], in_=mask[:, :], compare_op=ALU.is_ge, fill=0.0, base=15,
                               pattern=[[16, 8]], channel_multiplier=-1).then_inc(s["ident_set"], 1)
            pool.iota(iota8[:, :], [[1, E]], base=0, channel_multiplier=0, allow_small_or_imprecise_dtypes=True)\
                .then_inc(s["ident_set"], 1)
            pool.wait_ge(s["ident_set"], 5)
            attention_gpsimd(pool, layers[0])
            if PHASES >= 2:
                experts_gpsimd(pool, 0, E)
            if PHASES >= 3:
                pool.wait_ge(s["ffn"], FFN0)
                pool.memset(qflat, 0.0).then_inc(s["const_set"], 1)
                attention_gpsimd(pool, layers[1])
            if PHASES >= 4:
                experts_gpsimd(pool, 1, E + 1)

        @block.scalar
        def _(act):
            norm_scalar(act, 0)
            act.wait_ge(s["small_in"], 16 * 5)
            act.activation(tg[:, :], tg[:, :], ACT.Tanh).then_inc(s["tanh_done"], 1)
            chunks_scalar(act, 0, NC0)
            turn_scalar(act, 0)
            attention_scalar(act, layers[0])
            if PHASES >= 2:
                norm_scalar(act, 1)
                norm_scalar(act, 2)
                experts_scalar(act, 0, E, "first")
                turn_scalar(act, 1)
                router_scalar(act, 0)
                abel_scalar(act)
                experts_scalar(act, 0, E, "rest")
                moved_scalar(act)
                expm_scalar(act)
                mix_scalar(act)
            if PHASES >= 3:
                act.wait_ge(s["ffn"], FFN0)
                chunks_scalar(act, NC0, NC0 + 2)
                norm_scalar(act, 3)
                chunks_scalar(act, NC0 + 2, NC0 + LORA_CHUNKS)
                turn_scalar(act, 3)
                chunks_scalar(act, NC0 + LORA_CHUNKS, NC1)
                ipa_scalar(act)
                act.wait_ge(s["const_set"], 1)
                attention_scalar(act, layers[1])
            if PHASES >= 4:
                norm_scalar(act, 4)
                experts_scalar(act, 1, E + 1, "first")
                turn_scalar(act, 4)
                router_scalar(act, 1)
                experts_scalar(act, 1, E + 1, "rest")

        @block.vector
        def _(dve):
            dve.memset(ones16[:, :], 1.0).then_inc(s["ones_set"], 1)
            dve.memset(zero16[:, :], 0.0).then_inc(s["ones_set"], 1)
            dve.memset(os16[:, :], OS).then_inc(s["ones_set"], 1)
            dve.memset(cT[KC:KC + 1, 0, 1, :], 1.0).then_inc(s["ones_set"], 1)
            dve.memset(cT[KC:KC + 1, 1, 1, :], 0.0).then_inc(s["ones_set"], 1)
            dve.wait_ge(s["x_in"], 16)
            norm_vector(dve, 0, X, Y)
            chunks_vector(dve, 0, NC0)
            turn_vector(dve, 0)
            dve.wait_ge(s["tanh_done"], 1)
            dve.tensor_scalar(tgs[:, 0:1], tg[:, 0:1], 1.0 / WS, None, ALU.mult).then_inc(s["lora_scale"], 1)
            dve.tensor_scalar(tgs[:, 1:2], tg[:, 2:3], 1.0 / (WS * OS), None, ALU.mult).then_inc(s["lora_scale"], 1)
            dve.tensor_scalar(lora_s[:, :], lora_s[:, :], 1.0 / (RANK * WS * WS), None, ALU.mult)\
               .then_inc(s["lora_scale"], 1)
            dve.wait_ge(s["lora_scale"], 3)
            attention_vector(dve, layers[0])
            if PHASES >= 2:
                dve.wait_ge(s["g_free0"], G_ALL[0])
                norm_vector(dve, 1, X, Y)
                norm_vector(dve, 2, Y, Z)
                dve.wait_ge(s["ln_norm"], 3 * B)
                dve.tensor_tensor(Z[:, :, :], Z[:, :, :], bc(gam[:, 0:1, :], [S, B, C]), ALU.mult).then_inc(s["ffn"], 1)
                dve.wait_ge(s["ffn"], 1)
                dve.tensor_tensor(Z[:, :, :], Z[:, :, :], bc(gam[:, 1:2, :], [S, B, C]), ALU.add).then_inc(s["ffn"], 1)
                turn_vector(dve, 1)
                dve.wait_ge(s["ident_set"], 6)
                experts_vector(dve, 0, E, "first")
                router_vector(dve, 0)
                biases_vector(dve)
                experts_vector(dve, 0, E, "rest")
                moved_vector(dve)
                expm_vector(dve)
                mix_vector(dve)
            if PHASES >= 3:
                dve.wait_ge(s["ffn"], FFN0)
                norm_vector(dve, 3, X, Y)
                chunks_vector(dve, NC0, NC0 + LORA_CHUNKS)
                turn_vector(dve, 3)
                for q in range(2):
                    for k in range(2):
                        dve.tensor_copy(ci_sb[:, q, k, :].rearrange("p (b n) -> p b n", b=B), cI[q][k])\
                           .then_inc(s["ipa_ctx"], 1)
                chunks_vector(dve, NC0 + LORA_CHUNKS, NC1)
                ipa_vector(dve)
                dve.wait_ge(s["const_set"], 1)
                attention_vector(dve, layers[1])
            if PHASES >= 4:
                dve.wait_ge(s["g_free1"], G_ALL[1])
                norm_vector(dve, 4, X, Y)
                turn_vector(dve, 4)
                experts_vector(dve, 1, E + 1, "first")
                router_vector(dve, 1)
                experts_vector(dve, 1, E + 1, "rest")
                for g in range(2):
                    result_vector(dve, g)
                    result_add_vector(dve, g)

        @block.tensor
        def _(pe):
            pe.wait_ge(s["ident_set"], 2)
            pe.wait_ge(s["ln_norm"], B)
            turn_tensor(pe, 0, Y)
            pe.wait_ge(s["ln_tlo"], 4)
            pe.wait_ge(s["chunk_lo"], NC0)
            pe.wait_ge(s["ones_set"], 5)
            attention_tensor(pe, layers[0])
            if PHASES >= 2:
                pe.wait_ge(s["ffn"], 2)
                turn_tensor(pe, 1, Z)
                router_tensor(pe, 0, 8)
                abel_tensor(pe)
                experts_tensor(pe, 0, E)
                expm_tensor(pe)
                mix_tensor(pe, 12)
            if PHASES >= 3:
                pe.wait_ge(s["ln_norm"], 4 * B)
                turn_tensor(pe, 3, Y)
                pe.wait_ge(s["ln_tlo"], 16)
                chunks_tensor(pe, NC0, NC1)
                pe.wait_ge(s["chunk_added"], lora_before[NC1])
                pe.wait_ge(s["chunk_lo"], NC1)
                pe.wait_ge(s["ipa_ctx"], 4)
                ipa_tensor(pe)
                pe.wait_ge(s["ln_tlo"], 16)
                pe.wait_ge(s["ipa_lo"], 3)
                pe.wait_ge(s["const_set"], 1)
                attention_tensor(pe, layers[1])
            if PHASES >= 4:
                pe.wait_ge(s["ln_norm"], 5 * B)
                turn_tensor(pe, 4, Y)
                router_tensor(pe, 1, 20)
                experts_tensor(pe, 1, E + 1)
                for g in range(2):
                    result_tensor(pe, g)


def _layout(inputs, np):
    i = {k: np.asarray(v) for k, v in inputs.items()}
    f = np.float32

    def tiles(w, rows):
        n = w.shape[0] // rows
        return w.reshape(n, rows, -1).transpose(1, 0, 2).reshape(rows, -1)

    def biased(w, b):
        t = w.reshape(2, KC, -1)
        last = np.stack([np.zeros_like(b), b])[:, None, :]
        return np.concatenate([t, last], 1).transpose(1, 0, 2).reshape(KC + 1, -1)

    out = {
        "x": i["x"],
        "ctxT": i["ctx_768"].reshape(B * KV, CKV).T,
        "pa0": np.concatenate([tiles(w, 128) for w in (i["L0_xattn_Wq"], i["L0_xattn_Wo"], i["L0_ffn_abel_w"],
                                                       i["L0_ffn_moe_gate_w"], i["L1_ffn_Wr"].T)], 1),
        "kv0": np.concatenate([biased(i["L0_xattn_Wk"], i["L0_xattn_bk"]),
                               biased(i["L0_xattn_Wv"], i["L0_xattn_bv"])], 1),
        "rows": np.concatenate([i["L0_xattn_bq"], i["L0_xattn_bo"], i["L0_ffn_abel_b"], i["L0_ffn_moe_gate_b"],
                                i["L1_xattn_bo"], i["L1_ffn_rb"]])[None, :],
        "gates": np.stack([i["g_xattn"][0], i["g_ffn"][0], i["g_xattn"][1], i["g_ffn"][1]]),
        "alphas": np.concatenate([i["L1_xattn_q_alpha"], i["L1_xattn_k_alpha"], i["L1_xattn_v_alpha"],
                                  i["L1_xattn_o_alpha"]]),
        "vecs": np.stack([i["L0_ffn_ln_gamma"], i["L0_ffn_ln_beta"], i["L0_ffn_gc_w"][0:C, 0],
                          i["L0_ffn_gc_w"][C:, 0]]),
        "eb1": i["L0_ffn_eb1"].reshape(E, NM, 128).transpose(2, 0, 1),
        "gc_b": i["L0_ffn_gc_b"],
        "eb2": i["L0_ffn_eb2"],
        "moe0": np.stack([np.concatenate([tiles(i["L0_ffn_ew1"][e], 128), tiles(i["L0_ffn_ew2"][e], 128)], 1)
                          for e in range(E)]),
        "moe1": np.stack([np.concatenate([tiles(w.T, 128) for w in (g, u, d)], 1) for g, u, d in
                          [(i["L1_ffn_Wg_s"], i["L1_ffn_Wu_s"], i["L1_ffn_Wd_s"])] +
                          [(i["L1_ffn_Wg"][e], i["L1_ffn_Wu"][e], i["L1_ffn_Wd"][e]) for e in range(E)]]),
        "gens": np.stack([np.concatenate([tiles(m, 128) for m in ms], 1) for ms in
                          (i["L0_ffn_gens"].transpose(0, 2, 1), i["L0_ffn_gens"])]),
        "lora": np.tile(np.concatenate([i[f"L1_xattn_{n}_down"].T for n in "qkvo"] +
                                       [i[f"L1_xattn_{n}_up"] for n in "qkvo"], 1), (3, 1)),
        "w1q": tiles(i["L1_xattn_Wq"], 128),
        "w1k": tiles(i["L1_xattn_Wk"], KC),
        "w1v": tiles(i["L1_xattn_Wv"], KC),
        "w1o": tiles(i["L1_xattn_Wo"], 128),
        "w1ki": tiles(i["L1_xattn_Wk_ipa"], KC),
        "w1vi": tiles(i["L1_xattn_Wv_ipa"], KC),
    }
    return {k: np.ascontiguousarray(v) for k, v in out.items()}


PHASES = 4


def kernel(**inputs):
    import numpy as _np
    import concourse.bacc as _bacc
    from concourse.bass_utils import run_bass_kernel_spmd as _run

    arrays = _layout(inputs, _np)
    nc = _bacc.Bacc("TRN2", target_bir_lowering=False, num_devices=1)
    args = {n: nc.dram_tensor(f"in_{n}", v.shape, F32, kind="ExternalInput").ap() for n, v in arrays.items()}
    args["phases"] = PHASES
    res = nc.dram_tensor("out_0", (B, S, C), F32, kind="ExternalOutput").ap()
    build(nc, args, res)
    r = _run(nc, [{f"in_{n}": v for n, v in arrays.items()}], core_ids=[0])
    return r.results[0]["out_0"]
```

```python
from contextlib import ExitStack

import concourse.bass as bass
from concourse import mybir

F32 = mybir.dt.float32
F16 = mybir.dt.float16
U32 = mybir.dt.uint32
ALU = mybir.AluOpType
ACT = mybir.ActivationFunctionType
AX = mybir.AxisListType

B, S, C = 8, 112, 256
KV, CKV = 375, 192
H = 16
K2 = CKV - 128
CHUNK = 125
NCH = KV // CHUNK
T = B * S
HT = T // 2
E = 8
FF = 512
NM = FF // 128
WS = 64.0
CLAMP = 10000.0
EPS = 1e-5
IPA = 4
ORG = KV - IPA
RANK = 32
HS = 16.0
OS = 16.0
SQ, DEG = 2, 8
PARTS = ((0, 0), (0, 1), (1, 0))

ROW = {}
_at = 0
for _n, _l in (("bq", C), ("bo0", C), ("abel_b", C), ("gate_b", E), ("bo1", C), ("rb", E)):
    ROW[_n] = (_at, _l)
    _at += _l
ROWS = _at

PA0 = {"Wq": (0, C), "Wo": (2 * C, C), "abel": (4 * C, C), "gate": (6 * C, E), "router1": (6 * C + 2 * E, E)}
PA0_N = 6 * C + 4 * E
STAGE_N = 3072
NORM_LAG = (3, 3)
FIRST_BETWEEN = 6
SPLIT_AT = 4
HB = 4
DOWN_N, UP_N = C + 2 * 256 + 1024, 3 * 1024 + C
STAGES, CHUNK_N = 3, 2048

LN_SMALL = 7


class Layer:

    def __init__(self, index, dim):
        self.index, self.dim = index, dim
        self.width = H * dim
        self.tiles = self.width // 128
        self.qt = min(4, self.tiles)
        self.per_tile = 128 // dim
        self.vw = min(512, self.width)
        self.grouped = 512 // (2 * dim)
        self.groups = H // self.grouped
        self.keys = KV if index == 0 else ORG
        nq = self.tiles // self.qt
        self.q_units = [("q", g) for g in range(nq)]
        self.k_units = [("k", t) for t in range(self.tiles)]
        self.v_units = [("v", c, w) for c in range(NCH) for w in range(self.width // self.vw)]
        self.i_units = [("i",)] if index else []
        self.front = self.q_units + self.k_units + self.i_units + self.v_units
        self.out = [("t", g) for g in range(nq)] + [("o",)]
        if index == 0:
            at = {0: 0, 1: 3, 2: 5, 3: 7, 4: 9, 5: 11}
            out_at = {0: 5, 1: 8}
        else:
            at = {n: min(15, n) for n in range(len(self.front))}
            out_at = {0: 4, 1: 5, 2: 11}
        self.steps = [[] for _ in range(H)]
        for n, u in enumerate(self.front):
            self.steps[at[n]].append(("front", u))
        for n, u in enumerate(self.out):
            self.steps[out_at[n]].append(("out", u))

    def units(self, kinds):
        n, found = 0, []
        for h in range(H):
            for kind, u in self.steps[h]:
                if kind in kinds:
                    found.append((h, kind, u, n))
                    n += 1
        return found


def acts(u):
    return u[0] not in ("i", "o")


def build(nc, a, out):
    ctx = ExitStack()
    with ctx:
        def sb(name, shape, dt=F32):
            return ctx.enter_context(nc.sbuf_tensor(name, shape, dt))

        def sem(name):
            return ctx.enter_context(nc.semaphore(name))

        X = sb("X", [S, B, C])
        Y = sb("Y", [S, B, C])
        ZA = sb("Z", [128, B, C])
        Z = ZA[0:S]
        xT = sb("xT", [128, 2, 2, T], F16)
        cT = sb("cT", [128, 2, 2, B * KV], F16)
        ST = sb("ST", [128, 2, STAGE_N])
        W0 = sb("W0", [128, 2, PA0_N], F16)
        WKV0 = sb("WKV0", [128, 4, 2 * C], F16)
        RW = sb("RW", [1, 2, ROWS], F16)
        W1 = sb("W1", [128, 2, 8 * 1024], F16)
        qz = sb("qz", [128, 2, 2, H, S], F16)
        KT = sb("KT", [128, 12288], F16)
        V = sb("V", [128, 2, 2, NCH, 1024], F16)
        WI1 = KT[:, 0:8192].rearrange("p (q n) -> p q n", q=2)
        flat = ST[:, :, :].rearrange("p a n -> p (a n)")
        P_ = flat[0:S, 0:2 * KV].rearrange("p (a n) -> p a n", a=2)
        SC = flat[0:S, 768:768 + 2 * KV].rearrange("p (a n) -> p a n", a=2)
        OB = flat[0:S, 1536:1536 + 1024]
        PT = flat[0:CHUNK, 2560:2560 + 2 * NCH * S].bitcast(F16)\
            .rearrange("p (a q c n) -> p a q c n", a=2, q=2, c=NCH)
        OT = flat[:, 3328:3328 + 8 * S].bitcast(F16).rearrange("p (q t n) -> p q t n", q=2, t=8)
        qu = flat[:, 4352:4352 + 4 * S].bitcast(F16).rearrange("p (a q t n) -> p a q t n", a=2, q=2, t=2)
        mask = sb("mask", [128, 8], F16)
        qflat = qz[:, :, :, :, :].rearrange("p a q h n -> p (a q h n)")
        hf = qflat[:, 0:8 * HT].bitcast(F32).rearrange("p (a n) -> p a n", a=HB)
        sg = qflat[:, 8 * HT:16 * HT].bitcast(F32).rearrange("p (a n) -> p a n", a=HB)
        identf = sb("identf", [128, 128])
        ones16 = sb("ones16", [1, 512], F16)
        os16 = sb("os16", [1, S], F16)
        zero16 = sb("zero16", [1, 128], F16)
        iota8 = sb("iota8", [S, E])
        nm = sb("nm", [S, 4])
        sums = sb("sums", [S, 2, H])
        rinv = sb("rinv", [S, H])
        tg = sb("tg", [S, 4])
        tgs = sb("tgs", [S, 4])
        lora_s = sb("lora_s", [128, 4])
        gc_b = sb("gc_b", [S, 1])
        stats = sb("stats", [S, B, 6])
        mv = sb("mv", [S, B, 2])
        lnc = sb("lnc", [S, LN_SMALL, B])
        lg = sb("lg", [S, B, E])
        m8 = sb("m8", [S, B, 8])
        i8 = sb("i8", [S, B, 8], U32)
        i8f = sb("i8f", [S, B, 8])
        oh = sb("oh", [S, 2, B, E])
        w12 = sb("w12", [S, 4, B])
        wd = sb("wd", [S, B, E])
        wdf = sb("wdf", [E, 2, HT])
        wdT = sb("wdT", [E, 2, T], F16)
        gam = sb("gam", [S, 4, C])
        b1 = sb("b1", [128, E, NM])
        bcur = sb("bcur", [128, 2, NM])
        KI = sb("KI", [128, 2, 8, B * IPA], F16)
        zi = sb("zi", [S, 3, H, IPA])
        pn = sb("pn", [S, 2, H, IPA])
        si = sb("si", [S, 3, H])
        eb2 = sb("eb2", [E, 2, C], F16)
        zz = sb("zz", [S, 3, B])

        pb = [ctx.enter_context(nc.psum_tensor(f"pb{i}", [128, 512], F32)) for i in range(8)]
        SB_, TB_, OBK, GB = pb[0:2], pb[2:4], pb[4:6], pb[6:8]

        wdB = ZA[:, :, :].rearrange("p b c -> p (b c)")[:, 0:2 * T].rearrange("p (a n) -> p a n", a=2)
        wd_dram = [nc.dram_tensor(f"wd_scratch{l}", [E, 2, HT], F32).ap() for l in range(2)]
        vi_dram = nc.dram_tensor("vi_scratch", [B * IPA, 2, 1024], F16).ap()

        kT = [[KT[:, (2 * p + q) * 3000:(2 * p + q + 1) * 3000].rearrange("p (t k) -> p t k", t=8)
               for q in range(2)] for p in range(2)]
        MW = KT[:, :].rearrange("p (u q n) -> p u q n", u=2, q=2)
        VF = V[:, :, :, :, :].rearrange("p a b c d -> p (a b c d)")
        HTt = VF[:, 0:2 * 2 * NM * HT].rearrange("p (u q m n) -> p u q m n", u=2, q=2, m=NM)

        AB = VF[0:S, 7168:7168 + 2 * B * C].bitcast(F32).rearrange("p (b c) -> p b c", b=B)
        junk = VF[0:S, 7168 - 2 * HB * C:7168].bitcast(F32).rearrange("p (b c) -> p b c", b=HB)
        KF = KT[:, :].rearrange("p (u n) -> p u n", u=4)
        BT = KF[:, 0, :].rearrange("p (q g k n) -> p q g k n", q=2, g=3, k=2)
        R16 = KF[:, 1, :].rearrange("p (q g k n) -> p q g k n", q=2, g=3, k=2)
        RT = KF[:, 2, :].rearrange("p (q g k n) -> p q g k n", q=2, g=3, k=2)
        RF = qflat[:, 8 * HT:8 * HT + 3072].bitcast(F32).rearrange("p (g k n) -> p g k n", g=3, k=2)
        eyes = VF[:, 11264:11264 + (DEG - 1) * 128].rearrange("p (t n) -> p t n", n=128)

        def w0(name, q, k):
            o, n = PA0[name]
            return W0[:, q, o + k * n:o + (k + 1) * n]

        def row(name, q):
            o, n = ROW[name]
            return RW[0:1, q, o:o + n]

        def bc(ap, shape):
            return ap.broadcast_to(shape)

        names = """x_in small_in ident_set const_set ones_set below_set eyes_set
            tanh_done lora_scale
            chunk_lora_mm chunk_added chunk_hi chunk_lo
            ln_stats ln_aggr ln_small ln_sqrt ln_norm ln_tmm ln_thi ln_tlo
            ipa_mm ipa_hi ipa_lo ipa_stored ipa_ctx ffn ffn_rest mix halves0 halves1""".split()
        s = {n: sem(n) for n in names}
        s["chunk_in"] = [sem(f"chunk_in{i}") for i in range(STAGES)]
        for L in range(2):
            for n in """s_mm clip_done mx_done exp_done t_mm hi_done lo_done pv_mm g_mm g_hi g_free
                    qz_done o_rd r_done x_up ipa_patch ipa_sc ipa_z ipa_m ipa_e ipa_s ipa_r ipa_pn vi_in""".split():
                s[f"{n}{L}"] = sem(f"{n}{L}")
            for n in """m_in0 m_in1 m_hi m_lo u_mm u_act u_wt u_hf u_hi u_lo d_mm wd_mm wd_act wd_lo wd_out
                    w_in0 w_in1 moved rt_mm rt_lg rt_m8 rt_i8 rt_sm rt_wd rt_act f_mm f_act f_dve""".split():
                s[f"{n}_{L}"] = sem(f"{n}_{L}")
        for n in "e_mm e_hi e_lo e_f e_in".split():
            s[n] = sem(n)

        layers = [Layer(0, 16), Layer(1, 64)]

        LD = VF[0:3 * RANK, 0:DOWN_N + UP_N]
        LO, at = {}, 0
        for factor, length in (("qd", C), ("kd", 256), ("vd", 256), ("od", 1024),
                               ("qu", 1024), ("ku", 1024), ("vu", 1024), ("ou", C)):
            LO[factor] = at
            at += length

        def lo_(name, c0, n):
            return LD[:, LO[name] + c0:LO[name] + c0 + n]

        chunks0 = [
            (128, PA0_N, a["pa0"], W0[:, 0, :], W0[:, 1, :], []),
            (128, 6 * C, a["kv0"], WKV0[:, 0:3, :].rearrange("p a n -> p (a n)"),
             [(slice(0, 128), 0, 2 * C, WKV0[:, 3, :]),
              (slice(K2, 128), 2 * C, 2 * C, WKV0[K2:128, 1, :]),
              (slice(K2 + 32, K2 + 33), 4 * C, 2 * C, WKV0[K2 + 32:K2 + 33, 2, :])], []),
            (1, ROWS, a["rows"], RW[:, 0, :], RW[:, 1, :], []),
            (E, C, a["eb2"], eb2[:, 0, :], eb2[:, 1, :], []),
        ]
        for k in range(2):
            for g in range(2):
                c0, c1 = g * 4 * KV, (g + 1) * 4 * KV
                low = slice(0, K2 if k else 128)
                chunks0.append((128, 4 * KV, a["ctxT"][k, :, c0:c1], cT[:, 0, k, c0:c1],
                                [(low, 0, 4 * KV, cT[low, 1, k, c0:c1])], []))
        half = UP_N // 2
        lora_cols = [(0, DOWN_N), (DOWN_N, half), (DOWN_N + half, half)]
        LORA_CHUNKS = len(lora_cols)
        chunks1 = []
        for j, (c0, w) in enumerate(lora_cols):
            rows = slice(2 * RANK, 3 * RANK) if j == 0 else slice(RANK, 2 * RANK)
            chunks1.append((3 * RANK, w, a["lora"][:, c0:c0 + w], LD[:, c0:c0 + w],
                            [(rows, b, w // 2, LD[rows, c0 + b:c0 + b + w // 2]) for b in (0, w // 2)], []))

        def context_cut(dst, j):
            hi = dst[:, 0, j * 2048:(j + 1) * 2048]
            return hi, [(slice(0, 128), 0, 1024, dst[:, 1, j * 2048:j * 2048 + 1024]),
                        (slice(K2, 128), 1024, 1024, hi[K2:128, 1024:2048])]

        for name, j, kk, cols, dn, up in [("q", 0, 256, 1024, "qd", "qu"), ("k", 1, 256, 1024, "kd", "ku"),
                                          ("v", 2, 256, 1024, "vd", "vu"), ("o", 3, 1024, C, "od", "ou")]:
            lora = []
            w = min(512, cols)
            parts = [(kt * cols + c0, lo_(dn, kt * 128, 128), lo_(up, c0, w))
                     for kt in range(kk // 128) for c0 in range(0, cols, w)]
            for n in range(0, len(parts), 512 // w):
                lora.append((parts[n][0], w, parts[n:n + 512 // w], j))
            hi = W1[:, 0, j * 2048:(j + 1) * 2048]
            hi, lo = context_cut(W1, j) if name in "kv" else \
                (hi, [(slice(0, 128), c, 1024, W1[:, 1, j * 2048 + c:j * 2048 + c + 1024]) for c in (0, 1024)])
            chunks1.append((128, 2048, a["w1" + name], hi, lo, lora))
        for j, name in enumerate(("ki", "vi")):
            chunks1.append((128, 2048, a["w1" + name], *context_cut(WI1, j), []))
        chunks = chunks0 + chunks1
        lora_before = [sum(len(c[5]) for c in chunks[:n]) for n in range(len(chunks) + 1)]

        def staged(n, c0, w):
            o = (n % STAGES) * CHUNK_N + c0
            return flat[0:chunks[n][0], o:o + w]

        def chunks_sync(sp, first, last):
            for n in range(first, last):
                if n >= STAGES:
                    sp.wait_ge(s["chunk_lo"], n - STAGES + 1)
                sp.dma_start(staged(n, 0, chunks[n][1]), chunks[n][2]).then_inc(s["chunk_in"][n % STAGES], 16)

        def chunk_arrived(eng, n):
            eng.wait_ge(s["chunk_in"][n % STAGES], 16 * (n // STAGES + 1))

        def lora_product(pe, n, j):
            c0, w, parts, _ = chunks[n][5][j]
            k = lora_before[n] + j
            if k == 0:
                pe.wait_ge(s["chunk_lo"], len(chunks0) + LORA_CHUNKS)
            if k >= 2:
                pe.wait_ge(s["chunk_added"], k - 1)
            for at, dn, up in parts:
                mm = pe.matmul(GB[k % 2][:, at - c0:at - c0 + w], dn, up, start=True, stop=True)
            mm.then_inc(s["chunk_lora_mm"], 1)

        def lora_add(dve, n, j):
            c0, w, parts, which = chunks[n][5][j]
            k = lora_before[n] + j
            if j == 0:
                chunk_arrived(dve, n)
            if k == 0:
                dve.wait_ge(s["lora_scale"], 3)
            dve.wait_ge(s["chunk_lora_mm"], k + 1)
            dve.scalar_tensor_tensor(staged(n, c0, 512), GB[k % 2][:, :], lora_s[:, which:which + 1],
                                     staged(n, c0, 512), ALU.mult, ALU.add).then_inc(s["chunk_added"], 1)

        def cut_hi(act, n):
            rows, cols, src, hi, lo, lora = chunks[n]
            chunk_arrived(act, n)
            if lora:
                act.wait_ge(s["chunk_added"], lora_before[n + 1])
            act.activation(hi, staged(n, 0, cols), ACT.Copy,
                           scale=WS if n not in plain else 1.0).then_inc(s["chunk_hi"], 1)

        def lo_pieces(n):
            rows, cols, src, hi, lo, lora = chunks[n]
            return lo if isinstance(lo, list) else [(slice(0, rows), 0, cols, lo)]

        def cut_lo(dve, n, j):
            part, c0, w, dst = lo_pieces(n)[j]
            if j == 0:
                dve.wait_ge(s["chunk_hi"], n + 1)
            x = dve.scalar_tensor_tensor(dst, staged(n, c0, w)[part], WS if n not in plain else 1.0,
                                         chunks[n][3][part, c0:c0 + w], ALU.mult, ALU.subtract)
            if j == len(lo_pieces(n)) - 1:
                x.then_inc(s["chunk_lo"], 1)

        def chunks_vector(dve, first, last):
            for n in range(first, last):
                for j in range(len(lo_pieces(n))):
                    cut_lo(dve, n, j)

        def chunks_scalar(act, first, last):
            for n in range(first, last):
                cut_hi(act, n)

        plain = set(range(4, 8))
        NC0, NC1 = len(chunks0), len(chunks)

        def norm_vector(dve, r, src, dst):
            st_, ag_, sm_, nn_ = s["ln_stats"], s["ln_aggr"], s["ln_small"], s["ln_norm"]
            if r:
                dve.wait_ge(nn_, B * r)
            for b in range(B):
                dve.bn_stats(stats[:, b, :], src[:, b, :]).then_inc(st_, 1)
            dve.wait_ge(st_, B * (r + 1))
            for b in range(B):
                dve.bn_aggr(mv[:, b, :], stats[:, b, :]).then_inc(ag_, 1)
            dve.wait_ge(ag_, B * (r + 1))
            k = 6 * r
            dve.tensor_scalar(lnc[:, 0, :], mv[:, :, 1], EPS, None, ALU.add).then_inc(sm_, 1)
            dve.wait_ge(s["ln_sqrt"], r + 1)
            dve.reciprocal(lnc[:, 2, :], lnc[:, 1, :]).then_inc(sm_, 1)
            dve.wait_ge(sm_, k + 2)
            dve.tensor_tensor(lnc[:, 3, :], lnc[:, 2, :], lnc[:, 2, :], ALU.mult).then_inc(sm_, 1)
            dve.wait_ge(sm_, k + 3)
            dve.tensor_tensor(lnc[:, 4, :], lnc[:, 3, :], lnc[:, 0, :], ALU.mult).then_inc(sm_, 1)
            dve.wait_ge(sm_, k + 4)
            dve.tensor_scalar(lnc[:, 5, :], lnc[:, 4, :], -0.5, 1.5, ALU.mult, ALU.add).then_inc(sm_, 1)
            dve.wait_ge(sm_, k + 5)
            dve.tensor_tensor(lnc[:, 6, :], lnc[:, 5, :], lnc[:, 2, :], ALU.mult).then_inc(sm_, 1)
            dve.wait_ge(sm_, k + 6)
            for b in range(B):
                dve.tensor_scalar(dst[:, b, :], src[:, b, :], mv[:, b, 0:1], lnc[:, 6, b:b + 1],
                                  ALU.subtract, ALU.mult).then_inc(nn_, 1)

        def norm_scalar(act, r):
            act.wait_ge(s["ln_small"], 6 * r + 1)
            act.activation(lnc[:, 1, :], lnc[:, 0, :], ACT.Sqrt).then_inc(s["ln_sqrt"], 1)

        GROUPS = [(k, g) for g in range(2) for k in range(2)]

        def turn_tensor(pe, r, src, ready):
            for n, (k, g) in enumerate(GROUPS):
                i = 4 * r + n
                if k == 0:
                    pe.wait_ge(*ready[g])
                if i >= 2:
                    pe.wait_ge(s["ln_tlo"], i - 1)
                for j in range(4):
                    mm = pe.transpose(GB[i % 2][:, j * S:(j + 1) * S], src[:, 4 * g + j, k * 128:(k + 1) * 128],
                                      identf[0:S, 0:S])
                mm.then_inc(s["ln_tmm"], 1)

        def halves_of(use):
            return [(s["ln_norm"], B * use + B // 2), (s["ln_norm"], B * use + B)]

        def turn_scalar(act, r):
            for n, (k, g) in enumerate(GROUPS):
                i = 4 * r + n
                act.wait_ge(s["ln_tmm"], i + 1 - (4 if r > 2 else 0))
                act.activation(xT[:, 0, k, g * HT:(g + 1) * HT], GB[i % 2][:, 0:HT], ACT.Copy)\
                   .then_inc(s["ln_thi"], 1)

        def turn_vector(dve, r):
            for n, (k, g) in enumerate(GROUPS):
                i = 4 * r + n
                dve.wait_ge(s["ln_thi"], i + 1)
                dve.scalar_tensor_tensor(xT[:, 1, k, g * HT:(g + 1) * HT], GB[i % 2][:, 0:HT], 1.0,
                                         xT[:, 0, k, g * HT:(g + 1) * HT], ALU.mult, ALU.subtract)\
                   .then_inc(s["ln_tlo"], 1)

        def psum_out(L, group, h):
            c = (h % L.grouped) * 2 * L.dim
            return OBK[group % 2][0:S, c:c + 2 * L.dim].rearrange("p (q d) -> p q d", q=2)

        def counts(L):
            F, U = len(L.front), len(L.front) + len(L.out)
            hiF = sum(acts(u) for u in L.front)
            hiU = hiF + sum(acts(u) for u in L.out)
            return F, U, hiF, hiU

        def unit_numbers(L, where, bv, bs):
            F, U, hiF, hiU = counts(L)
            if where == "first":
                kinds, n0, s0, h0 = ("front",), F, F, hiF
            elif where == "last":
                kinds, n0, h0 = ("out",), 2 * F + (bv - 1) * U, 2 * hiF + (bv - 1) * hiU
                s0 = 2 * F + (bs - 1) * U
            else:
                kinds, n0, h0 = ("front", "out"), 2 * F + (bv - 1) * U, 2 * hiF + (bv - 1) * hiU
                s0 = 2 * F + (bs - 1) * U
            found, done = [], 0
            for h, kind, u, n in L.units(kinds):
                found.append((h, kind, u, n0 + n, s0 + n, h0 + done))
                done += acts(u)
            return found

        def prologue_units(L):
            found, done = [], 0
            for n, u in enumerate(L.front):
                found.append((0, "front", u, n, n, done))
                done += acts(u)
            return found

        def tail_units(L):
            F, U, hiF, hiU = counts(L)
            n0, h0 = 2 * F + (B - 2) * U + len(L.out), 2 * hiF + (B - 2) * hiU + (hiU - hiF)
            found, done = [], 0
            for n, u in enumerate(L.out):
                found.append((0, "out", u, n0 + n, n0 + n, h0 + done))
                done += acts(u)
            return found

        def front_done(L, bv, bs, which):
            F, U, _, _ = counts(L)
            last = {"q": len(L.q_units), "k": len(L.q_units) + len(L.k_units),
                    "i": len(L.q_units) + len(L.k_units) + len(L.i_units), "v": len(L.front)}[which]
            if isinstance(bs, int) and bs == 0:
                return last
            if bs == 1 and isinstance(bv, int):
                return F + last
            number = {("front", u) if kind == "front" else ("out", u): n
                      for _, kind, u, n in L.units(("front", "out"))}
            u = L.front[last - 1]
            inner = number[("front", u)] + 1
            return 2 * F + (bv - 2) * U + inner

        def context_products(w, j, cols, tokens):
            if w is WKV0:
                at = [w[:, n, j * C:(j + 1) * C][:, cols] for n in range(4)]
            else:
                first, second = (w[:, q, j * 2048:(j + 1) * 2048] for q in range(2))
                at = [first[:, 0:1024][:, cols], first[:, 1024:2048][:, cols], first[:, 1024:2048][:, cols],
                      second[:, 0:1024][:, cols]]
            return [(at[0], tokens(0, 0)), (at[0], tokens(1, 0)), (at[3], tokens(0, 0)),
                    (at[1], tokens(0, 1)), (at[2], tokens(1, 1))]

        def attention_tensor(pe, L):
            l = L.index
            g_mm, g_free = s[f"g_mm{l}"], s[f"g_free{l}"]
            kv, kj = (WKV0, 0) if l == 0 else (W1, 1)

            def wq(q, k, t):
                return w0("Wq", q, k)[:, t * 128:(t + 1) * 128] if l == 0 else \
                    W1[:, q, k * 1024 + t * 128:k * 1024 + (t + 1) * 128]

            def wo(q, t):
                return w0("Wo", q, t) if l == 0 else W1[:, q, 6144 + t * C:6144 + (t + 1) * C]

            def unit(kind, u, n, ns, bv, bs, behind=1):
                bank = GB[ns % 2]
                if ns >= 2:
                    pe.wait_ge(g_free, n - 1)
                if u[0] == "q":
                    for t in range(L.qt):
                        i = 0
                        for k in range(2):
                            for qa, qb in PARTS:
                                mm = pe.matmul(bank[:, t * S:(t + 1) * S], wq(qa, k, u[1] * 4 + t),
                                               xT[:, qb, k, bass.ds(bv * S, S)], start=(i == 0),
                                               stop=(i == 5 and l == 1))
                                i += 1
                        if l == 0:
                            for q in range(2):
                                mm = pe.matmul(bank[:, t * S:(t + 1) * S], row("bq", q)[:, t * 128:(t + 1) * 128],
                                               ones16[:, 0:S], start=False, stop=(q == 1))
                elif u[0] == "k":
                    pairs = context_products(kv, kj, slice(u[1] * 128, (u[1] + 1) * 128),
                                             lambda q, k: cT[:, q, k, bass.ds(bv * KV, L.keys)])
                    for i, (w, c) in enumerate(pairs):
                        mm = pe.matmul(bank[:, 0:L.keys], w, c, start=(i == 0), stop=(i == 4))
                elif u[0] == "v":
                    m = min(CHUNK, L.keys - u[1] * CHUNK)
                    pairs = context_products(kv, kj + 1, slice(u[2] * L.vw, (u[2] + 1) * L.vw),
                                             lambda q, k: cT[:, q, k, bass.ds(bv * KV + u[1] * CHUNK, m)])
                    for i, (w, c) in enumerate(pairs):
                        mm = pe.matmul(bank[0:m, 0:L.vw], c, w, start=(i == 0), stop=(i == 4))
                elif u[0] == "i":
                    pe.wait_ge(g_free, front_done(L, bv, bs, "q"))
                    for h in range(H):
                        dst = bank[0:S, h * 2 * IPA:(h + 1) * 2 * IPA].rearrange("p (q j) -> p q j", q=2)
                        for qa in range(2):
                            mm = pe.matmul(dst, qz[:, bs % 2, qa, h, :], KI[:, :, h // 2, bass.ds(bv * IPA, IPA)],
                                           start=(qa == 0), stop=(qa == 1))
                elif u[0] == "t":
                    if u[1] == 0:
                        pe.wait_ge(s[f"o_rd{l}"], (bv + 1) * L.groups)
                    for j in range(L.qt):
                        c0 = (u[1] * 4 + j) * 128
                        mm = pe.transpose(bank[:, j * S:(j + 1) * S], OB[:, c0:c0 + 128], identf[0:S, 0:S])
                else:
                    pe.wait_ge(g_free, n - behind + 1)
                    i, last = 0, 3 * L.tiles - 1
                    for t in range(L.tiles):
                        for qa, qb in PARTS:
                            pe.matmul(bank[0:S, 0:C], OT[:, qa, t, :], wo(qb, t), start=(i == 0), stop=False)
                            i += 1
                    for q in range(2):
                        mm = pe.matmul(bank[0:S, 0:C], (os16 if l else ones16)[:, 0:S], row(f"bo{l}", q), start=False, stop=(q == 1))
                mm.then_inc(g_mm, 1)

            def scores(bv, bs, h):
                i, st = bv * H + h, bs * H + h
                if h == 0:
                    pe.wait_ge(g_free, front_done(L, bv, bs, "k"))
                    if l == 0:
                        pe.wait_ge(s["qz_done0"], 4 * bv + 4)
                if st >= 2:
                    pe.wait_ge(s["mx_done0"] if l == 0 else s["exp_done1"], i - 1)
                for n, (qa, qb) in enumerate(PARTS):
                    mm = pe.matmul(SB_[st % 2][0:S, 0:L.keys], qz[:, bs % 2, qa, h, :],
                                   kT[bs % 2][qb][:, h // L.per_tile, 0:L.keys], start=(n == 0), stop=(n == 2))
                mm.then_inc(s[f"s_mm{l}"], 1)

            def turn(i, st):
                pe.wait_ge(s["exp_done0"] if l == 0 else s["ipa_patch1"], i + 1)
                if st >= 2:
                    pe.wait_ge(s[f"lo_done{l}"], i - 1)
                for c in range(NCH):
                    mm = pe.transpose(TB_[st % 2][0:CHUNK, c * S:(c + 1) * S],
                                      P_[:, st % 2, c * CHUNK:(c + 1) * CHUNK], identf[0:S, 0:S])
                mm.then_inc(s[f"t_mm{l}"], 1)

            def weigh(bv, bs, h):
                i, st = bv * H + h, bs * H + h
                if h == 0:
                    pe.wait_ge(g_free, front_done(L, bv, bs, "v"))
                    if l == 1:
                        pe.wait_ge(s[f"vi_in{bs % 2}"], (bv - bs % 2) * 16 + 32)
                group, gs = bv * L.groups + h // L.grouped, bs * L.groups + h // L.grouped
                if h % L.grouped == 0 and gs >= 2:
                    pe.wait_ge(s[f"o_rd{l}"], group - 1)
                pe.wait_ge(s[f"lo_done{l}"], i + 1)
                for c in range(NCH):
                    for qa in range(2):
                        mm = pe.matmul(psum_out(L, gs, h), PT[:, st % 2, qa, c, :],
                                       V[0:CHUNK, bs % 2, :, c, h * L.dim:(h + 1) * L.dim],
                                       start=(c == 0 and qa == 0), stop=(c == NCH - 1 and qa == 1))
                mm.then_inc(s[f"pv_mm{l}"], 1)

            def batch(where, bv, bs):
                todo = unit_numbers(L, where, bv, bs)
                at = {u: ns for _, kind, u, n, ns, _ in todo if kind == "out"}
                behind = at[L.out[-1]] - at[L.out[-2]] if at else 1
                for h in range(H):
                    scores(bv, bs, h)
                    if bs or h >= 2:
                        turn(bv * H + h - 2, bs * H + h - 2)
                    if bs or h >= 3:
                        if h >= 3:
                            weigh(bv, bs, h - 3)
                        else:
                            weigh(bv - 1, bs - 1, H + h - 3)
                    for hh, kind, u, n, ns, _ in todo:
                        if hh == h:
                            d = 1 if kind == "front" else -1
                            unit(kind, u, n, ns, bv + d, bs + d, behind)

            for _, kind, u, n, ns, _ in prologue_units(L):
                unit(kind, u, n, ns, 0, 0)
            batch("first", 0, 0)
            with pe.Fori(0, (B - 2) // 2) as r:
                b = r * 2 + 1
                batch("middle", b, 1)
                batch("middle", b + 1, 2)
            batch("last", B - 1, B - 1)
            for i in range(B * H - 2, B * H):
                turn(i, i)
                weigh(B - 1, B - 1, i - 1 - (B - 1) * H)
            weigh(B - 1, B - 1, H - 1)
            for _, kind, u, n, ns, _ in tail_units(L):
                unit(kind, u, n, ns, B - 1, B - 1)

        QSCALE = {0: -0.25 / WS, 1: 0.125 / WS}

        def q_cuts(L, u, bs):
            for side in range(2):
                r = slice(64 * side, 64 * side + 64)
                h0 = 8 * u[1] + side
                yield (r, lambda q, r=r, h0=h0: qz[r, bs % 2, q, h0:h0 + 7:2, :])

        def attention_scalar(act, L):
            l = L.index
            g_mm, g_hi = s[f"g_mm{l}"], s[f"g_hi{l}"]

            def unit(kind, u, n, ns, bv, bs):
                if not acts(u):
                    return
                bank = GB[ns % 2]
                act.wait_ge(g_mm, n + 1)
                if u[0] == "q" and l == 0:
                    act.activation(qu[:, bs % 2, 0, :, :], bank[:, 0:2 * S].rearrange("p (t n) -> p t n", t=2),
                                   ACT.Copy, scale=QSCALE[0]).then_inc(g_hi, 1)
                elif u[0] == "q":
                    for side, (r, dst) in enumerate(q_cuts(L, u, bs)):
                        x = act.activation(dst(0), bank[r, 0:4 * S].rearrange("p (t n) -> p t n", t=4),
                                           ACT.Copy, scale=QSCALE[1])
                        if side:
                            x.then_inc(g_hi, 1)
                elif u[0] == "k":
                    act.activation(kT[bs % 2][0][:, u[1], 0:L.keys], bank[:, 0:L.keys], ACT.Copy,
                                   scale=1.0 / WS).then_inc(g_hi, 1)
                elif u[0] == "v":
                    m = min(CHUNK, L.keys - u[1] * CHUNK)
                    act.activation(V[0:m, bs % 2, 0, u[1], u[2] * 512:u[2] * 512 + L.vw], bank[0:m, 0:L.vw],
                                   ACT.Copy, scale=1.0 / WS).then_inc(g_hi, 1)
                else:
                    g = u[1]
                    act.activation(OT[:, 0, g * L.qt:(g + 1) * L.qt, :],
                                   bank[:, 0:L.qt * S].rearrange("p (t n) -> p t n", t=L.qt), ACT.Copy)\
                       .then_inc(g_hi, 1)

            def exps(bv, bs, h):
                i, st = bv * H + h, bs * H + h
                act.wait_ge(s["mx_done1"] if l else s["clip_done0"], i + 1)
                if st >= 2:
                    act.wait_ge(s[f"t_mm{l}"], i - 1)
                if h == 0 and bs >= 2:
                    act.wait_ge(s[f"o_rd{l}"], (bv - 1) * L.groups)
                src = SC[:, st % 2, :] if l == 0 else SB_[st % 2][0:S, 0:L.keys]
                act.activation(P_[:, st % 2, 0:L.keys], src, ACT.Exp, bias=nm[:, st % 4:st % 4 + 1],
                               scale=1.0 if l else -1.0,
                               accum_out=sums[:, bs % 2, h:h + 1]).then_inc(s[f"exp_done{l}"], 1)

            def hi(i, st):
                act.wait_ge(s[f"t_mm{l}"], i + 1)
                if st >= 2:
                    act.wait_ge(s[f"pv_mm{l}"], i - 1)
                act.activation(PT[:, st % 2, 0, :, :], TB_[st % 2][0:CHUNK, 0:NCH * S]
                               .rearrange("p (c n) -> p c n", c=NCH), ACT.Copy).then_inc(s[f"hi_done{l}"], 1)

            def ipa_exp(bv, bs):
                act.wait_ge(s["ipa_z1"], bv + 1)
                act.activation(zi[:, 1, :, :], zi[:, 0, :, :], ACT.Exp).then_inc(s["ipa_e1"], 1)

            def batch(where, bv, bs):
                todo = unit_numbers(L, where, bv, bs)
                for h in range(H):
                    if bs or h >= 2:
                        hi(bv * H + h - 2, bs * H + h - 2)
                    exps(bv, bs, h)
                    for hh, kind, u, n, ns, nh in todo:
                        if hh == h:
                            d = 1 if kind == "front" else -1
                            unit(kind, u, n, ns, bv + d, bs + d)
                            if u[0] == "i":
                                ipa_exp(bv + d, bs + d)

            for _, kind, u, n, ns, nh in prologue_units(L):
                unit(kind, u, n, ns, 0, 0)
                if u[0] == "i":
                    ipa_exp(0, 0)
            batch("first", 0, 0)
            with act.Fori(0, (B - 2) // 2) as r:
                b = r * 2 + 1
                batch("middle", b, 1)
                batch("middle", b + 1, 2)
            batch("last", B - 1, B - 1)
            for i in range(B * H - 2, B * H):
                hi(i, i)
            for _, kind, u, n, ns, nh in tail_units(L):
                unit(kind, u, n, ns, B - 1, B - 1)

        def attention_vector(dve, L):
            l = L.index
            g_mm, g_hi, g_free = s[f"g_mm{l}"], s[f"g_hi{l}"], s[f"g_free{l}"]
            step = ALU.mult, ALU.subtract

            def unit(kind, u, n, ns, nh, bv, bs):
                bank = GB[ns % 2]
                if acts(u):
                    dve.wait_ge(g_hi, nh + 1)
                else:
                    dve.wait_ge(g_mm, n + 1)
                if u[0] == "q" and l == 0:
                    x = dve.scalar_tensor_tensor(qu[:, bs % 2, 1, :, :],
                                                 bank[:, 0:2 * S].rearrange("p (t n) -> p t n", t=2), QSCALE[0],
                                                 qu[:, bs % 2, 0, :, :], *step)
                elif u[0] == "q":
                    for r, dst in q_cuts(L, u, bs):
                        x = dve.scalar_tensor_tensor(dst(1), bank[r, 0:4 * S].rearrange("p (t n) -> p t n", t=4),
                                                     QSCALE[1], dst(0), *step)
                elif u[0] == "k":
                    x = dve.scalar_tensor_tensor(kT[bs % 2][1][:, u[1], 0:L.keys], bank[:, 0:L.keys], 1.0 / WS,
                                                 kT[bs % 2][0][:, u[1], 0:L.keys], *step)
                elif u[0] == "v":
                    m = min(CHUNK, L.keys - u[1] * CHUNK)
                    c = slice(u[2] * 512, u[2] * 512 + L.vw)
                    x = dve.scalar_tensor_tensor(V[0:m, bs % 2, 1, u[1], c], bank[0:m, 0:L.vw], 1.0 / WS,
                                                 V[0:m, bs % 2, 0, u[1], c], *step)
                elif u[0] == "t":
                    t = slice(u[1] * L.qt, (u[1] + 1) * L.qt)
                    x = dve.scalar_tensor_tensor(OT[:, 1, t, :],
                                                 bank[:, 0:L.qt * S].rearrange("p (t n) -> p t n", t=L.qt), 1.0,
                                                 OT[:, 0, t, :], *step)
                elif u[0] == "o":
                    xb = X[:, bass.ds(bv, 1), :]
                    x = dve.scalar_tensor_tensor(xb, bank[0:S, 0:C].rearrange("p (a n) -> p a n", a=1),
                                                 tgs[:, l:l + 1], xb, ALU.mult, ALU.add)
                else:
                    sc = zi[:, 2, :, :]
                    if bs >= 1:
                        dve.wait_ge(s["ipa_pn1"], bv)
                    dve.tensor_reduce(sc, bank[0:S, 0:H * 2 * IPA].rearrange("p (h q j) -> p h j q", h=H, q=2),
                                      AX.X, ALU.add).then_inc(s["ipa_sc1"], 1)
                    dve.wait_ge(s["ipa_sc1"], bv + 1)
                    dve.tensor_reduce(si[:, 0, :], sc, AX.X, ALU.max).then_inc(s["ipa_m1"], 1)
                    dve.wait_ge(s["ipa_m1"], bv + 1)
                    dve.tensor_tensor(zi[:, 0, :, :], sc, bc(si[:, 0, :].unsqueeze(2), [S, H, IPA]),
                                      ALU.subtract).then_inc(s["ipa_z1"], 1)
                    dve.wait_ge(s["ipa_z1"], bv + 1)
                    x = dve.tensor_copy(si[:, 0, 0:1], si[:, 0, 1:2])
                x.then_inc(g_free, 1)

            def ipa_rest(bv, bs):
                dve.wait_ge(s["ipa_e1"], bv + 1)
                dve.tensor_reduce(si[:, 1, :], zi[:, 1, :, :], AX.X, ALU.add).then_inc(s["ipa_s1"], 1)
                dve.wait_ge(s["ipa_s1"], bv + 1)
                dve.reciprocal(si[:, 2, :], si[:, 1, :]).then_inc(s["ipa_r1"], 1)
                dve.wait_ge(s["ipa_r1"], bv + 1)
                if bs >= 2:
                    dve.wait_ge(s["ipa_patch1"], (bv - 1) * H)
                dve.tensor_tensor(pn[:, bs % 2, :, :], zi[:, 1, :, :], bc(si[:, 2, :].unsqueeze(2), [S, H, IPA]),
                                  ALU.mult).then_inc(s["ipa_pn1"], 1)

            def maxima(bv, bs, h):
                i, st = bv * H + h, bs * H + h
                dve.wait_ge(s[f"s_mm{l}"], i + 1)
                src = SB_[st % 2][0:S, 0:L.keys]
                if l == 0:
                    if st >= 2:
                        dve.wait_ge(s["exp_done0"], i - 1)
                    dve.tensor_scalar(SC[:, st % 2, :], src, -CLAMP, CLAMP, ALU.max, ALU.min,
                                      accum_out=nm[:, st % 4:st % 4 + 1]).then_inc(s["mx_done0"], 1)
                    dve.wait_ge(s["mx_done0"], i + 1)
                    dve.tensor_scalar(SC[:, st % 2, :], SC[:, st % 2, :], CLAMP, None, ALU.min)\
                       .then_inc(s["clip_done0"], 1)
                    return
                dve.tensor_reduce(nm[:, st % 4:st % 4 + 1], src, AX.X, ALU.max, negate=True)\
                   .then_inc(s[f"mx_done{l}"], 1)

            def lo(i, st):
                dve.wait_ge(s[f"hi_done{l}"], i + 1)
                dve.scalar_tensor_tensor(PT[:, st % 2, 1, :, :], TB_[st % 2][0:CHUNK, 0:NCH * S]
                                         .rearrange("p (c n) -> p c n", c=NCH), 1.0, PT[:, st % 2, 0, :, :],
                                         *step).then_inc(s[f"lo_done{l}"], 1)

            def normalise(bv, bs, g):
                group, gs = bv * L.groups + g, bs * L.groups + g
                heads = slice(g * L.grouped, (g + 1) * L.grouped)
                dve.wait_ge(s[f"pv_mm{l}"], bv * H + (g + 1) * L.grouped)
                if gs >= 1:
                    dve.wait_ge(s[f"o_rd{l}"], group)
                dve.reciprocal(rinv[:, heads], sums[:, bs % 2, heads]).then_inc(s[f"r_done{l}"], 1)
                halves = OBK[gs % 2][0:S, :].rearrange("p (h q d) -> p h q d", h=L.grouped, q=2)
                ob = OB[:, g * 256:(g + 1) * 256].rearrange("p (h d) -> p h d", h=L.grouped)
                dve.tensor_copy(ob, halves[:, :, 0, :]).then_inc(s[f"halves{l}"], 1)
                dve.wait_ge(s[f"halves{l}"], 2 * group + 1)
                dve.tensor_tensor(ob, ob, halves[:, :, 1, :], ALU.add).then_inc(s[f"halves{l}"], 1)
                dve.wait_ge(s[f"halves{l}"], 2 * group + 2)
                dve.wait_ge(s[f"r_done{l}"], group + 1)
                dve.scalar_tensor_tensor(ob, ob, OS if l else 1.0,
                                         bc(rinv[:, heads].unsqueeze(2), [S, L.grouped, L.dim]),
                                         ALU.mult, ALU.mult).then_inc(s[f"o_rd{l}"], 1)

            def batch(where, bv, bs):
                todo = unit_numbers(L, where, bv, bs)
                for h in range(H):
                    maxima(bv, bs, h)
                    if bs or h >= 2:
                        lo(bv * H + h - 2, bs * H + h - 2)
                    for g in range(L.groups):
                        at = (g + 1) * L.grouped + NORM_LAG[l]
                        if at == h:
                            normalise(bv, bs, g)
                        elif at == h + H and bs:
                            normalise(bv - 1, bs - 1, g)
                    for hh, kind, u, n, ns, nh in todo:
                        if hh == h:
                            d = 1 if kind == "front" else -1
                            unit(kind, u, n, ns, nh, bv + d, bs + d)
                            if u[0] == "i":
                                ipa_rest(bv + d, bs + d)

            for _, kind, u, n, ns, nh in prologue_units(L):
                unit(kind, u, n, ns, nh, 0, 0)
                if u[0] == "i":
                    ipa_rest(0, 0)
            batch("first", 0, 0)
            with dve.Fori(0, (B - 2) // 2) as r:
                b = r * 2 + 1
                batch("middle", b, 1)
                batch("middle", b + 1, 2)
            batch("last", B - 1, B - 1)
            for i in range(B * H - 2, B * H):
                lo(i, i)
            normalise(B - 1, B - 1, L.groups - 1)
            for _, kind, u, n, ns, nh in tail_units(L):
                unit(kind, u, n, ns, nh, B - 1, B - 1)

        def attention_gpsimd(pool, L):
            l = L.index
            if l == 0:
                def masks(bv, bs):
                    pool.wait_ge(s["g_free0"], front_done(L, bv, bs, "q"))
                    for q in range(2):
                        for t in range(2):
                            pool.tensor_tensor(qz[:, bs % 2, q, 8 * t:8 * t + 8, :],
                                               bc(qu[:, bs % 2, q, t, :].unsqueeze(1), [128, 8, S]),
                                               bc(mask[:, :].unsqueeze(2), [128, 8, S]), ALU.mult)\
                                .then_inc(s["qz_done0"], 1)
                masks(0, 0)
                masks(1, 1)
                with pool.Fori(1, B // 2) as r:
                    b = r * 2
                    masks(b, 2)
                    masks(b + 1, 3)
                return

            def patches(bv, bs):
                pool.wait_ge(s["ipa_pn1"], bv + 1)
                for h in range(H):
                    i, st = bv * H + h, bs * H + h
                    pool.wait_ge(s["exp_done1"], i + 1)
                    pool.tensor_tensor(P_[:, st % 2, ORG:KV], pn[:, bs % 2, h, :],
                                       bc(sums[:, bs % 2, h:h + 1], [S, IPA]), ALU.mult)\
                        .then_inc(s["ipa_patch1"], 1)
            patches(0, 0)
            with pool.Fori(0, (B - 2) // 2) as r:
                b = r * 2 + 1
                patches(b, 1)
                patches(b + 1, 2)
            patches(B - 1, B - 1)

        def attention_sync(sp, L):
            for b in range(B):
                if b >= 2:
                    sp.wait_ge(s["pv_mm1"], (b - 1) * H)
                for q in range(2):
                    sp.dma_start(V[CHUNK - IPA:CHUNK, b % 2, q, NCH - 1, :],
                                 vi_dram[b * IPA:(b + 1) * IPA, q, :]).then_inc(s[f"vi_in{b % 2}"], 16)

        cI = [[cT[:, q, k, :].rearrange("p (b n) -> p b n", b=B)[:, :, ORG:KV] for k in range(2)] for q in range(2)]
        vi_sb = flat[0:B * IPA, 4352:4864].bitcast(F16)
        vi_sb2 = flat[0:B * IPA, 4864:5376].bitcast(F16)
        ci_sb = KT[:, 8192:8192 + 4 * B * IPA].rearrange("p (q k n) -> p q k n", q=2, k=2)

        def ipa_tensor(pe):
            for t in range(8):
                pairs = context_products(WI1, 0, slice(t * 128, (t + 1) * 128), lambda q, k: ci_sb[:, q, k, :])
                for i, (w, c) in enumerate(pairs):
                    mm = pe.matmul(GB[0][:, t * B * IPA:(t + 1) * B * IPA], w, c, start=(i == 0), stop=(i == 4))
            mm.then_inc(s["ipa_mm"], 1)
            for w in range(2):
                if w:
                    pe.wait_ge(s["ipa_lo"], 1)
                pairs = context_products(WI1, 1, slice(w * 512, (w + 1) * 512), lambda q, k: ci_sb[:, q, k, :])
                for i, (weight, c) in enumerate(pairs):
                    mm = pe.matmul(GB[1 - w][0:B * IPA, :], c, weight, start=(i == 0), stop=(i == 4))
                mm.then_inc(s["ipa_mm"], 1)

        def ipa_scalar(act):
            act.wait_ge(s["ipa_mm"], 1)
            act.activation(KI[:, 0, :, :].rearrange("p t n -> p (t n)"), GB[0][:, 0:8 * B * IPA], ACT.Copy,
                           scale=1.0 / WS).then_inc(s["ipa_hi"], 1)
            for w in range(2):
                act.wait_ge(s["ipa_mm"], 2 + w)
                act.activation(vi_sb[:, w * 512:(w + 1) * 512], GB[1 - w][0:B * IPA, :], ACT.Copy, scale=1.0 / WS)\
                   .then_inc(s["ipa_hi"], 1)

        def ipa_vector(dve):
            dve.wait_ge(s["ipa_hi"], 1)
            dve.scalar_tensor_tensor(KI[:, 1, :, :].rearrange("p t n -> p (t n)"), GB[0][:, 0:8 * B * IPA], 1.0 / WS,
                                     KI[:, 0, :, :].rearrange("p t n -> p (t n)"),
                                     ALU.mult, ALU.subtract).then_inc(s["ipa_lo"], 1)
            for w in range(2):
                dve.wait_ge(s["ipa_hi"], 2 + w)
                dve.scalar_tensor_tensor(vi_sb2[:, w * 512:(w + 1) * 512], GB[1 - w][0:B * IPA, :], 1.0 / WS,
                                         vi_sb[:, w * 512:(w + 1) * 512], ALU.mult, ALU.subtract)\
                   .then_inc(s["ipa_lo"], 1)

        def router_tensor(pe, l, turned):
            name, bias = ("gate", "gate_b") if l == 0 else ("router1", "rb")
            pe.wait_ge(s["ln_tlo"], turned)
            for b in range(B):
                dst = pb[4][0:S, b * E:(b + 1) * E]
                i = 0
                for k in range(2):
                    for qa, qb in PARTS:
                        pe.matmul(dst, xT[:, qa, k, b * S:(b + 1) * S], w0(name, qb, k), start=(i == 0), stop=False)
                        i += 1
                for q in range(2):
                    mm = pe.matmul(dst, ones16[:, 0:S], row(bias, q), start=False, stop=(q == 1))
            mm.then_inc(s[f"rt_mm_{l}"], 1)

        def router_scalar(act, l):
            if l == 0:
                act.wait_ge(s["rt_sm_0"], 1)
                act.activation(w12[:, 0, :], w12[:, 2, :], ACT.Sigmoid).then_inc(s["rt_act_0"], 1)
            else:
                act.wait_ge(s["rt_mm_1"], 1)
                act.activation(lg[:, :, :], pb[4][0:S, 0:B * E].rearrange("p (b e) -> p b e", b=B), ACT.Sigmoid,
                               scale=1.0 / WS).then_inc(s["rt_lg_1"], 1)

        def router_vector(dve, l):
            sm, n = s[f"rt_sm_{l}"], 0
            if l == 0:
                dve.wait_ge(s["rt_mm_0"], 1)
                dve.tensor_scalar(lg[:, :, :], pb[4][0:S, 0:B * E].rearrange("p (b e) -> p b e", b=B), 1.0 / WS,
                                  None, ALU.mult).then_inc(s["rt_lg_0"], 1)
            dve.wait_ge(s[f"rt_lg_{l}"], 1)
            for b in range(B):
                dve.max(m8[:, b, :], lg[:, b, :]).then_inc(s[f"rt_m8_{l}"], 1)
            for b in range(B):
                dve.wait_ge(s[f"rt_m8_{l}"], b + 1)
                dve.max_index(i8[:, b, :], m8[:, b, :], lg[:, b, :]).then_inc(s[f"rt_i8_{l}"], 1)
            dve.wait_ge(s[f"rt_i8_{l}"], B)
            if l == 0:
                dve.tensor_tensor(w12[:, 2, :], m8[:, :, 0], m8[:, :, 1], ALU.subtract).then_inc(sm, 1)
            else:
                dve.tensor_copy(w12[:, 0, :], m8[:, :, 0]).then_inc(sm, 1)
            dve.tensor_copy(i8f[:, :, :], i8[:, :, :]).then_inc(sm, 1)
            dve.wait_ge(sm, 2)
            for j in range(2):
                dve.tensor_tensor(oh[:, j, :, :], bc(iota8[:, :].unsqueeze(1), [S, B, E]),
                                  bc(i8f[:, :, j:j + 1], [S, B, E]), ALU.is_equal).then_inc(sm, 1)
            if l == 0:
                dve.wait_ge(s["rt_act_0"], 1)
                dve.tensor_scalar(w12[:, 1, :], w12[:, 0, :], -1.0, 1.0, ALU.mult, ALU.add).then_inc(sm, 1)
            else:
                dve.tensor_copy(w12[:, 1, :], m8[:, :, 1]).then_inc(sm, 1)
            dve.wait_ge(sm, 5)
            for j in range(2):
                dve.tensor_tensor(oh[:, j, :, :], oh[:, j, :, :], bc(w12[:, j, :].unsqueeze(2), [S, B, E]),
                                  ALU.mult).then_inc(sm, 1)
            dve.wait_ge(sm, 7)
            dve.tensor_tensor(wd[:, :, :], oh[:, 0, :, :], oh[:, 1, :, :], ALU.add).then_inc(s[f"rt_wd_{l}"], 1)

        def expert_order(e, first, last_split):
            todo = [("up", 0, 0)]
            if not last_split:
                todo.append(("cut", 1, 0))
            if not first:
                todo.append(("down", -1, 1))
            if not last_split:
                todo.append(("cut", 1, 1))
            return todo + [("up", 0, 1), ("down", 0, 0)]

        def experts(n, work, stage, eng):
            if stage == "first":
                work("cut", 0, 0, 0)
                work("cut", 0, 0, 1)
                return
            def turn(ev, es, first, last):
                for kind, d, half in expert_order(es, first, last):
                    work(kind, ev + d, es + d, half)
            turn(0, 0, True, False)
            pairs = (n - 2) // 2
            with eng.Fori(0, pairs) as r:
                turn(r * 2 + 1, 1, False, False)
                turn(r * 2 + 2, 2, False, False)
            for e in range(1 + 2 * pairs, n):
                turn(e, e, False, e == n - 1)
            work("down", n - 1, n - 1, 1)

        def up_col(l, part, k, m):
            if part == 2:
                return (2 if l else 1) * 1024 + k * C
            return part * 1024 + k * FF + m * 128

        UP_BANKS = [[pb[0:4]], [pb[0:2], pb[2:4]]]
        SUM = [pb[4:6], pb[6:8]]

        def experts_tensor(pe, l, n, stage="rest"):
            def work(kind, ev, es, half):
                if kind == "up":
                    u0, us = (ev * 2 + half) * NM, (es * 2 + half) * NM
                    if half == 0:
                        pe.wait_ge(s[f"m_lo_{l}"], 2 * ev + 2)
                    for m in range(NM):
                        for part in range(1 + l):
                            banks = UP_BANKS[l][part]
                            if us + m >= len(banks):
                                pe.wait_ge(s["u_hf_1"] if part else s[f"u_act_{l}"], u0 + m - len(banks) + 1)
                            i = 0
                            for k in range(2):
                                for qa, qb in PARTS:
                                    c = up_col(l, part, k, m)
                                    mm = pe.matmul(banks[m % len(banks)][:, 0:HT], MW[:, es % 2, qa, c:c + 128],
                                                   xT[:, qb, k, half * HT:(half + 1) * HT],
                                                   start=(i == 0), stop=(i == 5))
                                    i += 1
                        mm.then_inc(s[f"u_mm_{l}"], 1)
                    if es == 0 and half == 0:
                        biases_tensor(pe, l)
                elif kind == "down":
                    pe.wait_ge(s[f"u_lo_{l}"], (ev * 2 + half + 1) * NM)
                    for c in range(2):
                        i, last = 0, 3 * NM - 1
                        for k in range(NM):
                            for qa, qb in PARTS:
                                c0 = up_col(l, 2, k, 0) + c * 128
                                mm = pe.matmul(SUM[half][c][:, 0:HT], MW[:, es % 2, qa, c0:c0 + 128],
                                               HTt[:, half, qb, k, :],
                                               start=False,
                                               stop=(es == n - 1 and i == last))
                                i += 1
                    mm.then_inc(s[f"d_mm_{l}"], 1)
            experts(n, work, stage, pe)

        MN = [2048, 3072]

        def experts_scalar(act, l, n, stage):
            def work(kind, ev, es, half):
                if kind == "cut":
                    c = slice(0, 1024) if half == 0 else slice(1024, MN[l])
                    act.wait_ge(s[f"m_in{es % 2}_{l}"], (ev + 2 - es % 2) * 8)
                    if es >= 2:
                        act.wait_ge(s[f"d_mm_{l}"], 2 * ev - 3 + half)
                    act.activation(MW[:, es % 2, 0, c], ST[:, es % 2, c], ACT.Copy, scale=WS)\
                       .then_inc(s[f"m_hi_{l}"], 1)
                elif kind == "up":
                    u0, us = (ev * 2 + half) * NM, (es * 2 + half) * NM
                    for m in range(NM):
                        act.wait_ge(s[f"u_mm_{l}"], u0 + m + 1)
                        if us + m >= HB:
                            act.wait_ge(s[f"u_hf_{l}"] if l else s[f"u_lo_{l}"], u0 + m - HB + 1)
                        if l == 0:
                            act.activation(hf[:, m % HB, :], pb[m % 4][:, 0:HT], ACT.Gelu,
                                           bias=bcur[:, es % 2, m:m + 1], scale=1.0 / WS)\
                               .then_inc(s["u_act_0"], 1)
                        else:
                            act.activation(sg[:, m % HB, :], pb[m % 2][:, 0:HT], ACT.Silu, scale=1.0 / WS)\
                               .then_inc(s["u_act_1"], 1)
                    if l == 1 and es == 0 and half == 0:
                        weights_scalar(act, 1)
                elif l == 0 and es == n - 1 and half == 0:
                    expm_first_scalar(act)
            experts(n, work, stage, act)

        def experts_vector(dve, l, n, stage):
            def work(kind, ev, es, half):
                if kind == "cut":
                    c = slice(0, 1024) if half == 0 else slice(1024, MN[l])
                    dve.wait_ge(s[f"m_hi_{l}"], 2 * ev + half + 1)
                    if l == 0 and half == 0:
                        dve.tensor_copy(bcur[:, es % 2, :], b1[:, bass.ds(ev, 1), :].rearrange("p a m -> p (a m)"))
                    dve.scalar_tensor_tensor(MW[:, es % 2, 1, c], ST[:, es % 2, c], WS,
                                             MW[:, es % 2, 0, c], ALU.mult, ALU.subtract)\
                       .then_inc(s[f"m_lo_{l}"], 1)
                elif kind == "up":
                    u0, us = (ev * 2 + half) * NM, (es * 2 + half) * NM
                    for m in range(NM):
                        n_, ns = u0 + m, us + m
                        if l == 0:
                            dve.wait_ge(s["u_wt_0"], n_ + 1)
                        elif es == 0:
                            dve.wait_ge(s["u_act_1"], n_ + 1)
                        else:
                            dve.wait_ge(s["u_wt_1"], n_ - 2 * NM + 1)
                        if l == 1:
                            if ns >= HB:
                                dve.wait_ge(s["u_lo_1"], n_ - HB + 1)
                            dve.scalar_tensor_tensor(hf[:, m % HB, :], UP_BANKS[1][1][m % 2][:, 0:HT], HS / WS,
                                                     sg[:, m % HB, :],
                                                     ALU.mult, ALU.mult).then_inc(s["u_hf_1"], 1)
                            dve.wait_ge(s["u_hf_1"], n_ + 1)
                        if m == 0 and es >= 1:
                            dve.wait_ge(s[f"d_mm_{l}"], (ev - 1) * 2 + half + 1)
                        dve.tensor_copy(HTt[:, half, 0, m, :], hf[:, m % HB, :]).then_inc(s[f"u_hi_{l}"], 1)
                        dve.wait_ge(s[f"u_hi_{l}"], n_ + 1)
                        dve.tensor_tensor(HTt[:, half, 1, m, :], hf[:, m % HB, :], HTt[:, half, 0, m, :],
                                          ALU.subtract).then_inc(s[f"u_lo_{l}"], 1)
                else:
                    if l == 0 and half == 0 and es == 0:
                        gate_abel_vector(dve)
                        residual_abel_vector(dve)
                    if l == 0 and half == 0 and es == n - 1:
                        expm_first_vector(dve)
            experts(n, work, stage, dve)

        def experts_gpsimd(pool, l, n):
            def work(kind, ev, es, half):
                if kind != "up" or es < l:
                    return
                if half == 0:
                    pool.wait_ge(s[f"w_in{es % 2}_{l}"], (ev + 2 - es % 2) * 8 if l == 0 else (ev + es % 2) * 8)
                for m in range(NM):
                    n_ = (ev * 2 + half) * NM + m
                    tile = (sg if l else hf)[:, m % HB, :]
                    pool.wait_ge(s[f"u_act_{l}"], n_ + 1)
                    pool.tensor_tensor(tile, tile, wdB[:, es % 2, half * HT:(half + 1) * HT], ALU.mult)\
                        .then_inc(s[f"u_wt_{l}"], 1)
            experts(n, work, "rest", pool)

        def experts_sync(sp, l, n):
            def weights(e):
                if e >= 2:
                    sp.wait_ge(s[f"u_lo_{l}"], (e - 1) * 2 * NM)
                sp.dma_start(wdB[:, e % 2, :], wd_dram[l][e - l:e - l + 1, :, :].rearrange("a g n -> a (g n)")[0, :]
                             .partition_broadcast(128)).then_inc(s[f"w_in{e % 2}_{l}"], 16)
            for e in range(n):
                if e == 2:
                    sp.wait_ge(s[f"wd_act_{l}"], 2)
                    sp.dma_start(wd_dram[l], wdf[:, :, :]).then_inc(s[f"wd_out_{l}"], 16)
                    sp.wait_ge(s[f"wd_out_{l}"], 16)
                    for e0 in range(l, 2):
                        weights(e0)
                if e >= 2:
                    sp.wait_ge(s[f"m_lo_{l}"], 2 * (e - 1))
                sp.dma_start(ST[:, e % 2, 0:MN[l]], a[f"moe{l}"][e, :, :]).then_inc(s[f"m_in{e % 2}_{l}"], 16)
                if e >= 2:
                    weights(e)

        def weights_tensor(pe, l):
            pe.wait_ge(s[f"rt_wd_{l}"], 1)
            for g in range(2):
                for j in range(4):
                    mm = pe.transpose(pb[4 + g][0:E, j * S:(j + 1) * S], wd[:, 4 * g + j, :], identf[0:S, 0:S])
                mm.then_inc(s[f"wd_mm_{l}"], 1)

        def weights_scalar(act, l):
            for g in range(2):
                act.wait_ge(s[f"wd_mm_{l}"], g + 1)
                act.activation(wdf[:, g, :], pb[4 + g][0:E, 0:HT], ACT.Copy, scale=1.0 if l else HS)\
                   .then_inc(s[f"wd_act_{l}"], 1)

        def abel_tensor(pe):
            for b in range(B):
                if b == B // 2:
                    weights_tensor(pe, 0)
                if b >= 2:
                    pe.wait_ge(s["f_act_0"], b - 1)
                i = 0
                for k in range(2):
                    for qa, qb in PARTS:
                        pe.matmul(GB[b % 2][0:S, 0:C], xT[:, qa, k, b * S:(b + 1) * S], w0("abel", qb, k),
                                  start=(i == 0), stop=False)
                        i += 1
                for q in range(2):
                    mm = pe.matmul(GB[b % 2][0:S, 0:C], ones16[:, 0:S], row("abel_b", q), start=False, stop=(q == 1))
                mm.then_inc(s["f_mm_0"], 1)

        def abel_scalar(act):
            for b in range(B):
                if b == B // 2:
                    weights_scalar(act, 0)
                act.wait_ge(s["f_mm_0"], b + 1)
                act.activation(AB[:, b, :], GB[b % 2][0:S, 0:C], ACT.Gelu, scale=1.0 / WS).then_inc(s["f_act_0"], 1)
            act.wait_ge(s["wd_act_0"], 2)
            act.activation(wdT[:, 0, :], wdf[:, :, :].rearrange("p g n -> p (g n)"), ACT.Copy).then_inc(s["wd_act_0"], 1)

        def biases_vector(dve):
            dve.wait_ge(s["wd_act_0"], 3)
            dve.tensor_tensor(wdT[:, 1, :], wdf[:, :, :].rearrange("p g n -> p (g n)"), wdT[:, 0, :], ALU.subtract)\
               .then_inc(s["wd_lo_0"], 1)

        def biases_tensor(pe, l):
            if l:
                weights_tensor(pe, 1)
                pe.wait_ge(s["wd_act_1"], 2)
                for half in range(2):
                    for c in range(2):
                        pe.matmul(SUM[half][c][:, 0:HT], zero16[:, :], ones16[:, 0:HT], start=True, stop=False)
                return
            pe.wait_ge(s["f_act_0"], B)
            pe.wait_ge(s["wd_lo_0"], 1)
            for half in range(2):
                for c in range(2):
                    for i, (qa, qb) in enumerate(PARTS):
                        pe.matmul(SUM[half][c][:, 0:HT], eb2[:, qa, c * 128:(c + 1) * 128],
                                  wdT[:, qb, half * HT:(half + 1) * HT], start=(i == 0), stop=False)

        def moved_scalar(act):
            act.wait_ge(s["d_mm_0"], 2 * E)
            for k, g in GROUPS:
                act.activation(xT[:, 0, k, g * HT:(g + 1) * HT], SUM[g][k][:, 0:HT], ACT.Copy, scale=1.0 / (WS * HS))\
                   .then_inc(s["ln_thi"], 1)

        def moved_vector(dve):
            for n, (k, g) in enumerate(GROUPS):
                dve.wait_ge(s["ln_thi"], 8 + n + 1)
                dve.scalar_tensor_tensor(xT[:, 1, k, g * HT:(g + 1) * HT], SUM[g][k][:, 0:HT], 1.0 / (WS * HS),
                                         xT[:, 0, k, g * HT:(g + 1) * HT], ALU.mult, ALU.subtract)\
                   .then_inc(s["ln_tlo"], 1)

        RES = flat[:, 0:4 * HT].rearrange("p (g k n) -> p g k n", g=2, k=2)

        def result_vector(dve, g):
            dve.wait_ge(s["d_mm_1"], 2 * E + g + 1)
            for k in range(2):
                dve.tensor_scalar(RES[:, g, k, :], SUM[g][k][:, 0:HT], 1.0 / (WS * HS), None, ALU.mult)\
                   .then_inc(s["moved_1"], 1)

        def result_tensor(pe, g):
            pe.wait_ge(s["moved_1"], 2 * g + 2)
            pe.wait_ge(s["u_act_1"], (E + 1) * 2 * NM)
            pe.wait_ge(s["u_hf_1"], (E + 1) * 2 * NM)
            for j in range(2):
                for b in range(2):
                    for k in range(2):
                        mm = pe.transpose(pb[2 * g + j][0:S, b * C + k * 128:b * C + (k + 1) * 128],
                                          RES[:, g, k, (2 * j + b) * S:(2 * j + b + 1) * S], identf[:, :])
                mm.then_inc(s["f_mm_1"], 1)

        def result_add_vector(dve, g):
            for j in range(2):
                dve.wait_ge(s["f_mm_1"], 2 * g + j + 1)
                xb = X[:, 4 * g + 2 * j:4 * g + 2 * j + 2, :].rearrange("p b c -> p (b c)")
                dve.scalar_tensor_tensor(xb, pb[2 * g + j][0:S, 0:2 * C], tg[:, 3:4], xb, ALU.mult, ALU.add)\
                   .then_inc(s["ffn"], 1)

        EU = []
        for t in range(DEG - 1, 0, -1):
            EU += [("horner", g, t) for g in range(3)]
        for _ in range(SQ):
            EU += [("turn", g, 0) for g in range(3)] + [("square", g, 0) for g in range(3)]
        EU += [("turn", 0, 0), ("turn", 1, 0), ("pair", 1, 0), ("pair", 0, 0)]

        KEPT = [n for n, (kind, g, t) in enumerate(EU) if kind == "square" or (kind == "horner" and t == 1)]

        F0 = len(chunks0)
        W1ST, W1END = F0 + LORA_CHUNKS, F0 + LORA_CHUNKS + 4
        order = [("cut", n, j) for n in range(F0, W1ST) for j in range(len(lo_pieces(n)))]
        order += [("add", W1ST, j) for j in range(4)]
        for n in range(W1ST, W1END):
            adds = [("add", n + 1, j) for j in range(len(chunks[n + 1][5]))]
            order += adds[0:2] + [("cut", n, 0)] + adds[2:4] + [("cut", n, 1)]
        BETWEEN = {"tensor": {}, "scalar": {}, "vector": {}}
        for place, (what, n, j) in enumerate(order, FIRST_BETWEEN):
            BETWEEN["vector"].setdefault(place, []).append((what, n, j))
            if what == "add":
                BETWEEN["tensor"].setdefault(place - 1, []).append((n, j))
                if j == len(chunks[n][5]) - 1:
                    BETWEEN["scalar"].setdefault(place + 1, []).append(n)
        for n in range(F0, W1ST):
            BETWEEN["scalar"].setdefault(FIRST_BETWEEN - 3 + 2 * (n - F0), []).append(n)
        assert FIRST_BETWEEN + len(order) <= len(EU)

        def unit_scale(n):
            kind, g, t = EU[n]
            return {"horner": 1.0 / (WS * max(t, 1)), "turn": 1.0}.get(kind, 1.0 / WS)

        def expm_tensor(pe):
            pe.wait_ge(s["e_lo"], 4)
            pe.wait_ge(s["eyes_set"], 1)
            for n, (kind, g, t) in enumerate(EU):
                bank = pb[n % 3]
                if kind == "pair":
                    pe.wait_ge(s["e_lo"], 4 + n)
                elif n >= 3:
                    pe.wait_ge(s["e_lo"], 4 + n - 2)
                if kind == "turn":
                    last = [i for i, k in enumerate(KEPT) if k < n and EU[k][1] == g][-1]
                    pe.wait_ge(s["e_f"], 6 + last + 1)
                    for c in range(2):
                        for m in range(2):
                            mm = pe.transpose(bank[:, c * 256 + m * 128:c * 256 + (m + 1) * 128],
                                              RF[:, g, m, c * 128:(c + 1) * 128], identf[:, :])
                else:
                    left = BT if kind == "horner" else RT
                    right = 2 if kind == "pair" else g
                    for m in range(2):
                        i = 0
                        for k in range(2):
                            if kind == "horner" and k == 1:
                                c0 = m * 256 + m * 128
                                pe.matmul(bank[:, c0:c0 + 128], eyes[:, 0, :], eyes[:, t - 1, :],
                                          start=False, stop=False)
                            for qa, qb in PARTS:
                                mm = pe.matmul(bank[:, m * 256:(m + 1) * 256], left[:, qa, g, k, m * 128:(m + 1) * 128],
                                               R16[:, qb, right, k, :], start=(i == 0), stop=(i == 5))
                                i += 1
                mm.then_inc(s["e_mm"], 1)
                for chunk, j in BETWEEN["tensor"].get(n, []):
                    lora_product(pe, chunk, j)

        flatg = ST[:, :, 0:3 * 512].rearrange("p a (g n) -> p a g n", g=3)

        def expm_first_scalar(act):
            act.wait_ge(s["e_in"], 32)
            act.wait_ge(s["d_mm_0"], 2 * E - 2)
            act.activation(BT[:, 0, :, :, :].rearrange("p g k n -> p g (k n)"), flatg[:, 0, :, :], ACT.Copy,
                           scale=WS / 2 ** SQ).then_inc(s["e_hi"], 1)
            for g in range(3):
                act.wait_ge(s["e_f"], 3 + g + 1)
                act.activation(R16[:, 0, g, :, :], RF[:, g, :, :], ACT.Copy).then_inc(s["e_hi"], 1)

        def expm_scalar(act):
            for n, (kind, g, t) in enumerate(EU):
                act.wait_ge(s["e_mm"], n + 1)
                act.activation((RT if kind == "turn" else R16)[:, 0, 2 if kind == "pair" else g, :, :],
                               pb[n % 3][:, :].rearrange("p (k n) -> p k n", k=2), ACT.Copy, scale=unit_scale(n))\
                   .then_inc(s["e_hi"], 1)
                for chunk in BETWEEN["scalar"].get(n, []):
                    cut_hi(act, chunk)

        def expm_first_vector(dve):
            dve.wait_ge(s["e_in"], 32)
            for g in range(3):
                dve.tensor_scalar(RF[:, g, :, :].rearrange("p k n -> p (k n)"), flatg[:, 1, g, :],
                                  WS / 2 ** SQ / DEG, None, ALU.mult).then_inc(s["e_f"], 1)
            for g in range(3):
                dve.wait_ge(s["e_f"], g + 1)
                for k in range(2):
                    diag = RF[:, g, k, k * 128:(k + 1) * 128]
                    x = dve.scalar_tensor_tensor(diag, identf[:, :], WS, diag, ALU.mult, ALU.add)
                x.then_inc(s["e_f"], 1)
            dve.wait_ge(s["e_hi"], 1)
            dve.scalar_tensor_tensor(BT[:, 1, :, :, :].rearrange("p g k n -> p g (k n)"), flatg[:, 0, :, :],
                                     WS / 2 ** SQ, BT[:, 0, :, :, :].rearrange("p g k n -> p g (k n)"),
                                     ALU.mult, ALU.subtract).then_inc(s["e_lo"], 1)
            for g in range(3):
                dve.wait_ge(s["e_hi"], 2 + g)
                dve.tensor_tensor(R16[:, 1, g, :, :], RF[:, g, :, :], R16[:, 0, g, :, :], ALU.subtract)\
                   .then_inc(s["e_lo"], 1)

        def eyes_vector(dve):
            for t in range(1, DEG):
                x = dve.tensor_scalar(eyes[:, t - 1, :], identf[:, :], WS * t, None, ALU.mult)
            x.then_inc(s["eyes_set"], 1)

        def expm_vector(dve):
            for n, (kind, g, t) in enumerate(EU):
                src = pb[n % 3][:, :].rearrange("p (k n) -> p k n", k=2)
                r = 2 if kind == "pair" else g
                dve.wait_ge(s["e_hi"], 4 + n + 1)
                if n in KEPT:
                    dve.wait_ge(s["e_lo"], 4 + n - 2)
                    dve.tensor_scalar(RF[:, g, :, :], src, unit_scale(n), None, ALU.mult).then_inc(s["e_f"], 1)
                part = (RT if kind == "turn" else R16)[:, :, r, :, :]
                dve.scalar_tensor_tensor(part[:, 1, :, :], src, unit_scale(n), part[:, 0, :, :], ALU.mult,
                                         ALU.subtract).then_inc(s["e_lo"], 1)
                for what, chunk, j in BETWEEN["vector"].get(n, []):
                    (lora_add if what == "add" else cut_lo)(dve, chunk, j)

        def mix_tensor(pe, turned):
            pe.wait_ge(s["ln_tlo"], turned)
            pe.wait_ge(s["e_lo"], 4 + len(EU))
            for b in range(B):
                if b >= 2:
                    pe.wait_ge(s["f_dve_0"], b - 1)
                i = 0
                for k in range(2):
                    for qa, qb in PARTS:
                        mm = pe.matmul(GB[b % 2][0:S, 0:C], xT[:, qa, k, b * S:(b + 1) * S], R16[:, qb, 2, k, :],
                                       start=(i == 0), stop=(i == 5))
                        i += 1
                mm.then_inc(s["f_mm_0"], 1)

        def gate_abel_vector(dve):
            dve.tensor_tensor(gam[:, 2, :], gam[:, 2, :], gam[:, 3, :], ALU.add).then_inc(s["mix"], 1)
            dve.wait_ge(s["mix"], 1)
            dve.wait_ge(s["f_act_0"], B)
            for b in range(B):
                if b >= HB:
                    dve.wait_ge(s["mix"], 1 + b - HB + 1)
                dve.tensor_tensor_reduce(sg[0:S, b % HB, 0:C], AB[:, b, :], gam[:, 2, :], 1.0, 0.0, ALU.mult,
                                         ALU.add, zz[:, 0, b:b + 1]).then_inc(s["mix"], 1)

        def residual_abel_vector(dve):
            dve.tensor_tensor(Y[:, :, :], Y[:, :, :], AB[:, :, :], ALU.add).then_inc(s["mix"], 1)
            dve.wait_ge(s["mix"], B + 2)
            dve.scalar_tensor_tensor(X[:, :, :].rearrange("p b c -> p (b c)"), Y[:, :, :].rearrange("p b c -> p (b c)"),
                                     tg[:, 1:2], X[:, :, :].rearrange("p b c -> p (b c)"), ALU.mult, ALU.add)\
               .then_inc(s["mix"], 1)
            dve.wait_ge(s["mix"], B + 3)

        def mix_scalar(act):
            act.wait_ge(s["mix"], 2 * B + 4)
            act.activation(zz[:, 1, :], zz[:, 0, :], ACT.Sigmoid, bias=gc_b[:, 0:1], scale=1.0)\
               .then_inc(s["f_act_0"], 1)

        def mix_vector(dve):
            done = B + 3

            def gate(b):
                dve.wait_ge(s["f_dve_0"], b + 1)
                if b >= HB:
                    dve.wait_ge(s["mix"], done + b - HB + 1)
                dve.tensor_tensor_reduce(junk[:, b % HB, :], Z[:, b, :], gam[:, 3, :], 1.0, 0.0, ALU.mult,
                                         ALU.add, zz[:, 2, b:b + 1]).then_inc(s["mix"], 1)

            for b in range(B):
                dve.wait_ge(s["f_mm_0"], B + b + 1)
                dve.scalar_tensor_tensor(Z[:, b, :], GB[b % 2][0:S, 0:C], 1.0 / WS, AB[:, b, :], ALU.mult,
                                         ALU.subtract).then_inc(s["f_dve_0"], 1)
                if b >= 1:
                    gate(b - 1)
            gate(B - 1)
            dve.wait_ge(s["mix"], done + B)
            dve.tensor_tensor(zz[:, 0, :], zz[:, 0, :], zz[:, 2, :], ALU.add).then_inc(s["mix"], 1)
            dve.wait_ge(s["f_act_0"], B + 1)
            dve.tensor_scalar(zz[:, 2, :], zz[:, 1, :], tg[:, 1:2], None, ALU.mult).then_inc(s["mix"], 1)
            dve.wait_ge(s["mix"], done + B + 2)
            for b in range(B):
                dve.scalar_tensor_tensor(X[:, b, :], Z[:, b, :], zz[:, 2, b:b + 1], X[:, b, :], ALU.mult,
                                         ALU.add).then_inc(s["ffn"], 1)

        def affine(eng, b0, b1, done):
            eng.wait_ge(s["ln_norm"], 2 * B + b1)
            for n, op in enumerate((ALU.mult, ALU.add)):
                eng.tensor_tensor(Z[:, b0:b1, :], Z[:, b0:b1, :], bc(gam[:, n:n + 1, :], [S, b1 - b0, C]), op)\
                   .then_inc(done, 1)
                eng.wait_ge(done, n + 1)

        FFN0 = 2 + B
        G_ALL = [2 * counts(L)[0] + (B - 2) * counts(L)[1] + 2 * len(L.out) for L in layers]
        block = ctx.enter_context(nc.Block())

        @block.sync
        def _(sp):
            sp.dma_start(X[:, :, :], a["x"].rearrange("b s c -> s b c")).then_inc(s["x_in"], 16)
            sp.dma_start(tg[:, :], a["gates"].partition_broadcast(S)).then_inc(s["small_in"], 16)
            sp.dma_start(lora_s[:, :], a["alphas"].partition_broadcast(128)).then_inc(s["small_in"], 16)
            sp.dma_start(gam[:, :, :], a["vecs"].partition_broadcast(S)).then_inc(s["small_in"], 16)
            sp.dma_start(b1[:, :, :], a["eb1"]).then_inc(s["small_in"], 16)
            sp.dma_start(gc_b[:, :], a["gc_b"].partition_broadcast(S)).then_inc(s["small_in"], 16)
            chunks_sync(sp, 0, NC0)
            sp.wait_ge(s["g_free0"], G_ALL[0])
            experts_sync(sp, 0, E)
            sp.wait_ge(s["m_lo_0"], 2 * E)
            for j in range(2):
                sp.dma_start(ST[:, j, 0:3 * 512], a["gens"][j, :, :]).then_inc(s["e_in"], 16)
            sp.wait_ge(s["e_f"], 3)
            sp.wait_ge(s["e_lo"], 1)
            sp.wait_ge(s["chunk_lo"], NC0)
            chunks_sync(sp, NC0, NC1)
            sp.wait_ge(s["ipa_lo"], 3)
            for q, part in enumerate((vi_sb, vi_sb2)):
                sp.dma_start(vi_dram[:, q, :], part).then_inc(s["ipa_stored"], 16)
            sp.wait_ge(s["ipa_stored"], 32)
            attention_sync(sp, layers[1])
            sp.wait_ge(s["g_free1"], G_ALL[1])
            experts_sync(sp, 1, E + 1)
            sp.wait_ge(s["ffn"], FFN0 + 4)
            sp.dma_start(out.rearrange("b s c -> s b c"), X[:, :, :]).then_inc(s["x_in"], 16)
            sp.wait_ge(s["x_in"], 32)

        @block.gpsimd
        def _(pool):
            pool.memset(cT[K2:128, 1, 1, :], 1.0).then_inc(s["below_set"], 1)
            pool.wait_ge(s["below_set"], 1)
            pool.memset(identf[:, :], 0.0).then_inc(s["ident_set"], 1)
            pool.wait_ge(s["ident_set"], 1)
            pool.affine_select(out=identf[:, :], in_=identf[:, :], compare_op=ALU.not_equal, fill=1.0, base=0,
                               pattern=[[-1, 128]], channel_multiplier=1).then_inc(s["ident_set"], 1)
            pool.memset(mask[:, :], 1.0).then_inc(s["ident_set"], 1)
            pool.wait_ge(s["ident_set"], 3)
            pool.affine_select(out=mask[:, :], in_=mask[:, :], compare_op=ALU.is_ge, fill=0.0, base=0,
                               pattern=[[-16, 8]], channel_multiplier=1).then_inc(s["ident_set"], 1)
            pool.wait_ge(s["ident_set"], 4)
            pool.affine_select(out=mask[:, :], in_=mask[:, :], compare_op=ALU.is_ge, fill=0.0, base=15,
                               pattern=[[16, 8]], channel_multiplier=-1).then_inc(s["ident_set"], 1)
            pool.iota(iota8[:, :], [[1, E]], base=0, channel_multiplier=0, allow_small_or_imprecise_dtypes=True)\
                .then_inc(s["ident_set"], 1)
            pool.wait_ge(s["ident_set"], 5)
            attention_gpsimd(pool, layers[0])
            affine(pool, SPLIT_AT, B, s["ffn_rest"])
            pool.wait_ge(s["g_free0"], G_ALL[0])
            pool.memset(cT[K2:128, 1, 1, :], 0.0).then_inc(s["below_set"], 1)
            pool.wait_ge(s["below_set"], 2)
            experts_gpsimd(pool, 0, E)
            pool.wait_ge(s["ffn"], FFN0)
            pool.memset(qflat, 0.0).then_inc(s["const_set"], 1)
            attention_gpsimd(pool, layers[1])
            experts_gpsimd(pool, 1, E + 1)

        @block.scalar
        def _(act):
            norm_scalar(act, 0)
            act.wait_ge(s["small_in"], 16 * 5)
            act.activation(tg[:, :], tg[:, :], ACT.Tanh).then_inc(s["tanh_done"], 1)
            chunks_scalar(act, 0, NC0)
            turn_scalar(act, 0)
            attention_scalar(act, layers[0])
            norm_scalar(act, 1)
            norm_scalar(act, 2)
            experts_scalar(act, 0, E, "first")
            turn_scalar(act, 1)
            router_scalar(act, 0)
            abel_scalar(act)
            experts_scalar(act, 0, E, "rest")
            moved_scalar(act)
            expm_scalar(act)
            mix_scalar(act)
            norm_scalar(act, 3)
            turn_scalar(act, 3)
            chunks_scalar(act, W1END, NC1)
            ipa_scalar(act)
            act.wait_ge(s["const_set"], 1)
            attention_scalar(act, layers[1])
            norm_scalar(act, 4)
            experts_scalar(act, 1, E + 1, "first")
            turn_scalar(act, 4)
            router_scalar(act, 1)
            experts_scalar(act, 1, E + 1, "rest")

        @block.vector
        def _(dve):
            dve.memset(ones16[:, :], 1.0).then_inc(s["ones_set"], 1)
            dve.memset(zero16[:, :], 0.0).then_inc(s["ones_set"], 1)
            dve.memset(os16[:, :], OS).then_inc(s["ones_set"], 1)
            dve.wait_ge(s["x_in"], 16)
            norm_vector(dve, 0, X, Y)
            chunks_vector(dve, 0, NC0)
            turn_vector(dve, 0)
            dve.wait_ge(s["tanh_done"], 1)
            dve.tensor_scalar(tgs[:, 0:1], tg[:, 0:1], 1.0 / WS, None, ALU.mult).then_inc(s["lora_scale"], 1)
            dve.tensor_scalar(tgs[:, 1:2], tg[:, 2:3], 1.0 / (WS * OS), None, ALU.mult).then_inc(s["lora_scale"], 1)
            dve.tensor_scalar(lora_s[:, :], lora_s[:, :], 1.0 / (RANK * WS * WS), None, ALU.mult)\
               .then_inc(s["lora_scale"], 1)
            dve.wait_ge(s["lora_scale"], 3)
            attention_vector(dve, layers[0])
            dve.wait_ge(s["g_free0"], G_ALL[0])
            norm_vector(dve, 1, X, Y)
            norm_vector(dve, 2, Y, Z)
            affine(dve, 0, SPLIT_AT, s["ffn"])
            turn_vector(dve, 1)
            dve.wait_ge(s["ident_set"], 6)
            experts_vector(dve, 0, E, "first")
            router_vector(dve, 0)
            biases_vector(dve)
            eyes_vector(dve)
            experts_vector(dve, 0, E, "rest")
            moved_vector(dve)
            expm_vector(dve)
            mix_vector(dve)
            dve.wait_ge(s["ffn"], FFN0)
            norm_vector(dve, 3, X, Y)
            turn_vector(dve, 3)
            dve.wait_ge(s["below_set"], 2)
            for q in range(2):
                for k in range(2):
                    dve.tensor_copy(ci_sb[:, q, k, :].rearrange("p (b n) -> p b n", b=B), cI[q][k])\
                       .then_inc(s["ipa_ctx"], 1)
            chunks_vector(dve, W1END, NC1)
            ipa_vector(dve)
            dve.wait_ge(s["const_set"], 1)
            attention_vector(dve, layers[1])
            dve.wait_ge(s["g_free1"], G_ALL[1])
            norm_vector(dve, 4, X, Y)
            turn_vector(dve, 4)
            experts_vector(dve, 1, E + 1, "first")
            router_vector(dve, 1)
            experts_vector(dve, 1, E + 1, "rest")
            for g in range(2):
                result_vector(dve, g)
                result_add_vector(dve, g)

        @block.tensor
        def _(pe):
            pe.wait_ge(s["ident_set"], 2)
            turn_tensor(pe, 0, Y, halves_of(0))
            pe.wait_ge(s["ln_tlo"], 4)
            pe.wait_ge(s["chunk_lo"], NC0)
            pe.wait_ge(s["ones_set"], 3)
            pe.wait_ge(s["below_set"], 1)
            attention_tensor(pe, layers[0])
            turn_tensor(pe, 1, Z, [(s["ffn"], 2), (s["ffn_rest"], 2)])
            router_tensor(pe, 0, 8)
            abel_tensor(pe)
            experts_tensor(pe, 0, E)
            expm_tensor(pe)
            mix_tensor(pe, 12)
            turn_tensor(pe, 3, Y, halves_of(3))
            pe.wait_ge(s["ln_tlo"], 16)
            pe.wait_ge(s["chunk_lo"], NC1)
            pe.wait_ge(s["ipa_ctx"], 4)
            ipa_tensor(pe)
            pe.wait_ge(s["ln_tlo"], 16)
            pe.wait_ge(s["ipa_lo"], 3)
            pe.wait_ge(s["const_set"], 1)
            attention_tensor(pe, layers[1])
            turn_tensor(pe, 4, Y, halves_of(4))
            router_tensor(pe, 1, 20)
            experts_tensor(pe, 1, E + 1)
            for g in range(2):
                result_tensor(pe, g)


def _layout(inputs, np):
    i = {k: np.asarray(v) for k, v in inputs.items()}
    f = np.float32

    def tiles(w, rows):
        n = w.shape[0] // rows
        return w.reshape(n, rows, -1).transpose(1, 0, 2).reshape(rows, -1)

    def context(w):
        return np.concatenate([w[0:128], np.concatenate([w[128:], w[128:]])], 1)

    def kv0():
        w = np.concatenate([i["L0_xattn_Wk"], i["L0_xattn_Wv"]], 1)
        below = np.zeros((128 - K2, 2 * C), f)
        below[0] = below[32] = np.concatenate([i["L0_xattn_bk"], i["L0_xattn_bv"]])
        return np.concatenate([context(w), np.concatenate([w[128:], below])], 1)

    def down(n):
        w = i[f"L1_xattn_{n}_down"].T
        return np.concatenate([w, w[:, 128:]], 1) if n in "kv" else w

    ctxT = i["ctx_768"].reshape(B * KV, CKV).T
    out = {
        "x": i["x"],
        "ctxT": np.stack([ctxT[0:128], np.concatenate([ctxT[128:], ctxT[128:]])]),
        "pa0": np.concatenate([tiles(w, 128) for w in (i["L0_xattn_Wq"], i["L0_xattn_Wo"], i["L0_ffn_abel_w"],
                                                       i["L0_ffn_moe_gate_w"], i["L1_ffn_Wr"].T)], 1),
        "kv0": kv0(),
        "rows": np.concatenate([i["L0_xattn_bq"], i["L0_xattn_bo"], i["L0_ffn_abel_b"], i["L0_ffn_moe_gate_b"],
                                i["L1_xattn_bo"], i["L1_ffn_rb"]])[None, :],
        "gates": np.stack([i["g_xattn"][0], i["g_ffn"][0], i["g_xattn"][1], i["g_ffn"][1]]),
        "alphas": np.concatenate([i["L1_xattn_q_alpha"], i["L1_xattn_k_alpha"], i["L1_xattn_v_alpha"],
                                  i["L1_xattn_o_alpha"]]),
        "vecs": np.stack([i["L0_ffn_ln_gamma"], i["L0_ffn_ln_beta"], i["L0_ffn_gc_w"][0:C, 0],
                          i["L0_ffn_gc_w"][C:, 0]]),
        "eb1": i["L0_ffn_eb1"].reshape(E, NM, 128).transpose(2, 0, 1),
        "gc_b": i["L0_ffn_gc_b"],
        "eb2": i["L0_ffn_eb2"],
        "moe0": np.stack([np.concatenate([tiles(i["L0_ffn_ew1"][e], 128), tiles(i["L0_ffn_ew2"][e], 128)], 1)
                          for e in range(E)]),
        "moe1": np.stack([np.concatenate([tiles(w.T, 128) for w in (g, u, d)], 1) for g, u, d in
                          [(i["L1_ffn_Wg_s"], i["L1_ffn_Wu_s"], i["L1_ffn_Wd_s"])] +
                          [(i["L1_ffn_Wg"][e], i["L1_ffn_Wu"][e], i["L1_ffn_Wd"][e]) for e in range(E)]]),
        "gens": np.stack([np.concatenate([tiles(m, 128) for m in ms], 1) for ms in
                          (i["L0_ffn_gens"].transpose(0, 2, 1), i["L0_ffn_gens"])]),
        "lora": np.tile(np.concatenate([down(n) for n in "qkvo"] +
                                       [i[f"L1_xattn_{n}_up"] for n in "qkvo"], 1), (3, 1)),
        "w1q": tiles(i["L1_xattn_Wq"], 128),
        "w1k": context(i["L1_xattn_Wk"]),
        "w1v": context(i["L1_xattn_Wv"]),
        "w1o": tiles(i["L1_xattn_Wo"], 128),
        "w1ki": context(i["L1_xattn_Wk_ipa"]),
        "w1vi": context(i["L1_xattn_Wv_ipa"]),
    }
    return {k: np.ascontiguousarray(v) for k, v in out.items()}


def kernel(**inputs):
    import numpy as _np
    import concourse.bacc as _bacc
    from concourse.bass_utils import run_bass_kernel_spmd as _run

    arrays = _layout(inputs, _np)
    nc = _bacc.Bacc("TRN2", target_bir_lowering=False, num_devices=1)
    args = {n: nc.dram_tensor(f"in_{n}", v.shape, F32, kind="ExternalInput").ap() for n, v in arrays.items()}
    res = nc.dram_tensor("out_0", (B, S, C), F32, kind="ExternalOutput").ap()
    build(nc, args, res)
    r = _run(nc, [{f"in_{n}": v for n, v in arrays.items()}], core_ids=[0])
    return r.results[0]["out_0"]
```
